# Optimizing a Trainium2 kernel written in Bass

```python
import numpy as np
import jax
import jax.numpy as jnp

def _softmax(x, axis=-1):
    return jax.nn.softmax(x, axis=axis)

def _gelu(x):
    return jax.nn.gelu(x, approximate=True)

def _silu(x):
    return jax.nn.silu(x)

def _sigmoid(x):
    return jax.nn.sigmoid(x)

def _layernorm(x, axis=-1, eps=1e-05):
    m = jnp.mean(x, axis=axis, keepdims=True)
    v = jnp.var(x, axis=axis, keepdims=True)
    return (x - m) / jnp.sqrt(v + eps)

def _scatter_add(tgt, idx, src, axis=0):
    return tgt.at[idx].add(src)

def _segment_sum(src, seg, n):
    return jax.ops.segment_sum(src, seg, n)
kernel_name = 'mk_macaron_d2_jaxref_r8_82a74c'

def setup_inputs(seed: int=0):
    np.random.seed(seed)
    _w = jnp.asarray

    def _L0_attn_setup():
        import jax, jax.numpy as jnp
        import numpy as np
        D_MODEL = 128
        N_HEAD = 16
        HEAD_SIZE = D_MODEL // N_HEAD
        LAYER_ID = 12
        N_LAYER = 24
        HEAD_SIZE_DIVISOR = 8
        TM_DIM = 32
        TD_DIM = 64
        B, T = (4, 128)
        EPS = 1e-05 * HEAD_SIZE_DIVISOR ** 2

        def _wkv6(r, k, v, w, u):
            Bc, Tc, H, K = r.shape
            wdec = jnp.exp(-jnp.exp(w))

            def step(S, inp):
                r_t, k_t, v_t, wd_t = inp
                kv = k_t[:, :, :, None] * v_t[:, :, None, :]
                y = jnp.einsum('bhk,bhkj->bhj', r_t, S + u[None, :, :, None] * kv)
                S = S * wd_t[:, :, :, None] + kv
                return (S, y)
            S0 = jnp.zeros((Bc, H, K, K), r.dtype)
            xs = (jnp.swapaxes(r, 0, 1), jnp.swapaxes(k, 0, 1), jnp.swapaxes(v, 0, 1), jnp.swapaxes(wdec, 0, 1))
            _, ys = jax.lax.scan(step, S0, xs)
            return jnp.swapaxes(ys, 0, 1).reshape(Bc, Tc, H * K)
        key = jax.random.key(seed)
        ks = jax.random.split(key, 12)
        C = D_MODEL
        r0 = LAYER_ID / (N_LAYER - 1)
        r1 = 1.0 - LAYER_ID / N_LAYER
        ddd = np.arange(C, dtype=np.float64) / C
        time_maa_x = (1.0 - ddd ** r1).astype(np.float32)
        time_maa_w = (1.0 - ddd ** r1).astype(np.float32)
        time_maa_k = (1.0 - ddd ** r1).astype(np.float32)
        time_maa_v = (1.0 - (ddd ** r1 + 0.3 * r0)).astype(np.float32)
        time_maa_r = (1.0 - ddd ** (0.5 * r1)).astype(np.float32)
        time_maa_g = (1.0 - ddd ** (0.5 * r1)).astype(np.float32)
        n = np.arange(C, dtype=np.float64)
        time_decay = (-6.0 + 5.0 * (n / (C - 1)) ** (0.7 + 1.3 * r0)).astype(np.float32)
        zig = ((n + 1) % 3 - 1) * 0.1
        time_faaaa = (r0 * (1 - n / (C - 1)) + zig).astype(np.float32).reshape(N_HEAD, HEAD_SIZE)
        s = 1.0 / np.sqrt(C)
        inp = {'x': jax.random.normal(ks[0], (B, T, C), jnp.float32), 'time_maa_x': jnp.asarray(time_maa_x), 'time_maa_w': jnp.asarray(time_maa_w), 'time_maa_k': jnp.asarray(time_maa_k), 'time_maa_v': jnp.asarray(time_maa_v), 'time_maa_r': jnp.asarray(time_maa_r), 'time_maa_g': jnp.asarray(time_maa_g), 'time_maa_w1': jax.random.uniform(ks[1], (C, TM_DIM * 5), jnp.float32, -0.01, 0.01), 'time_maa_w2': jax.random.uniform(ks[2], (5, TM_DIM, C), jnp.float32, -0.01, 0.01), 'time_decay': jnp.asarray(time_decay), 'time_decay_w1': jax.random.uniform(ks[3], (C, TD_DIM), jnp.float32, -0.01, 0.01), 'time_decay_w2': jax.random.uniform(ks[4], (TD_DIM, C), jnp.float32, -0.01, 0.01), 'time_faaaa': jnp.asarray(time_faaaa), 'W_r': jax.random.normal(ks[5], (C, C), jnp.float32) * s, 'W_k': jax.random.normal(ks[6], (C, C), jnp.float32) * s, 'W_v': jax.random.normal(ks[7], (C, C), jnp.float32) * s, 'W_g': jax.random.normal(ks[8], (C, C), jnp.float32) * s, 'W_o': jax.random.normal(ks[9], (C, C), jnp.float32) * s, 'ln_gamma': jnp.ones((C,), jnp.float32), 'ln_beta': jnp.zeros((C,), jnp.float32)}
        return inp
    _L0_attn_in = _L0_attn_setup()

    def _L0_ffn_setup():
        import jax, jax.numpy as jnp
        import numpy as np
        B, N, C, H, REG = (1, 2309, 128, 16, 5)
        D = C // H
        key = jax.random.key(seed)
        k0, k1, k2, k3 = jax.random.split(key, 4)
        x = jax.random.normal(k0, (B, N, C), dtype=jnp.float32)
        g_info = jax.random.normal(k1, (12, 2, C), dtype=jnp.float32)
        W_qkv = jax.random.normal(k2, (C, 3 * C), dtype=jnp.float32) * 0.02
        W_proj = jax.random.normal(k3, (C, C), dtype=jnp.float32) * 0.02
        b_proj = jnp.zeros((C,), dtype=jnp.float32)
        return {'x': x, 'g_info': g_info, 'W_qkv': W_qkv, 'W_proj': W_proj, 'b_proj': b_proj}
    _L0_ffn_in = _L0_ffn_setup()

    def _L1_attn_setup():
        import jax, jax.numpy as jnp
        import numpy as np
        B, L, D_IN = (2, 256, 128)
        HD, N = (512, 16)
        BASE_FREQ = 10000.0

        def _hd_ssm(hd, a_log, b_proj, c_proj, dt_proj, skip_proj, floquet_phases):
            Bsz, Ls, Dh = hd.shape
            pos = jnp.arange(Ls, dtype=hd.dtype)
            hd_enc = hd * jnp.cos(pos[:, None] * floquet_phases[None, :])
            dt = jax.nn.softplus(dt_proj)
            A = -jnp.exp(a_log)
            decay = jnp.exp(dt[:, None] * A[None, :])
            Bseq = jnp.einsum('bld,dn->bln', hd_enc, b_proj)
            Cseq = jnp.einsum('bld,dn->bln', hd_enc, c_proj)

            def step(h, inp):
                x_t, B_t, C_t = inp
                h = decay[None] * h + dt[None, :, None] * x_t[:, :, None] * B_t[:, None, :]
                y_t = jnp.einsum('bdn,bn->bd', h, C_t)
                return (h, y_t)
            h0 = jnp.zeros((Bsz, Dh, A.shape[0]), hd.dtype)
            xs = (hd_enc.transpose(1, 0, 2), Bseq.transpose(1, 0, 2), Cseq.transpose(1, 0, 2))
            _, y = jax.lax.scan(step, h0, xs)
            y = y.transpose(1, 0, 2)
            return y + jnp.einsum('bld,de->ble', hd, skip_proj)
        key = jax.random.key(seed)
        ks = jax.random.split(key, 8)
        glorot = lambda k, shp: jax.random.normal(k, shp, jnp.float32) * jnp.sqrt(2.0 / (shp[0] + shp[1]))
        x = jax.random.normal(ks[0], (B, L, D_IN), jnp.float32)
        input_proj = glorot(ks[1], (D_IN, HD))
        output_proj = glorot(ks[2], (HD, D_IN))
        a_log = jax.random.uniform(ks[3], (N,), jnp.float32, -4.0, -1.0)
        b_proj = glorot(ks[4], (HD, N))
        c_proj = glorot(ks[5], (HD, N))
        dt_proj = jnp.full((HD,), 0.01, jnp.float32)
        skip_proj = jnp.eye(HD, dtype=jnp.float32)
        d = jnp.arange(HD, dtype=jnp.float32)
        floquet_phases = jnp.power(BASE_FREQ, -2.0 * d / HD)
        return {'x': x, 'input_proj': input_proj, 'output_proj': output_proj, 'a_log': a_log, 'b_proj': b_proj, 'c_proj': c_proj, 'dt_proj': dt_proj, 'skip_proj': skip_proj, 'floquet_phases': floquet_phases}
    _L1_attn_in = _L1_attn_setup()

    def _L1_ffn_setup():
        import jax, jax.numpy as jnp
        import numpy as np
        D_MODEL = 128
        D_FF = 512
        NUM_EXPERTS = 8
        TOP_K = 2
        B, S = (4, 512)
        key = jax.random.key(seed)
        ks = jax.random.split(key, 7)
        s_dm = 1.0 / np.sqrt(D_MODEL)
        s_ff = 1.0 / np.sqrt(D_FF)
        return {'x': jax.random.normal(ks[0], (B, S, D_MODEL), jnp.float32), 'router_w': jax.random.normal(ks[1], (D_MODEL, NUM_EXPERTS), jnp.float32) * s_dm, 'router_b': jnp.zeros((NUM_EXPERTS,), jnp.float32), 'w1': jax.random.normal(ks[2], (NUM_EXPERTS, D_MODEL, D_FF), jnp.float32) * s_dm, 'b1': jnp.zeros((NUM_EXPERTS, D_FF), jnp.float32), 'w2': jax.random.normal(ks[3], (NUM_EXPERTS, D_FF, D_MODEL), jnp.float32) * s_ff, 'b2': jnp.zeros((NUM_EXPERTS, D_MODEL), jnp.float32)}
    _L1_ffn_in = _L1_ffn_setup()
    _d = {'L0_attn_x': _L0_attn_in['x'], 'L0_attn_time_maa_x': _L0_attn_in['time_maa_x'], 'L0_attn_time_maa_w': _L0_attn_in['time_maa_w'], 'L0_attn_time_maa_k': _L0_attn_in['time_maa_k'], 'L0_attn_time_maa_v': _L0_attn_in['time_maa_v'], 'L0_attn_time_maa_r': _L0_attn_in['time_maa_r'], 'L0_attn_time_maa_g': _L0_attn_in['time_maa_g'], 'L0_attn_time_maa_w1': _L0_attn_in['time_maa_w1'], 'L0_attn_time_maa_w2': _L0_attn_in['time_maa_w2'], 'L0_attn_time_decay': _L0_attn_in['time_decay'], 'L0_attn_time_decay_w1': _L0_attn_in['time_decay_w1'], 'L0_attn_time_decay_w2': _L0_attn_in['time_decay_w2'], 'L0_attn_time_faaaa': _L0_attn_in['time_faaaa'], 'L0_attn_W_r': _L0_attn_in['W_r'], 'L0_attn_W_k': _L0_attn_in['W_k'], 'L0_attn_W_v': _L0_attn_in['W_v'], 'L0_attn_W_g': _L0_attn_in['W_g'], 'L0_attn_W_o': _L0_attn_in['W_o'], 'L0_attn_ln_gamma': _L0_attn_in['ln_gamma'], 'L0_attn_ln_beta': _L0_attn_in['ln_beta'], 'L0_ffn_g_info': _L0_ffn_in['g_info'], 'L0_ffn_W_qkv': _L0_ffn_in['W_qkv'], 'L0_ffn_W_proj': _L0_ffn_in['W_proj'], 'L0_ffn_b_proj': _L0_ffn_in['b_proj'], 'L1_attn_input_proj': _L1_attn_in['input_proj'], 'L1_attn_output_proj': _L1_attn_in['output_proj'], 'L1_attn_a_log': _L1_attn_in['a_log'], 'L1_attn_b_proj': _L1_attn_in['b_proj'], 'L1_attn_c_proj': _L1_attn_in['c_proj'], 'L1_attn_dt_proj': _L1_attn_in['dt_proj'], 'L1_attn_skip_proj': _L1_attn_in['skip_proj'], 'L1_attn_floquet_phases': _L1_attn_in['floquet_phases'], 'L1_ffn_router_w': _L1_ffn_in['router_w'], 'L1_ffn_router_b': _L1_ffn_in['router_b'], 'L1_ffn_w1': _L1_ffn_in['w1'], 'L1_ffn_b1': _L1_ffn_in['b1'], 'L1_ffn_w2': _L1_ffn_in['w2'], 'L1_ffn_b2': _L1_ffn_in['b2']}
    _x0 = _d['L0_attn_x']
    _d['L0_attn_x'] = jax.random.normal(jax.random.fold_in(jax.random.key(seed), 1), (2, 1024, 128), dtype=_x0.dtype)
    del _x0
    return _d

def reference(L0_attn_x, L0_attn_time_maa_x, L0_attn_time_maa_w, L0_attn_time_maa_k, L0_attn_time_maa_v, L0_attn_time_maa_r, L0_attn_time_maa_g, L0_attn_time_maa_w1, L0_attn_time_maa_w2, L0_attn_time_decay, L0_attn_time_decay_w1, L0_attn_time_decay_w2, L0_attn_time_faaaa, L0_attn_W_r, L0_attn_W_k, L0_attn_W_v, L0_attn_W_g, L0_attn_W_o, L0_attn_ln_gamma, L0_attn_ln_beta, L0_ffn_g_info, L0_ffn_W_qkv, L0_ffn_W_proj, L0_ffn_b_proj, L1_attn_input_proj, L1_attn_output_proj, L1_attn_a_log, L1_attn_b_proj, L1_attn_c_proj, L1_attn_dt_proj, L1_attn_skip_proj, L1_attn_floquet_phases, L1_ffn_router_w, L1_ffn_router_b, L1_ffn_w1, L1_ffn_b1, L1_ffn_w2, L1_ffn_b2):

    def _L0_attn_ref(x, time_maa_x, time_maa_w, time_maa_k, time_maa_v, time_maa_r, time_maa_g, time_maa_w1, time_maa_w2, time_decay, time_decay_w1, time_decay_w2, time_faaaa, W_r, W_k, W_v, W_g, W_o, ln_gamma, ln_beta):
        import jax, jax.numpy as jnp
        import numpy as np
        D_MODEL = 128
        N_HEAD = 16
        HEAD_SIZE = D_MODEL // N_HEAD
        LAYER_ID = 12
        N_LAYER = 24
        HEAD_SIZE_DIVISOR = 8
        TM_DIM = 32
        TD_DIM = 64
        B, T = (4, 128)
        EPS = 1e-05 * HEAD_SIZE_DIVISOR ** 2

        def _wkv6(r, k, v, w, u):
            Bc, Tc, H, K = r.shape
            wdec = jnp.exp(-jnp.exp(w))

            def step(S, inp):
                r_t, k_t, v_t, wd_t = inp
                kv = k_t[:, :, :, None] * v_t[:, :, None, :]
                y = jnp.einsum('bhk,bhkj->bhj', r_t, S + u[None, :, :, None] * kv)
                S = S * wd_t[:, :, :, None] + kv
                return (S, y)
            S0 = jnp.zeros((Bc, H, K, K), r.dtype)
            xs = (jnp.swapaxes(r, 0, 1), jnp.swapaxes(k, 0, 1), jnp.swapaxes(v, 0, 1), jnp.swapaxes(wdec, 0, 1))
            _, ys = jax.lax.scan(step, S0, xs)
            return jnp.swapaxes(ys, 0, 1).reshape(Bc, Tc, H * K)
        Bc, Tc, C = x.shape
        H, K = (N_HEAD, HEAD_SIZE)
        xs = jnp.pad(x, ((0, 0), (1, 0), (0, 0)))[:, :-1]
        xx = xs - x
        xxx = x + xx * time_maa_x
        m = jnp.tanh(xxx @ time_maa_w1).reshape(Bc, Tc, 5, TM_DIM)
        m = jnp.einsum('btfe,fec->fbtc', m, time_maa_w2)
        mw, mk, mv, mr, mg = (m[0], m[1], m[2], m[3], m[4])
        xw = x + xx * (time_maa_w + mw)
        xk = x + xx * (time_maa_k + mk)
        xv = x + xx * (time_maa_v + mv)
        xr = x + xx * (time_maa_r + mr)
        xg = x + xx * (time_maa_g + mg)
        r = xr @ W_r
        k = xk @ W_k
        v = xv @ W_v
        g = jax.nn.silu(xg @ W_g)
        w = time_decay + jnp.tanh(xw @ time_decay_w1) @ time_decay_w2
        y = _wkv6(r.reshape(Bc, Tc, H, K), k.reshape(Bc, Tc, H, K), v.reshape(Bc, Tc, H, K), w.reshape(Bc, Tc, H, K), time_faaaa)
        yg = y.reshape(Bc, Tc, H, K)
        mu = jnp.mean(yg, axis=-1, keepdims=True)
        var = jnp.mean((yg - mu) ** 2, axis=-1, keepdims=True)
        yn = ((yg - mu) / jnp.sqrt(var + EPS)).reshape(Bc, Tc, C)
        yn = yn * ln_gamma + ln_beta
        return yn * g @ W_o

    def _L0_ffn_ref(x, g_info, W_qkv, W_proj, b_proj):
        import jax, jax.numpy as jnp
        import numpy as np
        B, N, C, H, REG = (1, 2309, 128, 16, 5)
        D = C // H
        Bx, Nx, Cx = x.shape
        scale = D ** (-0.5)
        qkv = (x @ W_qkv).reshape(Bx, Nx, 3, H, D)
        q, k, v = (qkv[:, :, 0], qkv[:, :, 1], qkv[:, :, 2])
        g_layer = g_info[0].reshape(-1, H, D)
        q_g = g_layer[0]
        q_pure = q[:, REG:]
        q_n = q_pure / jnp.linalg.norm(q_pure, axis=-1, keepdims=True)
        qg_n = q_g / jnp.linalg.norm(q_g, axis=-1, keepdims=True)
        sim = (qg_n[None, None] * q_n).sum(-1).mean(-1)
        sim = (sim - sim.min()) / (sim.max() - sim.min())
        pos = sim > 0.9
        logits = jnp.einsum('bqhd,bkhd->bhqk', q * scale, k)

        def masked_attn(tok_mask):
            key_mask = jnp.concatenate([jnp.ones((Bx, REG), bool), tok_mask], axis=1)
            l = jnp.where(key_mask[:, None, None, :], logits, -jnp.inf)
            a = jax.nn.softmax(l, axis=-1)
            return jnp.einsum('bhqk,bkhd->bqhd', a, v)
        x_pos = masked_attn(pos)
        x_neg = masked_attn(~pos)
        reg_out = (x_pos[:, :REG] + x_neg[:, :REG]) * 0.5
        tok_out = jnp.where(pos[:, :, None, None], x_pos[:, REG:], x_neg[:, REG:])
        out = jnp.concatenate([reg_out, tok_out], axis=1).reshape(Bx, Nx, Cx)
        return out @ W_proj + b_proj

    def _L1_attn_ref(x, input_proj, output_proj, a_log, b_proj, c_proj, dt_proj, skip_proj, floquet_phases):
        import jax, jax.numpy as jnp
        import numpy as np
        B, L, D_IN = (2, 256, 128)
        HD, N = (512, 16)
        BASE_FREQ = 10000.0

        def _hd_ssm(hd, a_log, b_proj, c_proj, dt_proj, skip_proj, floquet_phases):
            Bsz, Ls, Dh = hd.shape
            pos = jnp.arange(Ls, dtype=hd.dtype)
            hd_enc = hd * jnp.cos(pos[:, None] * floquet_phases[None, :])
            dt = jax.nn.softplus(dt_proj)
            A = -jnp.exp(a_log)
            decay = jnp.exp(dt[:, None] * A[None, :])
            Bseq = jnp.einsum('bld,dn->bln', hd_enc, b_proj)
            Cseq = jnp.einsum('bld,dn->bln', hd_enc, c_proj)

            def step(h, inp):
                x_t, B_t, C_t = inp
                h = decay[None] * h + dt[None, :, None] * x_t[:, :, None] * B_t[:, None, :]
                y_t = jnp.einsum('bdn,bn->bd', h, C_t)
                return (h, y_t)
            h0 = jnp.zeros((Bsz, Dh, A.shape[0]), hd.dtype)
            xs = (hd_enc.transpose(1, 0, 2), Bseq.transpose(1, 0, 2), Cseq.transpose(1, 0, 2))
            _, y = jax.lax.scan(step, h0, xs)
            y = y.transpose(1, 0, 2)
            return y + jnp.einsum('bld,de->ble', hd, skip_proj)
        hd = jnp.einsum('bld,dh->blh', x, input_proj)
        out_hd = _hd_ssm(hd, a_log, b_proj, c_proj, dt_proj, skip_proj, floquet_phases)
        return jnp.einsum('blh,hd->bld', out_hd, output_proj)

    def _L1_ffn_ref(x, router_w, router_b, w1, b1, w2, b2):
        import jax, jax.numpy as jnp
        import numpy as np
        D_MODEL = 128
        D_FF = 512
        NUM_EXPERTS = 8
        TOP_K = 2
        B, S = (4, 512)
        Bx, Sx, D = x.shape
        xf = x.reshape(-1, D)
        logits = xf @ router_w + router_b
        top_w, sel = jax.lax.top_k(logits, TOP_K)
        gates = jax.nn.softmax(top_w, axis=-1)

        def body(i, acc):
            h = jax.nn.gelu(xf @ w1[i] + b1[i], approximate=False)
            out_i = h @ w2[i] + b2[i]
            gate_i = jnp.sum(gates * (sel == i), axis=-1, keepdims=True)
            return acc + out_i * gate_i
        out = jax.lax.fori_loop(0, NUM_EXPERTS, body, jnp.zeros_like(xf))
        return out.reshape(Bx, Sx, D)
    x = L0_attn_x
    x = x + 0.5 * _L0_ffn_ref(_layernorm(x, axis=-1), L0_ffn_g_info, L0_ffn_W_qkv, L0_ffn_W_proj, L0_ffn_b_proj)
    x = x + _L0_attn_ref(_layernorm(x, axis=-1), L0_attn_time_maa_x, L0_attn_time_maa_w, L0_attn_time_maa_k, L0_attn_time_maa_v, L0_attn_time_maa_r, L0_attn_time_maa_g, L0_attn_time_maa_w1, L0_attn_time_maa_w2, L0_attn_time_decay, L0_attn_time_decay_w1, L0_attn_time_decay_w2, L0_attn_time_faaaa, L0_attn_W_r, L0_attn_W_k, L0_attn_W_v, L0_attn_W_g, L0_attn_W_o, L0_attn_ln_gamma, L0_attn_ln_beta)
    x = x + 0.5 * _L0_ffn_ref(_layernorm(x, axis=-1), L0_ffn_g_info, L0_ffn_W_qkv, L0_ffn_W_proj, L0_ffn_b_proj)
    x = x + 0.5 * _L1_ffn_ref(_layernorm(x, axis=-1), L1_ffn_router_w, L1_ffn_router_b, L1_ffn_w1, L1_ffn_b1, L1_ffn_w2, L1_ffn_b2)
    x = x + _L1_attn_ref(_layernorm(x, axis=-1), L1_attn_input_proj, L1_attn_output_proj, L1_attn_a_log, L1_attn_b_proj, L1_attn_c_proj, L1_attn_dt_proj, L1_attn_skip_proj, L1_attn_floquet_phases)
    x = x + 0.5 * _L1_ffn_ref(_layernorm(x, axis=-1), L1_ffn_router_w, L1_ffn_router_b, L1_ffn_w1, L1_ffn_b1, L1_ffn_w2, L1_ffn_b2)
    return x

_drawn_inputs = setup_inputs


def setup_inputs(seed=0):
    import zlib

    import numpy as np

    out = dict(_drawn_inputs(seed))
    spreads = {'L0_attn_ln_gamma': (1.0, 0.2),
     'L0_attn_ln_beta': (0.0, 0.1),
     'L0_ffn_b_proj': (0.0, 0.1),
     'L1_attn_dt_proj': (0.009999999776482582, 0.6),
     'L1_ffn_router_b': (0.0, 0.1),
     'L1_ffn_b1': (0.0, 0.1),
     'L1_ffn_b2': (0.0, 0.1)}
    factors = {'L0_attn_time_maa_x': 8.0,
     'L0_attn_time_maa_w': 8.0,
     'L0_attn_time_maa_w1': 4.832,
     'L0_attn_time_maa_w2': 4.447,
     'L0_attn_time_decay_w1': 8.0,
     'L0_attn_time_decay_w2': 8.0,
     'L0_ffn_g_info': 8.0,
     'L0_ffn_W_qkv': 5.069,
     'L0_ffn_W_proj': 4.946}
    for name, (base, spread) in spreads.items():
        noise = np.random.default_rng([zlib.crc32(name.encode()), seed]).standard_normal(out[name].shape)
        drawn = base * np.exp(spread * noise) if base else spread * noise
        out[name] = jnp.asarray(drawn.astype(out[name].dtype))
    for name, factor in factors.items():
        out[name] = (out[name] * factor).astype(out[name].dtype)
    return out
```

```python
import concourse.bass as bass
from concourse import mybir
from contextlib import ExitStack

F32 = mybir.dt.float32
BF16 = mybir.dt.bfloat16
U32 = mybir.dt.uint32
ALU = mybir.AluOpType
ACT = mybir.ActivationFunctionType
AX_X = mybir.AxisListType.X

P = 128
B, T, C = 2, 1024, 128
TOK = B * T
NT = TOK // P
TPB = T // P
H, D = 16, 8
BANK = 512
NCH = TOK // BANK
LN_EPS = 1e-5


class Env:
    pass


class Sublayer:

    def __init__(self, parts, done):
        self.parts, self.done = parts, done


class LayerNorm:

    def __init__(self, dve, pool, pe, act, ready):
        self.dve, self.pool, self.pe, self.act, self.ready = dve, pool, pe, act, ready


class Chain:

    def __init__(self, eng, sem):
        self.eng, self.sem, self.base, self.n = eng, sem, 0, 0

    def __call__(self, ins):
        self.n += 1
        ins.then_inc(self.sem, 1)
        self.eng.wait_ge(self.sem, self.base + self.n)


def layer_norm(nc, env, tag, xn_cm, banks):
    sb, sem, x, ident = env.sb, env.sem, env.x, env.ident
    stats = sb(f"{tag}_stats", [P, NT, 6], F32)
    mv = sb(f"{tag}_mv", [P, NT, 2], F32)
    var_eps = sb(f"{tag}_var_eps", [P, NT], F32)
    rstd = sb(f"{tag}_rstd", [P, NT], F32)
    xn_tm = sb(f"{tag}_xn_tm", [P, NT, C], F32)
    stat_step = sem(f"{tag}_stat_step")
    var_ready = sem(f"{tag}_var_ready")
    rstd_ready = sem(f"{tag}_rstd_ready")
    xn_tm_ready = sem(f"{tag}_xn_tm_ready")
    transposed = sem(f"{tag}_transposed")
    xn_ready = sem(f"{tag}_xn_ready")

    def dve(v):
        for t in range(NT):
            nc.vector.bn_stats(stats[:, t, :], x[:, t, :]).then_inc(stat_step, 1)
        for t in range(NT):
            v.wait_ge(stat_step, t + 1)
            nc.vector.bn_aggr(mv[:, t, :], stats[:, t, :]).then_inc(stat_step, 1)
        v.wait_ge(stat_step, 2 * NT)
        nc.vector.tensor_scalar(var_eps[:], mv[:, :, 1], LN_EPS, None, ALU.add).then_inc(var_ready, 1)
        v.wait_ge(rstd_ready, 1)
        for t in range(NT):
            nc.vector.tensor_scalar(xn_tm[:, t, :], x[:, t, :], mv[:, t, 0:1], rstd[:, t:t + 1],
                                    ALU.subtract, ALU.mult).then_inc(xn_tm_ready, 1)

    def pool(g):
        g.wait_ge(var_ready, 1)
        nc.gpsimd.tensor_tensor(rstd[:], var_eps[:], env.minus_half[:, 0:NT], ALU.pow).then_inc(rstd_ready, 1)

    def pe(t_):
        for k in range(NCH):
            if k >= 2:
                t_.wait_ge(xn_ready, k - 1)
            for j in range(4):
                t_.wait_ge(xn_tm_ready, 4 * k + j + 1)
                last = nc.tensor.transpose(banks[k % 2][:, j * P:(j + 1) * P], xn_tm[:, 4 * k + j, :], ident[:])
            last.then_inc(transposed, 1)

    def act(s):
        for k in range(NCH):
            s.wait_ge(transposed, k + 1)
            nc.scalar.activation(xn_cm[:, k * BANK:(k + 1) * BANK], banks[k % 2], ACT.Copy).then_inc(xn_ready, 1)

    return LayerNorm(dve=dve, pool=pool, pe=pe, act=act, ready=xn_ready)


REG = 5
XQ = 32
QW = T + XQ
NQ = T + REG
QC = NQ // 3
KT = T // P
ROWS_S = 2 + 6 * D
ROWS = ROWS_S + 3
NQUAD = B * H // 4
SLOTS = 3
MC = 4 * TPB + 1
HALVES = 2 * MC
BIG = 1e30
Q_PARTS = [0, 0, 1, 1, 0, 2]
K_PARTS = [0, 1, 0, 1, 2, 0]


def attention(nc, env, tag):
    ctx = env.open()
    sb, sem, x = env.sb, env.sem, env.x
    ps = env.ps
    bank = [ps[:, i, :] for i in range(8)]

    QS = env.dram(f"{tag}_QS", [B * H, ROWS, QW], BF16)
    KS = env.dram(f"{tag}_KS", [B * H, ROWS_S, T], BF16)
    MR = env.dram(f"{tag}_MR", [4, TOK], BF16)
    CX = env.dram(f"{tag}_CX", [2, XQ], BF16)
    MD = env.dram(f"{tag}_MD", [SLOTS, 3, MC * P], BF16)

    QX = [sb(f"{tag}_QX{i}", [P, 4, QW], BF16) for i in range(SLOTS)]
    KX = [sb(f"{tag}_KX{i}", [P, 2, T], BF16) for i in range(SLOTS)]
    VX = [sb(f"{tag}_VX{i}", [P, KT, 4, 32], F32) for i in range(SLOTS)]
    vq = sb(f"{tag}_vq", [P, NQUAD, KT, 4 * D], F32)
    PR = 4
    prob = [sb(f"{tag}_prob{i}", [P, 2, QC], F32) for i in range(PR)]
    mx = sb(f"{tag}_mx", [P, 2, MC], F32)
    neg = sb(f"{tag}_neg", [P, MC], F32)
    rest = sb(f"{tag}_rest", [P, MC], F32)
    msplit = sb(f"{tag}_msplit", [P, 3, MC], BF16)
    mT = sb(f"{tag}_mT", [3 * MC, P], BF16)
    ast = [sb(f"{tag}_ast{i}", [P, NQ], F32) for i in range(SLOTS)]
    xb = sb(f"{tag}_xb", [P, NT, C], F32)
    tiny = sb(f"{tag}_tiny", [P, 64], F32)
    mark = env.mark()
    xn = sb(f"{tag}_xn", [P, TOK], F32)
    qf = sb(f"{tag}_qf", [P, B, QW], F32)
    kf = sb(f"{tag}_kf", [P, B, T], F32)
    qpart = [sb(f"{tag}_qp{i}", [P, B, QW], BF16) for i in range(3)]
    kpart = [sb(f"{tag}_kp{i}", [P, B, T], BF16) for i in range(3)]
    q_tm = sb(f"{tag}_q_tm", [P, NT, C], F32)
    work = sb(f"{tag}_work", [P, NT, C], F32)
    n2 = sb(f"{tag}_n2", [P, NT, H], F32)
    rn = sb(f"{tag}_rn", [P, NT, H], F32)
    dot = sb(f"{tag}_dot", [P, NT, H], F32)
    sim = sb(f"{tag}_sim", [P, NT], F32)
    ext = sb(f"{tag}_ext", [P, 2, NT], F32)
    mm2 = sb(f"{tag}_mm2", [P, 2], F32)
    mm2a = sb(f"{tag}_mm2a", [P, 2], F32)
    masks = sb(f"{tag}_masks", [P, 4, NT], F32)
    pos = sb(f"{tag}_pos", [P, NT], F32)
    mrow = sb(f"{tag}_mrow", [4 * NT, P], BF16)
    cx = sb(f"{tag}_cx", [2, XQ], BF16)
    ln = layer_norm(nc, env, f"{tag}_ln", xn, [bank[4], bank[5]])
    env.rewind(mark)
    A = sb(f"{tag}_A", [P, NQUAD, NQ], F32)
    o_tm = sb(f"{tag}_o_tm", [P, NT, C], F32)
    o_cm = sb(f"{tag}_o_cm", [P, NT, P], F32)
    rden = sb(f"{tag}_rden", [P, NT + B, H], F32)
    ox = sb(f"{tag}_ox", [REG, B, C], F32)
    env.close(ctx)

    s = lambda n: sem(f"{tag}_{n}")
    proj_mm, proj_out, qk_out = s("proj_mm"), s("proj_out"), s("qk_out")
    padded, high_q, rest_q, mid_q, low_q = s("padded"), s("high_q"), s("rest_q"), s("mid_q"), s("low_q")
    high_k, rest_k, mid_k, low_k = s("high_k"), s("rest_k"), s("mid_k"), s("low_k")
    n2_ready, rn_ready, mm_ready, mm_all = s("n2_ready"), s("rn_ready"), s("mm_ready"), s("mm_all")
    masks_ready, masks_t, mrow_ready, cx_ready = s("masks_ready"), s("masks_t"), s("mrow_ready"), s("cx_ready")
    rows_out, consts_out, parts_out, zeros_ready = s("rows_out"), s("consts_out"), s("parts_out"), s("zeros_ready")
    loaded = [s(f"loaded{i}") for i in range(SLOTS)]
    m_saved = [s(f"m_saved{i}") for i in range(SLOTS)]
    m_loaded = [s(f"m_loaded{i}") for i in range(SLOTS)]
    a_free = [s(f"a_free{i}") for i in range(SLOTS)]
    score_ready, score_free = s("score_ready"), s("score_free")
    msplit_ready, m_t, mT_ready = s("msplit_ready"), s("m_t"), s("mT_ready")
    v_ready = s("v_ready")
    st_ready, exp_done, prob_free = s("st_ready"), s("exp_done"), s("prob_free")
    sums_out = s("sums_out")
    chain_sem = s("dve_step")
    fin_t, fin_o, fin_xt, fin_b, fin_oc, fin_p = s("fin_t"), s("fin_o"), s("fin_xt"), s("fin_b"), s("fin_oc"), s("fin_p")
    x_done, passed = s("x_done"), s("passed")
    STEPS = 3 * KT

    score = [bank[4], bank[5]]
    acc = [bank[6], bank[7]]

    def sp(e):
        def rows_of(dst, part, b, j, width):
            e.dma_start(dst[b * H:(b + 1) * H, 2 + D * j:2 + D * j + D, 0:width],
                        part[:, b, 0:width]).then_inc(parts_out, 16)
        e.wait_ge(cx_ready, 2)
        e.dma_start(CX, cx[:, :]).then_inc(consts_out, 16)
        for part, (q_sem, k_sem) in enumerate(((high_q, high_k), (mid_q, mid_k), (low_q, low_k))):
            for dst, tiles, table, ready, width in ((QS, qpart, Q_PARTS, q_sem, QW), (KS, kpart, K_PARTS, k_sem, T)):
                e.wait_ge(ready, 1)
                for j in range(6):
                    if table[j] == part:
                        for b in range(B):
                            rows_of(dst, tiles[part], b, j, width)
        e.wait_ge(mrow_ready, 1)
        e.dma_start(MR.rearrange("k (t p) -> (k t) p", p=P), mrow[:, :]).then_inc(rows_out, 16)
        e.wait_ge(zeros_ready, 3 * SLOTS)
        e.dma_start(QS[:, ROWS_S:ROWS, :], QX[0][0:B * H, 0:3, :]).then_inc(parts_out, 16)
        e.wait_ge(rows_out, 16)
        e.wait_ge(consts_out, 16)
        for b in range(B):
            heads = slice(b * H, (b + 1) * H)
            e.dma_start(QS[heads, 0:2, 0:T],
                        MR[0:2, b * T:(b + 1) * T].rearrange("(o k) n -> o k n", o=1).broadcast_to([H, 2, T]))\
                .then_inc(parts_out, 16)
            e.dma_start(KS[heads, 0:2, :],
                        MR[2:4, b * T:(b + 1) * T].rearrange("(o k) n -> o k n", o=1).broadcast_to([H, 2, T]))\
                .then_inc(parts_out, 16)
            e.dma_start(QS[heads, 0:2, T:QW], CX.rearrange("(o k) n -> o k n", o=1).broadcast_to([H, 2, XQ]))\
                .then_inc(parts_out, 16)
        e.wait_ge(parts_out, 16 * (12 * B + 3 * B + 1))

        def load(q, slot):
            for half in range(2):
                e.dma_start(QX[slot][64 * half:64 * half + ROWS, half::2, :],
                            QS[bass.ds(q * 4, 4)]
                            .rearrange("(p e) r n -> e r p n", e=2)[half]).then_inc(loaded[slot], 16)
                e.dma_start(KX[slot][64 * half:64 * half + ROWS_S, :, :],
                            KS[bass.ds(q * 4, 4)].rearrange("(p e) r n -> e r p n", e=2)[half])\
                    .then_inc(loaded[slot], 16)

        def maxima(q, slot, it):
            e.wait_ge(mT_ready, q + 1)
            e.dma_start(MD[slot].rearrange("j (c p) -> (j c) p", p=P), mT[:, :]).then_inc(m_saved[slot], 16)
            e.wait_ge(m_saved[slot], 16 * (it + 1))
            for half in range(2):
                rows = slice(64 * half + ROWS_S, 64 * half + ROWS)
                src = MD[slot][:, 0:4 * T].rearrange("j (p e n) -> e j p n", p=2, e=2)[half]
                e.dma_start(QX[slot][rows, half::2, 0:T], src).then_inc(m_loaded[slot], 16)
                src = MD[slot][:, 4 * T:].rearrange("j (p e n) -> e j p n", p=2, e=2)[half]
                e.dma_start(QX[slot][rows, half::2, T:QW], src).then_inc(m_loaded[slot], 16)

        def keep(q, slot):
            e.wait_ge(sums_out, 3 * q + 4)
            e.dma_start(A[:, bass.ds(q, 1), :].rearrange("p o n -> p (o n)"), ast[slot][:, :]).then_inc(a_free[slot], 16)

        for slot in range(SLOTS):
            e.sem_inc(a_free[slot], 16)
        load(0, 0)
        load(1, 1)
        maxima(0, 0, 0)
        with e.Fori(0, 2) as it:
            for u in range(3):
                q = it * 3 + u
                e.wait_ge(st_ready, q * (2 * STEPS) + 1)
                load(q + 2, (u + 2) % 3)
                maxima(q + 1, (u + 1) % 3, it + (1 if u == 2 else 0))
                keep(q, u)
        maxima(7, 1, 2)
        keep(6, 0)
        keep(7, 1)
        for slot in range(SLOTS):
            e.wait_ge(a_free[slot], 16 * (4 if slot < 2 else 3))

    def pool(g):
        for i in range(SLOTS):
            nc.gpsimd.memset(KX[i][:, :, :], 1.0).then_inc(zeros_ready, 1)
            nc.gpsimd.memset(QX[i][:, :, :], 0.0).then_inc(zeros_ready, 1)
            nc.gpsimd.memset(VX[i][:, :, :, :], 0.0).then_inc(zeros_ready, 1)
        nc.gpsimd.memset(qf[:, :, NQ:QW], 0.0).then_inc(padded, 1)
        nc.gpsimd.memset(cx[:], 0.0).then_inc(cx_ready, 1)
        g.wait_ge(cx_ready, 1)
        nc.gpsimd.memset(cx[0:1, 0:REG], 1.0).then_inc(cx_ready, 1)
        g.wait_ge(zeros_ready, 3 * SLOTS)
        for i in range(SLOTS):
            nc.gpsimd.memset(VX[i][:, :, :, D:D + 1], 1.0).then_inc(padded, 1)
        ln.pool(g)
        g.wait_ge(high_k, 1)
        nc.gpsimd.tensor_tensor(kf[:], kf[:], kpart[0][:], ALU.subtract).then_inc(rest_k, 1)
        g.wait_ge(n2_ready, 1)
        nc.gpsimd.tensor_tensor(rn[:], n2[:], env.minus_half[:, 0:NT * H].rearrange("p (t h) -> p t h", h=H),
                                ALU.pow).then_inc(rn_ready, 1)
        g.wait_ge(mid_k, 1)
        nc.gpsimd.tensor_tensor(kpart[2][:], kf[:], kpart[1][:], ALU.subtract).then_inc(low_k, 1)
        g.wait_ge(mm_ready, 1)
        nc.gpsimd.partition_all_reduce(mm2a[:], mm2[:], P, env.rmax).then_inc(mm_all, 1)

    def act(a):
        ln.act(a)
        for j in range(8):
            c, is_k = j // 2, j % 2
            b, half = c // 2, c % 2
            a.wait_ge(proj_mm, j + 1)
            dst = (kf if is_k else qf)[:, b, half * BANK:(half + 1) * BANK]
            nc.scalar.activation(dst, bank[j % 4], ACT.Copy, scale=1.0 if is_k else D ** -0.5).then_inc(proj_out, 1)
        a.wait_ge(proj_out, 8)
        nc.scalar.activation(kpart[0][:], kf[:], ACT.Copy).then_inc(high_k, 1)
        for j in range(8, 16):
            t0 = 2 * (j - 8)
            b, k0 = t0 // KT, t0 % KT
            a.wait_ge(proj_mm, j + 1)
            both = bank[j % 4].rearrange("p (t c) -> p t c", t=2)
            nc.scalar.activation(q_tm[:, t0:t0 + 2, :], both[:, :, 0:C], ACT.Copy).then_inc(qk_out, 1)
            for t in range(2):
                last = nc.scalar.activation(vq[:, 4 * b:4 * b + 4, k0 + t, :],
                                            both[:, t, C:2 * C].rearrange("p (q n) -> p q n", q=4), ACT.Copy)
            last.then_inc(proj_out, 1)
        a.wait_ge(padded, SLOTS + 2)
        nc.scalar.activation(qpart[0][:], qf[:], ACT.Copy).then_inc(high_q, 1)
        a.wait_ge(rest_k, 1)
        nc.scalar.activation(kpart[1][:], kf[:], ACT.Copy).then_inc(mid_k, 1)
        a.wait_ge(rest_q, 1)
        nc.scalar.activation(qpart[1][:], qf[:], ACT.Copy).then_inc(mid_q, 1)
        a.wait_ge(masks_t, 1)
        nc.scalar.activation(mrow[:, :], bank[0][0:4 * NT, 0:P], ACT.Copy).then_inc(mrow_ready, 1)
        a.sem_inc(exp_done, 2)
        a.sem_inc(sums_out, 1)

        def quad(q, slot, it):
            for i in range(STEPS):
                for p in range(2):
                    n = 2 * i + p
                    a.wait_ge(prob_free, q * STEPS + i + 1)
                    a.wait_ge(st_ready, q * 2 * STEPS + n + 1)
                    nc.scalar.activation(prob[n % PR][:, :, :], ps[:, 2 * (n % 2):2 * (n % 2) + 2, 0:QC], ACT.Exp)\
                        .then_inc(exp_done, 1)
                if i % KT == 1 and i > KT:
                    copy_sums(q, slot, it, i // KT - 1)
            copy_sums(q, slot, it, 2)

        def copy_sums(q, slot, it, c):
            a.wait_ge(prob_free, q * STEPS + (c + 1) * KT + 2)
            if c == 0:
                a.wait_ge(a_free[slot], 16 * (it + 1))
            nc.scalar.activation(ast[slot][:, c * QC:(c + 1) * QC], acc_of(c)[:, 0:QC], ACT.Copy)\
                .then_inc(sums_out, 1)

        with a.Fori(0, 2) as it:
            for u in range(3):
                quad(it * 3 + u, u, it)
        quad(6, 0, 2)
        quad(7, 1, 2)
        for t in range(NT):
            a.wait_ge(fin_b, t + 1)
            nc.scalar.activation(o_cm[:, t, :], bank[2 + t % 2][:, 0:P], ACT.Copy).then_inc(fin_oc, 1)

    def acc_of(c):
        return acc[c % 2]

    def dve(v):
        ln.dve(v)
        ch = Chain(v, chain_sem)
        v.wait_ge(ln.ready, NCH)
        ch(nc.vector.tensor_tensor(xb[:], x[:], env.half_bproj.unsqueeze(1).broadcast_to([P, NT, C]), ALU.add))
        v.wait_ge(proj_out, 8)
        v.wait_ge(padded, 1)
        nc.vector.tensor_copy(qf[:, :, T:NQ], qf[:, :, 0:REG]).then_inc(padded, 1)
        v.wait_ge(qk_out, 8)
        heads = lambda ap: ap.rearrange("p t (h d) -> p t h d", d=D)
        ch(nc.vector.tensor_tensor(work[:], q_tm[:], q_tm[:], ALU.mult))
        nc.vector.reduce_sum(n2[:], heads(work[:]), AX_X).then_inc(n2_ready, 1)
        v.wait_ge(n2_ready, 1)
        v.wait_ge(high_q, 1)
        nc.vector.tensor_tensor(qf[:], qf[:], qpart[0][:], ALU.subtract).then_inc(rest_q, 1)
        ch(nc.vector.tensor_tensor(work[:], q_tm[:], env.qg_unit.unsqueeze(1).broadcast_to([P, NT, C]), ALU.mult))
        ch(nc.vector.reduce_sum(dot[:], heads(work[:]), AX_X))
        v.wait_ge(rn_ready, 1)
        ch(nc.vector.tensor_tensor(dot[:], dot[:], rn[:], ALU.mult))
        ch(nc.vector.reduce_sum(sim[:], dot[:], AX_X))
        ch(nc.vector.tensor_scalar(ext[:, 0, :], sim[:], -1.0, None, ALU.mult))
        ch(nc.vector.tensor_copy(ext[:, 1, :], sim[:]))
        for b in range(B):
            ch(nc.vector.memset(ext[0:REG, :, b * TPB:b * TPB + 1], -3e38))
        nc.vector.reduce_max(mm2[:], ext[:], AX_X).then_inc(mm_ready, 1)
        v.wait_ge(mid_q, 1)
        nc.vector.tensor_tensor(qpart[2][:], qf[:], qpart[1][:], ALU.subtract).then_inc(low_q, 1)
        v.wait_ge(mm_all, 1)
        ch(nc.vector.tensor_tensor(tiny[:, 0:1], mm2a[:, 0:1], mm2a[:, 1:2], ALU.add))
        ch(nc.vector.reciprocal(tiny[:, 1:2], tiny[:, 0:1]))
        ch(nc.vector.tensor_scalar(pos[:], sim[:], mm2a[:, 0:1], tiny[:, 1:2], ALU.add, ALU.mult))
        ch(nc.vector.tensor_scalar(pos[:], pos[:], 0.9, None, ALU.is_gt))
        ch(nc.vector.tensor_tensor(masks[:, 1, :], pos[:], env.is_reg[:], ALU.max))
        ch(nc.vector.tensor_scalar(masks[:, 0, :], masks[:, 1, :], -1.0, 1.0, ALU.mult, ALU.add))
        ch(nc.vector.tensor_scalar(masks[:, 3, :], masks[:, 0, :], -BIG, None, ALU.mult))
        ch(nc.vector.tensor_tensor(masks[:, 2, :], masks[:, 1, :], env.is_reg[:], ALU.subtract))
        nc.vector.tensor_scalar(masks[:, 2, :], masks[:, 2, :], -BIG, None, ALU.mult).then_inc(masks_ready, 1)
        v.wait_ge(zeros_ready, 3 * SLOTS)
        v.wait_ge(padded, 1 + SLOTS + 1)
        v.wait_ge(proj_out, 16)
        v.sem_inc(score_free, 2)
        per, first = 5, ch.n

        def maxima(q, slot, it):
            ch.base, ch.n = q * per + first, 0
            for k in range(HALVES):
                if k == HALVES // 2:
                    if it is not None:
                        v.wait_ge(prob_free, (q - 1) * STEPS + 2)
                    nc.vector.tensor_scalar(VX[slot][:, :, :, 0:D],
                                            vq[:, bass.ds(q, 1), :, :].rearrange("p o k (h d) -> p (o k) h d", d=D),
                                            1.0, None, ALU.mult).then_inc(v_ready, 1)
                col, half = k // 2, k % 2
                v.wait_ge(score_ready, q * HALVES + k + 1)
                nc.vector.reduce_max(mx[:, half, col:col + 1], score[k % 2], AX_X)\
                    .then_inc(score_free, 1)
            v.wait_ge(score_free, q * HALVES + HALVES + 2)
            ch(nc.vector.tensor_tensor(neg[:], mx[:, 0, :], mx[:, 1, :], ALU.max))
            ch(nc.vector.tensor_scalar(neg[:], neg[:], -1.0, None, ALU.mult))
            ch(nc.vector.tensor_scalar(msplit[:, 0, :], neg[:], 1.0, None, ALU.mult))
            ch(nc.vector.tensor_tensor(rest[:], neg[:], msplit[:, 0, :], ALU.subtract))
            ch(nc.vector.tensor_scalar(msplit[:, 1, :], rest[:], 1.0, None, ALU.mult))
            nc.vector.tensor_tensor(msplit[:, 2, :], rest[:], msplit[:, 1, :], ALU.subtract).then_inc(msplit_ready, 1)
            if it is not None:
                v.wait_ge(m_saved[(slot - 1) % SLOTS], 16 * it)
            v.wait_ge(m_t, q + 1)
            nc.vector.tensor_scalar(mT[:, :], score[0][:, 0:P // 2].bitcast(BF16)[0:3 * MC, :], 1.0, None, ALU.mult)\
                .then_inc(mT_ready, 1)
            assert ch.n == per

        maxima(0, 0, None)
        with v.Fori(0, 2) as it:
            for u in range(3):
                maxima(it * 3 + (u + 1), (u + 1) % 3, it + 1)
        maxima(7, 1, 3)
        ch.base, ch.n = first + 8 * per, 0
        for b in range(B):
            r = NT + b
            v.wait_ge(fin_xt, b + 1)
            hv = bank[6 + b].rearrange("p (h d) -> p h d", d=32)
            ch(nc.vector.reciprocal(rden[0:REG, r, :], hv[0:REG, :, D]))
            ch(nc.vector.tensor_tensor(ox[:, b, :].rearrange("p (h d) -> p h d", d=D), hv[0:REG, :, 0:D],
                                       rden[0:REG, r, :].unsqueeze(2).broadcast_to([REG, H, D]), ALU.mult))
        for t in range(NT):
            v.wait_ge(fin_t, t + 1)
            hv = bank[t % 2].rearrange("p (h d) -> p h d", d=32)
            ch(nc.vector.reciprocal(rden[:, t, :], hv[:, :, D]))
            last = nc.vector.tensor_tensor(o_tm[:, t, :].rearrange("p (h d) -> p h d", d=D), hv[:, :, 0:D],
                                           rden[:, t, :].unsqueeze(2).broadcast_to([P, H, D]), ALU.mult)
            if t % TPB == 0:
                ch(last)
                ch(nc.vector.tensor_tensor(o_tm[0:REG, t, :], o_tm[0:REG, t, :], ox[:, t // TPB, :], ALU.add))
                last = nc.vector.tensor_scalar(o_tm[0:REG, t, :], o_tm[0:REG, t, :], 0.5, None, ALU.mult)
            last.then_inc(fin_o, 1)
            if t >= 2:
                add(v, t - 2)
        add(v, NT - 2)
        add(v, NT - 1)

    def add(v, t):
        v.wait_ge(fin_p, t + 1)
        nc.vector.scalar_tensor_tensor(x[:, t, :], bank[4 + t % 2][:, 0:C], 0.5, xb[:, t, :], ALU.mult, ALU.add)\
            .then_inc(x_done, 1)

    def pe(t_):
        wqkv, wproj = env.w["qkv"], env.w["proj"]
        ln.pe(t_)
        for j in range(8):
            c, is_k = j // 2, j % 2
            t_.wait_ge(ln.ready, c + 1)
            if j >= 4:
                t_.wait_ge(proj_out, j - 3)
            nc.tensor.matmul(bank[j % 4], wqkv[:, is_k * C:(is_k + 1) * C], xn[:, c * BANK:(c + 1) * BANK],
                             start=True, stop=True).then_inc(proj_mm, 1)
        for j in range(8, 16):
            t_.wait_ge(proj_out, j - 3)
            for t in range(2):
                tile = 2 * (j - 8) + t
                for which in (0, 2):
                    at = t * 2 * C + (which // 2) * C
                    last = nc.tensor.matmul(bank[j % 4][:, at:at + C], xn[:, tile * P:(tile + 1) * P],
                                            wqkv[:, which * C:(which + 1) * C], start=True, stop=True)
            last.then_inc(proj_mm, 1)
        t_.wait_ge(masks_ready, 1)
        t_.wait_ge(proj_out, 16)
        nc.tensor.transpose(bank[0][0:4 * NT, 0:P], masks[:, :, :].rearrange("p k t -> p (k t)"), env.ident[:])\
            .then_inc(masks_t, 1)
        t_.wait_ge(mrow_ready, 1)
        t_.sem_inc(prob_free, 2)

        def scores(q, slot, k):
            col, half = k // 2, k % 2
            t_.wait_ge(score_free, q * HALVES + k + 1)
            if col == MC - 1:
                t_.sem_inc(passed, 1)
                for h in range(4):
                    last = nc.tensor.matmul(score[k % 2][XQ * h:XQ * h + XQ, :], QX[slot][:, h, T:QW],
                                            KX[slot][:, h // 2, half * BANK:(half + 1) * BANK], start=True, stop=True)
            else:
                head, tile = col // TPB, col % TPB
                last = nc.tensor.matmul(score[k % 2], QX[slot][:, head, tile * P:(tile + 1) * P],
                                        KX[slot][:, head // 2, half * BANK:(half + 1) * BANK], start=True, stop=True)
            last.then_inc(score_ready, 1)

        def turn(q):
            t_.wait_ge(msplit_ready, q + 1)
            nc.tensor.transpose(score[0][:, 0:P // 2].bitcast(BF16)[0:3 * MC, :],
                                msplit[:, :, :].rearrange("p j c -> p (j c)"), env.ident_b[:]).then_inc(m_t, 1)

        def pair(q, slot, i):
            c, kt = i // KT, i % KT
            for p in range(2):
                t_.wait_ge(exp_done, q * 2 * STEPS + 2 * i + p + 1)
                for e in range(2):
                    last = nc.tensor.matmul(bank[2 * p + e][:, 0:QC], KX[slot][:, p, kt * P:(kt + 1) * P],
                                            QX[slot][:, 2 * p + e, c * QC:(c + 1) * QC], start=True, stop=True)
                last.then_inc(st_ready, 1)

        def sums(q, slot, i):
            c, kt = i // KT, i % KT
            if kt == 0 and c != 1:
                t_.wait_ge(sums_out, q * 3 + (1 if c == 0 else 2))
            t_.wait_ge(exp_done, q * 2 * STEPS + 2 * i + 4)
            for h in range(4):
                n = 2 * i + h // 2
                last = nc.tensor.matmul(acc_of(c)[32 * h:32 * h + 32, 0:QC], VX[slot][:, kt, h, :],
                                        prob[n % PR][:, h % 2, :], start=(kt == 0), stop=(kt == KT - 1))
            last.then_inc(prob_free, 1)

        def quad(q, slot, it, nxt):
            todo = list(range(HALVES)) if nxt else []
            head_start = 14 if nxt else 0
            if nxt:
                nslot = (slot + 1) % SLOTS
                t_.wait_ge(loaded[nslot], 64 * (it + (1 if slot == 2 else 0)) + 64)
                t_.wait_ge(mT_ready, q + 1)
                for _ in range(head_start):
                    scores(q + 1, nslot, todo.pop(0))
            t_.wait_ge(m_loaded[slot], 64 * it + 64)
            t_.wait_ge(v_ready, q + 1)
            for i in range(STEPS):
                pair(q, slot, i)
                while todo and len(todo) > (HALVES - head_start) * (STEPS - 1 - i) // STEPS:
                    scores(q + 1, nslot, todo.pop(0))
                if i:
                    sums(q, slot, i - 1)
            sums(q, slot, STEPS - 1)
            if nxt:
                turn(q + 1)

        t_.wait_ge(loaded[0], 64)
        for k in range(HALVES):
            scores(0, 0, k)
        turn(0)
        with t_.Fori(0, 2) as it:
            for u in range(3):
                quad(it * 3 + u, u, it, True)
        quad(6, 0, 2, True)
        quad(7, 1, 2, False)
        for slot in range(SLOTS):
            t_.wait_ge(a_free[slot], 16 * (4 if slot < 2 else 3))
        t_.wait_ge(sums_out, 3 * NQUAD + 1)
        for b in range(B):
            for qd in range(4):
                last = nc.tensor.transpose(bank[6 + b][0:REG, qd * P:(qd + 1) * P], A[:, 4 * b + qd, T:NQ], env.ident[:])
            last.then_inc(fin_xt, 1)

        def back(t):
            t_.wait_ge(fin_o, t + 1)
            if t >= 2:
                t_.wait_ge(fin_oc, t - 1)
            nc.tensor.transpose(bank[2 + t % 2][:, 0:P], o_tm[:, t, :], env.ident[:]).then_inc(fin_b, 1)

        def project(t):
            t_.wait_ge(fin_oc, t + 1)
            if t >= 2:
                t_.wait_ge(x_done, t - 1)
            nc.tensor.matmul(bank[4 + t % 2][:, 0:C], o_cm[:, t, :], wproj[:], start=True, stop=True)\
                .then_inc(fin_p, 1)

        for t in range(NT):
            if t >= 2:
                t_.wait_ge(fin_o, t - 1)
            for qd in range(4):
                b, tt = t // TPB, t % TPB
                last = nc.tensor.transpose(bank[t % 2][:, qd * P:(qd + 1) * P], A[:, 4 * b + qd, tt * P:(tt + 1) * P],
                                           env.ident[:])
            last.then_inc(fin_t, 1)
            if t >= 1:
                back(t - 1)
            if t >= 2:
                project(t - 2)
        back(NT - 1)
        project(NT - 2)
        project(NT - 1)

    return Sublayer(parts=dict(sp=sp, pool=pool, act=act, dve=dve, pe=pe), done=(x_done, NT))


TM, TD = 32, 64
GN_EPS = 1e-5 * 64
MIXES = ("w", "k", "v", "r", "g")


def rwkv_weights(env, weight, loads, ins):
    for n in "rkvgo":
        weight(f"W_{n}", ins[f"L0_attn_W_{n}"], [C, C])
    weight("maa_w1", ins["L0_attn_time_maa_w1"], [C, 5 * TM])
    weight("td_w1", ins["L0_attn_time_decay_w1"], [C, TD])
    weight("td_w2", ins["L0_attn_time_decay_w2"], [TD, C])
    env.w["rows"] = env.sb("w_rows", [10, C], F32)
    names = ["time_maa_" + m for m in MIXES] + ["time_maa_x", "time_decay", "ln_gamma", "ln_beta"]
    for i, n in enumerate(names):
        loads.append((env.w["rows"][i:i + 1, :], ins[f"L0_attn_{n}"].rearrange("(o c) -> o c", o=1)))
    loads.append((env.w["rows"][9:10, :], ins["L0_attn_time_faaaa"].rearrange("(o h) k -> o (h k)", o=1)))


def rwkv(nc, env, tag):
    m0 = env.mark()
    sb, x, w = env.sb, env.x, env.w
    ps = env.ps
    bank = [ps[:, i, :] for i in range(8)]
    w2_dram = env.ins["L0_attn_time_maa_w2"]
    xn = sb(f"{tag}_xn", [P, B, T], F32)
    xx = sb(f"{tag}_xx", [P, B, T], F32)
    mixed = [sb(f"{tag}_mixed{i}", [P, B, T], F32) for i in range(2)]
    low = [sb(f"{tag}_low{i}", [P, B, T], F32) for i in range(2)]
    w2 = sb(f"{tag}_w2", [P, 5, C], F32)
    cols = sb(f"{tag}_cols", [P, 10], F32)
    r_cm = sb(f"{tag}_r", [P, B, T], F32)
    k_cm = sb(f"{tag}_k", [P, B, T], F32)
    g_cm = sb(f"{tag}_g", [P, B, T], F32)
    wd_cm = sb(f"{tag}_wd", [P, B, T], F32)
    xv = sb(f"{tag}_xv", [P, B, T], F32)
    head_sum = sb(f"{tag}_head_sum", [P, H], F32)
    wv_rep = [sb(f"{tag}_wv_rep{i}", [P, C], F32) for i in range(2)]
    bonus = sb(f"{tag}_bonus", [P, NT, H], F32)
    stat = sb(f"{tag}_stat", [P, 4, NT * H], F32)
    mark = env.mark()
    ln = layer_norm(nc, env, f"{tag}_ln", xn[:].rearrange("p b t -> p (b t)"), [bank[4], bank[5]])
    env.rewind(mark)
    kv = sb(f"{tag}_kv", [P, B, T], F32)
    state = [sb(f"{tag}_state{i}", [P, B, T + 1], F32) for i in range(2)]
    read = [sb(f"{tag}_read{i}", [P, B, T], F32) for i in range(2)]
    env.close(m0)
    v_tm, y, yn, yg = low[0], low[1], mixed[0], mixed[1]
    tm = lambda t: t[:].rearrange("p b t -> p (b t)").rearrange("p (n h j) -> p n h j", h=H, j=D)
    flat = lambda t: t[:].rearrange("p b t -> p (b t)")

    s = lambda n: env.sem(f"{tag}_{n}")
    w2_zero, w2_in, cols_t, cols_ready, hs_step, hs_ready = (s(n) for n in ("w2_zero", "w2_in", "cols_t", "cols_ready", "hs_step", "hs_ready"))
    step_sem, xxx_ready, low_mm, low_ready, mix_mm, mix_read, mix_ready = (s(n) for n in ("dve_step", "xxx_ready", "low_mm", "low_ready", "mix_mm", "mix_read", "mix_ready"))
    proj_mm, proj_out, decay_step, td_ready = s("proj_mm"), s("proj_out"), s("decay_step"), s("td_ready")
    rep_w, v_mm, v_read, kv_step, st_ready, read_ready, y_mm = (s(n) for n in ("rep_w", "v_mm", "v_read", "kv_step", "st_ready", "read_ready", "y_mm"))
    ruk_ready, bonus_mm, vtm_mm, vtm_ready, y_out = s("ruk_ready"), s("bonus_mm"), s("vtm_mm"), s("vtm_ready"), s("y_out")
    var_ready, gn_pow, yn_ready, yn_t, yn_cm, gated, out_mm, x_done = (s(n) for n in ("var_ready", "gn_pow", "yn_ready", "yn_t", "yn_cm", "gated", "out_mm", "x_done"))
    FN = len(MIXES)

    def sp(e):
        e.wait_ge(w2_zero, 1)
        for f in range(FN):
            at = f * TM if f < 4 else 3 * TM
            e.dma_start(w2[at:at + TM, f, :], w2_dram[f]).then_inc(w2_in, 16)

    def pool(g):
        nc.gpsimd.memset(w2[:], 0.0).then_inc(w2_zero, 1)
        nc.gpsimd.memset(head_sum[:], 1.0).then_inc(hs_step, 1)
        g.wait_ge(hs_step, 1)
        nc.gpsimd.affine_select(out=head_sum[:], in_=head_sum[:], compare_op=ALU.is_ge, fill=0.0, base=0,
                                pattern=[[-D, H]], channel_multiplier=1).then_inc(hs_step, 1)
        g.wait_ge(hs_step, 2)
        nc.gpsimd.affine_select(out=head_sum[:], in_=head_sum[:], compare_op=ALU.is_ge, fill=0.0, base=D - 1,
                                pattern=[[D, H]], channel_multiplier=-1).then_inc(hs_ready, 1)
        ln.pool(g)
        g.wait_ge(proj_out, 3 * NCH)
        with g.Fori(0, D // 2) as it:
            for u in range(2):
                g.wait_ge(y_mm, it * 2 + (u + 1))
                g.wait_ge(st_ready, it * 2 + (u + 1))
                nc.gpsimd.tensor_tensor(read[u][:], state[u][:, :, 0:T], r_cm[:], ALU.mult).then_inc(read_ready, 1)
        g.wait_ge(var_ready, 1)
        nc.gpsimd.tensor_tensor(stat[:, 2, :], stat[:, 1, :], env.minus_half[:, 0:NT * H], ALU.pow).then_inc(gn_pow, 1)

    def act(a):
        a.wait_ge(cols_t, 1)
        nc.scalar.activation(cols[:], bank[7][:, 0:10], ACT.Copy).then_inc(cols_ready, 1)
        ln.act(a)
        for j in range(2 * NCH):
            i, c = j % 2, j // 2
            a.wait_ge(low_mm, j + 1)
            nc.scalar.activation(flat(low[i])[:, c * BANK:(c + 1) * BANK], bank[i * 2 + c % 2], ACT.Tanh)\
                .then_inc(low_ready, 1)
        a.wait_ge(cols_ready, 1)
        n = 0
        for c in range(NCH):
            a.wait_ge(proj_mm, n + 1)
            nc.scalar.activation(flat(wd_cm)[0:TD, c * BANK:(c + 1) * BANK], bank[4 + n % 2][0:TD, :], ACT.Tanh)\
                .then_inc(td_ready, 1)
            n += 1
        for c in range(NCH):
            a.wait_ge(proj_mm, n + 1)
            nc.scalar.activation(flat(g_cm)[:, c * BANK:(c + 1) * BANK], bank[4 + n % 2], ACT.Exp, bias=cols[:, 6:7])\
                .then_inc(proj_out, 1)
            n += 1
        a.wait_ge(proj_out, NCH)
        nc.scalar.activation(wd_cm[:], g_cm[:], ACT.Exp, scale=-1.0).then_inc(decay_step, 1)
        a.wait_ge(decay_step, 1)
        for dst in (k_cm, r_cm):
            for c in range(NCH):
                a.wait_ge(proj_mm, n + 1)
                nc.scalar.activation(flat(dst)[:, c * BANK:(c + 1) * BANK], bank[4 + n % 2], ACT.Copy).then_inc(proj_out, 1)
                n += 1
        for c in range(NCH):
            a.wait_ge(proj_mm, n + 1)
            nc.scalar.activation(flat(g_cm)[:, c * BANK:(c + 1) * BANK], bank[4 + n % 2], ACT.Silu).then_inc(proj_out, 1)
            n += 1
        for c in range(NCH):
            a.wait_ge(vtm_mm, c + 1)
            nc.scalar.activation(flat(v_tm)[:, c * BANK:(c + 1) * BANK], bank[c], ACT.Copy).then_inc(vtm_ready, 1)
        for c in range(NCH):
            a.wait_ge(yn_t, c + 1)
            nc.scalar.activation(flat(y)[:, c * BANK:(c + 1) * BANK], bank[c], ACT.Identity,
                                 scale=cols[:, 7:8], bias=cols[:, 8:9]).then_inc(yn_cm, 1)

    def dve(v):
        ln.dve(v)
        ch = Chain(v, step_sem)
        v.wait_ge(ln.ready, NCH)
        nc.vector.tensor_tensor(xx[:, :, 1:T], xn[:, :, 0:T - 1], xn[:, :, 1:T], ALU.subtract).then_inc(step_sem, 1)
        nc.vector.tensor_scalar(xx[:, :, 0:1], xn[:, :, 0:1], -1.0, None, ALU.mult).then_inc(step_sem, 1)
        ch.n += 2
        v.wait_ge(step_sem, ch.n)
        v.wait_ge(cols_ready, 1)
        nc.vector.scalar_tensor_tensor(mixed[0][:], xx[:], cols[:, 5:6], xn[:], ALU.mult, ALU.add).then_inc(xxx_ready, 1)
        for i, m in enumerate(ORDER):
            f = MIXES.index(m)
            dst = xv if m == "v" else mixed[(i + 1) % 2]
            if NEEDED[i]:
                v.wait_ge(proj_mm, NEEDED[i])
            if i == 0:
                v.wait_ge(low_mm, 2 * NCH)
            for c in range(NCH):
                sl = slice(c * BANK, (c + 1) * BANK)
                v.wait_ge(mix_mm, i * NCH + c + 1)
                nc.vector.scalar_tensor_tensor(flat(dst)[:, sl], bank[c], cols[:, f:f + 1], flat(xx)[:, sl],
                                               ALU.add, ALU.mult).then_inc(mix_read, 1)
            v.wait_ge(mix_read, (i + 1) * NCH)
            nc.vector.tensor_tensor(dst[:], dst[:], xn[:], ALU.add).then_inc(mix_ready, 1)
        v.wait_ge(proj_out, 3 * NCH)
        ch(nc.vector.tensor_scalar(kv[:], r_cm[:], cols[:, 9:10], None, ALU.mult))
        nc.vector.tensor_tensor(kv[:], kv[:], k_cm[:], ALU.mult).then_inc(ruk_ready, 1)
        v.wait_ge(bonus_mm, 1)
        ch(nc.vector.tensor_copy(bonus[:].rearrange("p t h -> p (t h)"), bank[6][:, 0:NT * H]))
        for i in range(2):
            ch(nc.vector.memset(state[i][:, :, 0:1], 0.0))
        v.sem_inc(v_read, NCH)
        v.sem_inc(y_mm, 2)
        v.sem_inc(read_ready, 2)
        v.wait_ge(decay_step, 1)
        with v.Fori(0, D // 2) as it:
            for u in range(2):
                v.wait_ge(v_mm, it * 8 + (4 * u + 1))
                nc.vector.tensor_scalar(wv_rep[u][:].rearrange("c (h k) -> c h k", k=D),
                                        w["W_v"][:].rearrange("c (h j) -> c h j", j=D)[:, :, bass.ds(it * 2 + u, 1)]
                                        .broadcast_to([P, H, D]), 1.0, None, ALU.mult).then_inc(rep_w, 1)
                for c in range(NCH):
                    sl = slice(c * BANK, (c + 1) * BANK)
                    v.wait_ge(v_mm, it * 8 + (4 * u + c + 5))
                    nc.vector.tensor_tensor(flat(kv)[:, sl], bank[4 + c], flat(k_cm)[:, sl], ALU.mult).then_inc(v_read, 1)
                v.wait_ge(v_read, it * 8 + (4 * u + 8))
                v.wait_ge(read_ready, it * 2 + (u + 1))
                for b in range(B):
                    last = nc.vector.tensor_tensor_scan(state[u][:, b, 1:T + 1], wd_cm[:, b, :], kv[:, b, :], 0.0,
                                                        ALU.mult, ALU.add)
                last.then_inc(st_ready, 1)
        v.wait_ge(y_mm, D + 2)
        yb = ps[:, 0:4, :].rearrange("p k (n j h) -> p (k n) j h", j=D, h=H)
        nc.vector.tensor_copy(tm(y).rearrange("p n h j -> p n j h"), yb).then_inc(y_out, 1)
        v.wait_ge(y_out, 1)
        v.wait_ge(vtm_ready, NCH)
        ch(nc.vector.tensor_tensor(tm(yn), tm(v_tm), bonus[:].unsqueeze(3).broadcast_to([P, NT, H, D]), ALU.mult))
        ch(nc.vector.tensor_tensor(flat(y), flat(y), flat(yn), ALU.add))
        per_head = lambda k: stat[:, k, :].rearrange("p (n h) -> p n h", h=H)
        ch(nc.vector.reduce_sum(per_head(0), tm(y), AX_X))
        ch(nc.vector.tensor_scalar(stat[:, 0, :], stat[:, 0, :], 1.0 / D, None, ALU.mult))
        ch(nc.vector.tensor_tensor(tm(y), tm(y), per_head(0).unsqueeze(3).broadcast_to([P, NT, H, D]), ALU.subtract))
        ch(nc.vector.tensor_tensor(flat(yn), flat(y), flat(y), ALU.mult))
        ch(nc.vector.reduce_sum(per_head(1), tm(yn), AX_X))
        nc.vector.tensor_scalar(stat[:, 1, :], stat[:, 1, :], 1.0 / D, GN_EPS, ALU.mult, ALU.add).then_inc(var_ready, 1)
        v.wait_ge(gn_pow, 1)
        nc.vector.tensor_tensor(tm(yn), tm(y), per_head(2).unsqueeze(3).broadcast_to([P, NT, H, D]), ALU.mult)\
            .then_inc(yn_ready, 1)
        for c in range(NCH):
            sl = slice(c * BANK, (c + 1) * BANK)
            v.wait_ge(yn_cm, c + 1)
            nc.vector.tensor_tensor(flat(yg)[:, sl], flat(y)[:, sl], flat(g_cm)[:, sl], ALU.mult).then_inc(gated, 1)
        for t in range(NT):
            v.wait_ge(out_mm, t + 1)
            nc.vector.tensor_tensor(x[:, t, :], bank[4 + t % 4][:, 0:C], x[:, t, :], ALU.add).then_inc(x_done, 1)

    ORDER = ("w", "k", "r", "g", "v")
    NEEDED = [0, 0, NCH, 3 * NCH, 0]
    PROJ = {"w": "td_w1", "k": "W_k", "r": "W_r", "g": "W_g"}

    def pe(t_):
        nc.tensor.transpose(bank[7][:, 0:10], w["rows"][:], env.ident[0:10, 0:10]).then_inc(cols_t, 1)
        ln.pe(t_)
        t_.wait_ge(xxx_ready, 1)
        for j in range(2 * NCH):
            i, c = j % 2, j // 2
            if c >= 2:
                t_.wait_ge(low_ready, j - 3)
            nc.tensor.matmul(bank[i * 2 + c % 2], w["maa_w1"][:, i * TM:i * TM + 4 * TM],
                             flat(mixed[0])[:, c * BANK:(c + 1) * BANK], start=True, stop=True).then_inc(low_mm, 1)
        t_.wait_ge(w2_in, 16 * FN)
        t_.wait_ge(low_ready, 2 * NCH)
        n = 0

        def mix(i):
            f = MIXES.index(ORDER[i])
            for c in range(NCH):
                if i:
                    t_.wait_ge(mix_read, (i - 1) * NCH + c + 1)
                nc.tensor.matmul(bank[c], w2[:, f, :], flat(low[0 if f < 4 else 1])[:, c * BANK:(c + 1) * BANK],
                                 start=True, stop=True).then_inc(mix_mm, 1)

        def outs(k):
            if k >= NCH:
                t_.wait_ge(td_ready, NCH)
                if k > NCH:
                    t_.wait_ge(proj_out, k - NCH)
            elif k > 0:
                t_.wait_ge(td_ready, k)

        mix(0)
        for i, m in enumerate(ORDER):
            if i + 1 < FN:
                mix(i + 1)
            t_.wait_ge(mix_ready, i + 1)
            if m == "v":
                break
            src = mixed[(i + 1) % 2]
            wt = w[PROJ[m]]
            for c in range(NCH):
                outs(n - 1)
                rows = TD if m == "w" else P
                nc.tensor.matmul(bank[4 + n % 2][0:rows, :], wt[:], flat(src)[:, c * BANK:(c + 1) * BANK],
                                 start=True, stop=True).then_inc(proj_mm, 1)
                n += 1
            if m == "w":
                for c in range(NCH):
                    outs(n - 1)
                    t_.wait_ge(td_ready, c + 1)
                    nc.tensor.matmul(bank[4 + n % 2], w["td_w2"][:], flat(wd_cm)[0:TD, c * BANK:(c + 1) * BANK],
                                     start=True, stop=True).then_inc(proj_mm, 1)
                    n += 1
        t_.wait_ge(hs_ready, 1)
        t_.wait_ge(ruk_ready, 1)
        for t in range(NT):
            last = nc.tensor.matmul(bank[6][:, t * H:(t + 1) * H], flat(kv)[:, t * P:(t + 1) * P], head_sum[:],
                                    start=True, stop=True)
        last.then_inc(bonus_mm, 1)
        t_.wait_ge(proj_out, 4 * NCH)
        t_.wait_ge(mix_read, FN * NCH)
        for t in range(NT):
            last = nc.tensor.matmul(bank[t // 4][:, t % 4 * P:(t % 4 + 1) * P], flat(xv)[:, t * P:(t + 1) * P],
                                    w["W_v"][:], start=True, stop=True)
            if t % 4 == 3:
                last.then_inc(vtm_mm, 1)
        t_.wait_ge(vtm_ready, NCH)
        t_.sem_inc(v_mm, NCH)
        with t_.Fori(0, D // 2) as it:
            for u in range(2):
                t_.wait_ge(rep_w, it * 2 + (u + 1))
                for c in range(NCH):
                    t_.wait_ge(v_read, it * 8 + (4 * u + c + 1))
                    nc.tensor.matmul(bank[4 + c], wv_rep[u][:], flat(xv)[:, c * BANK:(c + 1) * BANK],
                                     start=True, stop=True).then_inc(v_mm, 1)
                t_.wait_ge(read_ready, it * 2 + (u + 3))
                for t in range(NT):
                    at = t % 4 * P
                    last = nc.tensor.matmul(ps[:, t // 4, bass.ds((it * 2 + u) * H + at, H)],
                                            flat(read[u])[:, t * P:(t + 1) * P], head_sum[:], start=True, stop=True)
                last.then_inc(y_mm, 1)
        t_.wait_ge(yn_ready, 1)
        for t in range(NT):
            last = nc.tensor.transpose(bank[t // 4][:, t % 4 * P:(t % 4 + 1) * P], flat(yn)[:, t * P:(t + 1) * P],
                                       env.ident[:])
            if t % 4 == 3:
                last.then_inc(yn_t, 1)
        for t in range(NT):
            t_.wait_ge(gated, t // 4 + 1)
            if t >= 4:
                t_.wait_ge(x_done, t - 3)
            nc.tensor.matmul(bank[4 + t % 4][:, 0:C], flat(yg)[:, t * P:(t + 1) * P], w["W_o"][:],
                             start=True, stop=True).then_inc(out_mm, 1)

    return Sublayer(parts=dict(sp=sp, pool=pool, act=act, dve=dve, pe=pe), done=(x_done, NT))


NE, FF = 8, 512
FB = FF // P


def moe_weights(env, weight, loads, ins):
    if "router" in env.w:
        return
    weight("router", ins["L1_ffn_router_w"], [C, NE])
    weight("router_b", ins["L1_ffn_router_b"].rearrange("(o e) -> o e", o=1).broadcast_to([P, NE]), [P, NE])
    weight("b1_rows", ins["L1_ffn_b1"].rearrange("e (f p) -> (e f) p", p=P), [NE * FB, P])
    weight("b2", ins["L1_ffn_b2"], [NE, C])


def moe(nc, env, tag):
    m0 = env.mark()
    sb, x = env.sb, env.x
    ps = env.ps
    bank = [ps[:, i, :] for i in range(8)]
    w1, w2 = env.ins["L1_ffn_w1"], env.ins["L1_ffn_w2"]
    xn = sb(f"{tag}_xn", [P, TOK], F32)
    W1 = [sb(f"{tag}_W1_{i}", [P, FF], F32) for i in range(2)]
    W2 = [sb(f"{tag}_W2_{i}", [P, FB, C], F32) for i in range(2)]
    b1_all = sb(f"{tag}_b1_all", [P, NE, FB], F32)
    b1 = [sb(f"{tag}_b1_{i}", [P, FB], F32) for i in range(2)]
    hid = [sb(f"{tag}_hid{i}", [P, FB, BANK], F32) for i in range(2)]
    logits = sb(f"{tag}_logits", [P, NT, NE], F32)
    top = sb(f"{tag}_top", [P, NT, 8], F32)
    idx = sb(f"{tag}_idx", [P, NT, 8], U32)
    idxf = sb(f"{tag}_idxf", [P, NT, 8], F32)
    expert_no = sb(f"{tag}_expert_no", [P, NE], F32)
    gap = sb(f"{tag}_gap", [P, NT], F32)
    ratio = sb(f"{tag}_ratio", [P, NT], F32)
    g1 = sb(f"{tag}_g1", [P, NT], F32)
    g2 = sb(f"{tag}_g2", [P, NT], F32)
    hit = sb(f"{tag}_hit", [P, 2, NT, NE], F32)
    gate = sb(f"{tag}_gate", [P, NT, NE], F32)
    gate_e = sb(f"{tag}_gate_e", [P, NE, NT], F32)
    gate_t = sb(f"{tag}_gate_t", [NE, NT, P], F32)
    ln = layer_norm(nc, env, f"{tag}_ln", xn, [bank[4], bank[5]])
    env.close(m0)

    s = lambda n: env.sem(f"{tag}_{n}")
    loaded = [s("loaded0"), s("loaded1")]
    logits_mm, b1_t, b1_all_ready, gap_ready, ratio_ready = (s(n) for n in ("logits_mm", "b1_t", "b1_all_ready", "gap_ready", "ratio_ready"))
    gates_ready, gates_t, gate_t_ready, b2_mm = (s(n) for n in ("gates_ready", "gates_t", "gate_t_ready", "b2_mm"))
    iota_ready, step_sem, b1_ready = s("iota_ready"), s("dve_step"), s("b1_ready")
    up_ready, gelu_done, out_ready, added = s("up_ready"), s("gelu_done"), s("out_ready"), s("added")

    def sp(e):
        def load(i, slot):
            e.dma_start(W1[slot][:], w1[bass.ds(i, 1)].rearrange("o c f -> (o c) f")).then_inc(loaded[slot], 16)
            e.dma_start(W2[slot][:], w2[bass.ds(i, 1)].rearrange("o (f p) c -> p (o f) c", p=P))\
                .then_inc(loaded[slot], 16)
        load(0, 0)
        load(1, 1)
        with e.Fori(0, NE // 2 - 1) as it:
            for u in range(2):
                e.wait_ge(out_ready, (it * 2 + u) * NCH + (NCH + 2))
                load(it * 2 + (u + 2), u)

    def pool(g):
        nc.gpsimd.iota(expert_no[:], pattern=[[1, NE]], base=0, channel_multiplier=0,
                       allow_small_or_imprecise_dtypes=True).then_inc(iota_ready, 1)
        ln.pool(g)

    def act(a):
        ln.act(a)
        a.wait_ge(b1_t, 1)
        nc.scalar.activation(b1_all[:].rearrange("p e f -> p (e f)"), bank[7][:, 0:NE * FB], ACT.Copy)\
            .then_inc(b1_all_ready, 1)
        a.wait_ge(gap_ready, 1)
        nc.scalar.activation(ratio[:], gap[:], ACT.Exp).then_inc(ratio_ready, 1)
        for k in range(NCH):
            a.wait_ge(gates_t, k + 1)
            nc.scalar.activation(gate_t[:, 4 * k:4 * k + 4, :].rearrange("e t p -> e (t p)"), bank[k][0:NE, :], ACT.Copy)\
                .then_inc(gate_t_ready, 1)
        a.sem_inc(gelu_done, FB)
        with a.Fori(0, NE // 2) as it:
            for u in range(2):
                a.wait_ge(b1_ready, it * 2 + (u + 1))
                for c in range(NCH):
                    n = it * (2 * NCH) + (u * NCH + c)
                    a.wait_ge(out_ready, n + 1)
                    for f in range(FB):
                        a.wait_ge(up_ready, n * FB + (f + 1))
                        nc.scalar.activation(hid[c % 2][:, f, :], bank[f], ACT.Gelu, bias=b1[u][:, f:f + 1])\
                            .then_inc(gelu_done, 1)

    def dve(v):
        ln.dve(v)
        ch = Chain(v, step_sem)
        v.wait_ge(logits_mm, 1)
        ch(nc.vector.tensor_tensor(logits[:], bank[6][:, 0:NT * NE].rearrange("p (t e) -> p t e", e=NE),
                                   env.w["router_b"].unsqueeze(1).broadcast_to([P, NT, NE]), ALU.add))
        for t in range(NT):
            nc.vector.max(top[:, t, :], logits[:, t, :]).then_inc(step_sem, 1)
            ch.n += 1
        for t in range(NT):
            v.wait_ge(step_sem, ch.n - NT + 1 + t)
            nc.vector.max_index(idx[:, t, :], top[:, t, :], logits[:, t, :]).then_inc(step_sem, 1)
        ch.n += NT
        v.wait_ge(step_sem, ch.n)
        nc.vector.tensor_tensor(gap[:], top[:, :, 1], top[:, :, 0], ALU.subtract).then_inc(gap_ready, 1)
        ch(nc.vector.tensor_copy(idxf[:], idx[:]))
        v.wait_ge(iota_ready, 1)
        for k in range(2):
            ch(nc.vector.tensor_tensor(hit[:, k], expert_no[:].unsqueeze(1).broadcast_to([P, NT, NE]),
                                       idxf[:, :, k:k + 1].broadcast_to([P, NT, NE]), ALU.is_equal))
        v.wait_ge(ratio_ready, 1)
        ch(nc.vector.tensor_scalar(g1[:], ratio[:], 1.0, None, ALU.add))
        ch(nc.vector.reciprocal(g1[:], g1[:]))
        ch(nc.vector.tensor_scalar(g1[:], g1[:], 0.5, None, ALU.mult))
        ch(nc.vector.tensor_tensor(g2[:], ratio[:], g1[:], ALU.mult))
        ch(nc.vector.tensor_tensor(hit[:, 0], hit[:, 0], g1[:].unsqueeze(2).broadcast_to([P, NT, NE]), ALU.mult))
        ch(nc.vector.tensor_tensor(hit[:, 1], hit[:, 1], g2[:].unsqueeze(2).broadcast_to([P, NT, NE]), ALU.mult))
        nc.vector.tensor_tensor(gate[:], hit[:, 0], hit[:, 1], ALU.add).then_inc(gates_ready, 1)
        v.wait_ge(gates_ready, 1)
        ch(nc.vector.tensor_copy(gate_e[:].rearrange("p e t -> p t e"), gate[:]))
        v.wait_ge(b1_all_ready, 1)
        for t in range(NT):
            if t % 4 == 0:
                v.wait_ge(b2_mm, t // 4 + 1)
            nc.vector.tensor_tensor(x[:, t, :], bank[4 + t // 4 % 2][:, (t % 4) * P:(t % 4 + 1) * P], x[:, t, :], ALU.add)\
                .then_inc(added, 1)
        with v.Fori(0, NE // 2) as it:
            for u in range(2):
                i = it * 2 + u
                v.wait_ge(gelu_done, (it * 2 + u) * (NCH * FB) + 1)
                nc.vector.tensor_scalar(b1[u][:], b1_all[:, bass.ds(i, 1), :].rearrange("p o f -> p (o f)"), 1.0, None,
                                        ALU.mult).then_inc(b1_ready, 1)
                for c in range(NCH):
                    n = it * (2 * NCH) + (u * NCH + c)
                    v.wait_ge(out_ready, n + 3)
                    for j in range(4):
                        t = 4 * c + j
                        v.wait_ge(added, n * 4 + (j + 1))
                        nc.vector.scalar_tensor_tensor(
                            x[:, t, :], bank[4 + c % 2][:, j * P:(j + 1) * P],
                            gate_e[:, bass.ds(i, 1), t], x[:, t, :], ALU.mult, ALU.add).then_inc(added, 1)

    def pe(t_):
        t_.sem_inc(out_ready, 2)
        nc.tensor.transpose(bank[7][:, 0:NE * FB], env.w["b1_rows"][:], env.ident[0:NE * FB, 0:NE * FB]).then_inc(b1_t, 1)
        ln.pe(t_)
        for t in range(NT):
            if t % 4 == 0:
                t_.wait_ge(ln.ready, t // 4 + 1)
            last = nc.tensor.matmul(bank[6][:, t * NE:(t + 1) * NE], xn[:, t * P:(t + 1) * P], env.w["router"][:],
                                    start=True, stop=True)
        last.then_inc(logits_mm, 1)
        t_.wait_ge(gates_ready, 1)
        for k in range(NCH):
            for j in range(4):
                last = nc.tensor.transpose(bank[k][0:NE, j * P:(j + 1) * P], gate[:, 4 * k + j, :], env.ident[:])
            last.then_inc(gates_t, 1)
        for k in range(NCH):
            t_.wait_ge(gate_t_ready, k + 1)
            if k >= 2:
                t_.wait_ge(added, 4 * (k - 1))
            for j in range(4):
                last = nc.tensor.matmul(bank[4 + k % 2][:, j * P:(j + 1) * P], gate_t[:, 4 * k + j, :], env.w["b2"][:],
                                        start=True, stop=True)
            last.then_inc(b2_mm, 1)

        def up(n, u, c):
            for f in range(FB):
                t_.wait_ge(gelu_done, n * FB + (f + 1))
                nc.tensor.matmul(bank[f], W1[u][:, f * P:(f + 1) * P], xn[:, c * BANK:(c + 1) * BANK],
                                 start=True, stop=True).then_inc(up_ready, 1)

        def down(n, u, c):
            t_.wait_ge(gelu_done, n * FB + 2 * FB)
            t_.wait_ge(added, n * 4 + (16 - 4))
            for j in range(4):
                for f in range(FB):
                    last = nc.tensor.matmul(bank[4 + c % 2][:, j * P:(j + 1) * P], hid[c % 2][:, f, j * P:(j + 1) * P],
                                            W2[u][:, f, :], start=(f == 0), stop=(f == FB - 1))
            last.then_inc(out_ready, 1)

        with t_.Fori(0, NE // 2) as it:
            for k in range(2 * NCH + 1):
                if k < 2 * NCH:
                    u, c = k // NCH, k % NCH
                    if c == 0:
                        t_.wait_ge(loaded[u], it * 32 + 32)
                    up(it * (2 * NCH) + k, u, c)
                if k:
                    down(it * (2 * NCH) + (k - 1), (k - 1) // NCH, (k - 1) % NCH)

    return Sublayer(parts=dict(sp=sp, pool=pool, act=act, dve=dve, pe=pe), done=(added, NT * (NE + 1)))


HD, NS = 512, 16
DT = HD // P
TWO_PI = 6.283185307179586
TURN_1 = 6.28125
TURN_2 = int((TWO_PI - TURN_1) * 2 ** 21) / 2 ** 21
TURN = (TURN_1, TURN_2, TWO_PI - TURN_1 - TURN_2)
ROUND = 12582912.0


def ssm_weights(env, weight, loads, ins):
    if "w_in" in env.w:
        return
    weight("w_in", ins["L1_attn_input_proj"], [C, HD])
    weight("w_out", ins["L1_attn_output_proj"].rearrange("(t p) e -> p t e", p=P), [P, DT, C])
    weight("skip", ins["L1_attn_skip_proj"].rearrange("(t p) e -> p t e", p=P), [P, DT, HD])
    env.w["bc"] = env.sb("w_bc", [P, DT, 2 * NS], F32)
    loads.append((env.w["bc"][:, :, 0:NS], ins["L1_attn_b_proj"].rearrange("(t p) n -> p t n", p=P)))
    loads.append((env.w["bc"][:, :, NS:2 * NS], ins["L1_attn_c_proj"].rearrange("(t p) n -> p t n", p=P)))
    weight("a_log", ins["L1_attn_a_log"].rearrange("(o n) -> o n", o=1).broadcast_to([P, NS]), [P, NS])
    weight("dt_rows", ins["L1_attn_dt_proj"].rearrange("(t p) -> t p", p=P), [DT, P])
    weight("phase_rows", ins["L1_attn_floquet_phases"].rearrange("(t p) -> t p", p=P), [DT, P])


def ssm(nc, env, tag):
    m0 = env.mark()
    sb, x, w = env.sb, env.x, env.w
    ps = env.ps
    bank = [ps[:, i, :] for i in range(8)]
    xn = sb(f"{tag}_xn", [P, TOK], F32)
    X = sb(f"{tag}_X", [P, DT, TOK], F32)
    decay = sb(f"{tag}_decay", [P, NS, DT], F32)
    small = sb(f"{tag}_small", [P, 8, DT], F32)
    rates = sb(f"{tag}_rates", [P, NS], F32)
    bc_part = sb(f"{tag}_bc_part", [6 * NS, TOK], BF16)
    sel = sb(f"{tag}_sel", [6 * NS, 2 * NS, P], BF16)
    Y = sb(f"{tag}_Y", [P, TOK], F32)
    zc = sb(f"{tag}_zc", [P, TOK], F32)
    skip_out = sb(f"{tag}_skip_out", [P, C], F32)
    mark = env.mark()
    Br = [sb(f"{tag}_Br{i}", [P, TOK], F32) for i in range(2)]
    Cr = [sb(f"{tag}_Cr{i}", [P, TOK], F32) for i in range(2)]
    inj = [sb(f"{tag}_inj{i}", [P, TOK], F32) for i in range(2)]
    hst = [sb(f"{tag}_hst{i}", [P, TOK], F32) for i in range(2)]
    env.rewind(mark)
    cosine = sb(f"{tag}_cosine", [P, DT, T], F32)
    turns = sb(f"{tag}_turns", [P, DT, T], F32)
    where = sb(f"{tag}_where", [P, T], F32)
    w_in_t = sb(f"{tag}_w_in_t", [P, DT, C], F32)
    chain_n = sb(f"{tag}_chain_n", [P, HD], F32)
    chain_nt = sb(f"{tag}_chain_nt", [P, DT, C], F32)
    rest = sb(f"{tag}_rest", [2 * NS, TOK], F32)
    mid = sb(f"{tag}_mid", [2 * NS, TOK], BF16)
    ln = layer_norm(nc, env, f"{tag}_ln", xn, [bank[4], bank[5]])
    env.close(m0)

    s = lambda n: env.sem(f"{tag}_{n}")
    step_sem, where_ready, sel_zero, sel_ready = s("dve_step"), s("where_ready"), s("sel_zero"), s("sel_ready")
    cols_t, cols_ready, angle_ready, cos_ready = s("cols_t"), s("cols_ready"), s("angle_ready"), s("cos_ready")
    dt_exp_in, dt_exp, dt_ln, rates_exp, decay_in, decay_ready = (s(n) for n in ("dt_exp_in", "dt_exp", "dt_ln", "rates_exp", "decay_in", "decay_ready"))
    win_t, win_t_ready, skip_mm, skip_ready = s("win_t"), s("win_t_ready"), s("skip_mm"), s("skip_ready")
    hd_mm, x_ready, bc_mm, bc_read, x_scaled = s("hd_mm"), s("x_ready"), s("bc_mm"), s("bc_read"), s("x_scaled")
    hi_ready, parts_ready, mid_ready = s("hi_ready"), s("parts_ready"), s("mid_ready")
    rep_mm, rep_ready, inj_dve, inj_pool, scanned, z_mm, z_read, y_ready = (s(n) for n in ("rep_mm", "rep_ready", "inj_dve", "inj_pool", "scanned", "z_mm", "z_read", "y_ready"))
    out_mm, x_done = s("out_mm"), s("x_done")

    def pool(g):
        nc.gpsimd.iota(where[:], pattern=[[1, T]], base=0, channel_multiplier=0,
                       allow_small_or_imprecise_dtypes=True).then_inc(where_ready, 1)
        nc.gpsimd.memset(sel[:], 0.0).then_inc(sel_zero, 1)
        for j in range(3):
            g.wait_ge(sel_zero, j + 1)
            nc.gpsimd.affine_select(out=sel[:], in_=sel[:], compare_op=ALU.not_equal, fill=1.0, base=-2 * NS * j,
                                    pattern=[[-1, 2 * NS], [0, P]], channel_multiplier=1).then_inc(sel_zero, 1)
        ln.pool(g)
        g.wait_ge(x_scaled, DT)
        g.sem_inc(z_read, 2 * NCH)
        with g.Fori(0, NS // 2) as it:
            for u in range(2):
                g.wait_ge(rep_ready, it * 16 + (8 * u + 8))
                for d in (0, 2, 3):
                    g.wait_ge(scanned, it * 16 + (8 * u + 2 * d + 2))
                    nc.gpsimd.tensor_tensor(inj[d % 2][:], X[:, d, :], Br[u][:], ALU.mult).then_inc(inj_pool, 1)

    def act(a):
        a.wait_ge(cols_t, 1)
        nc.scalar.activation(small[:, 0:2, :], bank[7][:, 0:2 * DT].rearrange("p (k t) -> p k t", k=2), ACT.Copy)\
            .then_inc(cols_ready, 1)
        nc.scalar.activation(rates[:], w["a_log"][:], ACT.Exp).then_inc(rates_exp, 1)
        a.wait_ge(dt_exp_in, 1)
        nc.scalar.activation(small[:, 3, :], small[:, 2, :], ACT.Exp, scale=-1.0).then_inc(dt_exp, 1)
        a.wait_ge(dt_exp, 1)
        nc.scalar.activation(small[:, 4, :], small[:, 3, :], ACT.Ln, bias=1.0).then_inc(dt_ln, 1)
        a.wait_ge(decay_in, 1)
        nc.scalar.activation(decay[:], decay[:], ACT.Exp, scale=-1.0).then_inc(decay_ready, 1)
        a.wait_ge(win_t, 1)
        nc.scalar.activation(w_in_t[:].rearrange("p t c -> p (t c)"), bank[0], ACT.Copy).then_inc(win_t_ready, 1)
        a.wait_ge(skip_mm, 1)
        nc.scalar.activation(chain_n[:], bank[1], ACT.Copy).then_inc(skip_ready, 1)
        a.wait_ge(skip_mm, 2)
        nc.scalar.activation(chain_nt[:].rearrange("p t c -> p (t c)"), bank[2], ACT.Copy).then_inc(skip_ready, 1)
        a.wait_ge(skip_mm, 3)
        nc.scalar.activation(skip_out[:], bank[3][:, 0:C], ACT.Copy).then_inc(skip_ready, 1)
        ln.act(a)
        a.wait_ge(angle_ready, 1)
        nc.scalar.activation(cosine[:], cosine[:], ACT.Sin).then_inc(cos_ready, 1)
        for k in range(NCH):
            cols = slice(k * BANK, (k + 1) * BANK)
            a.wait_ge(mid_ready, k + 1)
            nc.scalar.activation(bc_part[2 * NS:4 * NS, cols], mid[:, cols], ACT.Copy).then_inc(parts_ready, 1)
        a.sem_inc(rep_ready, NCH)
        with a.Fori(0, NS // 2) as it:
            for u in range(2):
                for k in range(2 * NCH):
                    dst = (Br if k < NCH else Cr)[u]
                    c = k % NCH
                    if k == 0:
                        a.wait_ge(inj_pool, it * 6 + (3 * u + 3))
                        a.wait_ge(inj_dve, it * 2 + (u + 1))
                    if k == NCH:
                        a.wait_ge(z_read, it * 8 + (4 * u + 4))
                    a.wait_ge(rep_mm, it * 16 + (8 * u + k + 1))
                    nc.scalar.activation(dst[:, c * BANK:(c + 1) * BANK], bank[c], ACT.Copy).then_inc(rep_ready, 1)

    def dve(v):
        ch = Chain(v, step_sem)
        v.wait_ge(cols_ready, 1)
        ch(nc.vector.tensor_scalar(small[:, 2, :], small[:, 0, :], -1.0, None, ALU.mult))
        nc.vector.tensor_tensor(small[:, 2, :], small[:, 2, :], small[:, 0, :], ALU.max).then_inc(dt_exp_in, 1)
        ch(nc.vector.tensor_scalar(small[:, 5, :], small[:, 0, :], 0.0, None, ALU.max))
        v.wait_ge(where_ready, 1)
        for d in range(DT):
            nc.vector.tensor_scalar(cosine[:, d, :], where[:], small[:, 1, d:d + 1], None, ALU.mult).then_inc(step_sem, 1)
            ch.n += 1
        v.wait_ge(step_sem, ch.n)
        ch(nc.vector.tensor_scalar(turns[:], cosine[:], 1.0 / TWO_PI, 0.25, ALU.mult, ALU.add))
        ch(nc.vector.tensor_scalar(turns[:], turns[:], ROUND, ROUND, ALU.add, ALU.subtract))
        for part in TURN:
            ch(nc.vector.scalar_tensor_tensor(cosine[:], turns[:], -part, cosine[:], ALU.mult, ALU.add))
        ch(nc.vector.tensor_scalar(cosine[:], cosine[:], TWO_PI / 4, 3.1415925, ALU.add, ALU.min))
        nc.vector.tensor_scalar(cosine[:], cosine[:], -3.1415925, None, ALU.max).then_inc(angle_ready, 1)
        v.wait_ge(dt_ln, 1)
        ch(nc.vector.tensor_tensor(small[:, 6, :], small[:, 5, :], small[:, 4, :], ALU.add))
        v.wait_ge(rates_exp, 1)
        nc.vector.tensor_tensor(decay[:], small[:, 6, :].unsqueeze(1).broadcast_to([P, NS, DT]),
                                rates[:].unsqueeze(2).broadcast_to([P, NS, DT]), ALU.mult).then_inc(decay_in, 1)
        ln.dve(v)
        v.wait_ge(cos_ready, 1)
        for k in range(NCH):
            half = k % 2
            for d in range(DT):
                n = k * DT + d
                v.wait_ge(hd_mm, n + 1)
                nc.vector.tensor_tensor(X[:, d, k * BANK:(k + 1) * BANK], bank[n % 4],
                                        cosine[:, d, half * BANK:(half + 1) * BANK], ALU.mult).then_inc(x_ready, 1)
        for k in range(NCH):
            cols = slice(k * BANK, (k + 1) * BANK)
            v.wait_ge(bc_mm, k + 1)
            rows = bank[4 + k % 2][0:2 * NS, :]
            nc.vector.tensor_copy(bc_part[0:2 * NS, cols], rows).then_inc(hi_ready, 1)
            v.wait_ge(hi_ready, k + 1)
            nc.vector.tensor_tensor(rest[:, cols], rows, bc_part[0:2 * NS, cols], ALU.subtract).then_inc(bc_read, 1)
            v.wait_ge(bc_read, k + 1)
            nc.vector.tensor_copy(mid[:, cols], rest[:, cols]).then_inc(mid_ready, 1)
            v.wait_ge(mid_ready, k + 1)
            nc.vector.tensor_tensor(bc_part[4 * NS:6 * NS, cols], rest[:, cols], mid[:, cols], ALU.subtract)\
                .then_inc(parts_ready, 1)
        for d in range(DT):
            v.wait_ge(bc_mm, NCH)
            nc.vector.tensor_scalar(X[:, d, :], X[:, d, :], small[:, 6, d:d + 1], None, ALU.mult).then_inc(x_scaled, 1)
        nc.vector.memset(Y[:], 0.0).then_inc(y_ready, 1)
        v.sem_inc(inj_pool, 6)
        v.sem_inc(inj_dve, 2)
        v.sem_inc(scanned, 4)
        v.wait_ge(decay_ready, 1)
        v.wait_ge(x_scaled, DT)
        with v.Fori(0, NS // 2) as it:
            for u in range(2):
                for d in range(DT):
                    if d == 1:
                        v.wait_ge(rep_ready, it * 16 + (8 * u + 8))
                        v.wait_ge(scanned, it * 16 + (8 * u + 4))
                        nc.vector.tensor_tensor(inj[1][:], X[:, 1, :], Br[u][:], ALU.mult).then_inc(inj_dve, 1)
                        v.wait_ge(inj_dve, it * 2 + (u + 3))
                    else:
                        v.wait_ge(inj_pool, it * 6 + (3 * u + 6 + (1, 0, 2, 3)[d]))
                    v.wait_ge(z_mm, it * 32 + (16 * u + 4 * d + 4))
                    for b in range(B):
                        cols = slice(b * T, (b + 1) * T)
                        nc.vector.tensor_tensor_scan(hst[d % 2][:, cols],
                                                     decay[:, bass.ds(it * 2 + u, 1), d].broadcast_to([P, T]),
                                                     inj[d % 2][:, cols], 0.0, ALU.mult, ALU.add).then_inc(scanned, 1)
                for c in range(NCH):
                    cols = slice(c * BANK, (c + 1) * BANK)
                    if c == 0:
                        v.wait_ge(rep_ready, it * 16 + (8 * u + 12))
                    v.wait_ge(z_mm, it * 32 + (16 * u + 21 + c))
                    nc.vector.tensor_tensor(zc[:, cols], bank[4 + c], Cr[u][:, cols], ALU.mult).then_inc(z_read, 1)
                v.wait_ge(z_read, it * 8 + (4 * u + 12))
                v.wait_ge(y_ready, it * 2 + (u + 1))
                nc.vector.tensor_tensor(Y[:], Y[:], zc[:], ALU.add).then_inc(y_ready, 1)
        for t in range(NT):
            v.wait_ge(out_mm, t + 1)
            nc.vector.tensor_tensor(x[:, t, :], bank[t % 4][:, 0:C], x[:, t, :], ALU.add).then_inc(x_done, 1)

    def pe(t_):
        nc.tensor.transpose(bank[7][:, 0:DT], w["dt_rows"][:], env.ident[0:DT, 0:DT])
        nc.tensor.transpose(bank[7][:, DT:2 * DT], w["phase_rows"][:], env.ident[0:DT, 0:DT]).then_inc(cols_t, 1)
        for d in range(DT):
            last = nc.tensor.transpose(bank[0][:, d * P:(d + 1) * P], w["w_in"][:, d * P:(d + 1) * P], env.ident[:])
        last.then_inc(win_t, 1)
        t_.wait_ge(win_t_ready, 1)
        for d in range(DT):
            last = nc.tensor.matmul(bank[1], w_in_t[:, d, :], w["skip"][:, d, :], start=(d == 0), stop=(d == DT - 1))
        last.then_inc(skip_mm, 1)
        t_.wait_ge(skip_ready, 1)
        for d in range(DT):
            last = nc.tensor.transpose(bank[2][:, d * P:(d + 1) * P], chain_n[:, d * P:(d + 1) * P], env.ident[:])
        last.then_inc(skip_mm, 1)
        t_.wait_ge(skip_ready, 2)
        for d in range(DT):
            last = nc.tensor.matmul(bank[3][:, 0:C], chain_nt[:, d, :], w["w_out"][:, d, :],
                                    start=(d == 0), stop=(d == DT - 1))
        last.then_inc(skip_mm, 1)
        ln.pe(t_)
        t_.wait_ge(skip_ready, 3)
        for k in range(NCH):
            t_.wait_ge(ln.ready, k + 1)
            for d in range(DT):
                n = k * DT + d
                if n >= 4:
                    t_.wait_ge(x_ready, n - 3)
                nc.tensor.matmul(bank[n % 4], w["w_in"][:, d * P:(d + 1) * P], xn[:, k * BANK:(k + 1) * BANK],
                                 start=True, stop=True).then_inc(hd_mm, 1)
        for k in range(NCH):
            t_.wait_ge(x_ready, (k + 1) * DT)
            if k >= 2:
                t_.wait_ge(bc_read, k - 1)
            for d in range(DT):
                last = nc.tensor.matmul(bank[4 + k % 2][0:2 * NS, :], w["bc"][:, d, :], X[:, d, k * BANK:(k + 1) * BANK],
                                        start=(d == 0), stop=(d == DT - 1))
            last.then_inc(bc_mm, 1)
        t_.wait_ge(sel_zero, 4)
        t_.wait_ge(parts_ready, 2 * NCH)
        t_.sem_inc(z_mm, 2 * NCH)

        def spread(it, u, k):
            c = k % NCH
            row = it * 2 + u + (NS if k >= NCH else 0)
            nc.tensor.matmul(bank[c], sel[:, bass.ds(row, 1), :].rearrange("r o p -> r (o p)"),
                             bc_part[:, c * BANK:(c + 1) * BANK], start=True, stop=True).then_inc(rep_mm, 1)

        with t_.Fori(0, NS // 2) as it:
            for u in range(2):
                for k in range(2 * NCH):
                    t_.wait_ge(rep_ready, it * 16 + (8 * u + k + 1))
                    spread(it, u, k)
                for d in range(DT):
                    for c in range(NCH):
                        if c % 2 == 0:
                            t_.wait_ge(scanned, it * 16 + (8 * u + 2 * d + c // 2 + 5))
                        if d == 0:
                            t_.wait_ge(z_read, it * 8 + (4 * u + c + 5))
                        nc.tensor.matmul(bank[4 + c], w["w_out"][:, d, :], hst[d % 2][:, c * BANK:(c + 1) * BANK],
                                         start=(d == 0), stop=(d == DT - 1)).then_inc(z_mm, 1)
        t_.wait_ge(y_ready, NS + 1)
        for t in range(NT):
            if t >= 4:
                t_.wait_ge(x_done, t - 3)
            nc.tensor.matmul(bank[t % 4][:, 0:C], Y[:, t * P:(t + 1) * P], env.ident[:], start=True, stop=False)
            nc.tensor.matmul(bank[t % 4][:, 0:C], xn[:, t * P:(t + 1) * P], skip_out[:], start=False, stop=True)\
                .then_inc(out_mm, 1)

    return Sublayer(parts=dict(pool=pool, act=act, dve=dve, pe=pe), done=(x_done, NT))


STAGES = ("attn", "rwkv", "attn", "moe", "ssm", "moe",)
EXTRA_WEIGHTS = {"rwkv": rwkv_weights, "moe": moe_weights, "ssm": ssm_weights}


def build(nc, out, **ins):
    ctx = ExitStack()
    with ctx:
        drams = {}

        def sem(name):
            one = nc.alloc_semaphore(f"{name}_{len(used)}")
            used[-1].append(one)
            return one

        def dram(name, shape, dt):
            if name not in drams:
                drams[name] = nc.dram_tensor(name, shape, dt).ap()
            return drams[name]

        used = [[]]
        LIMIT = nc.sbuf_usable_end if not callable(nc.sbuf_usable_end) else nc.sbuf_usable_end()
        top = [nc.sbuf_base if not callable(nc.sbuf_base) else nc.sbuf_base()]
        top[0] = (top[0] + 31) // 32 * 32
        size = {F32: 4, BF16: 2, U32: 4}

        def sb(name, shape, dt):
            n = size[dt]
            for k in shape[1:]:
                n *= k
            at = top[0]
            top[0] = at + (n + 31) // 32 * 32
            env.peak = max(env.peak, top[0])
            assert top[0] <= LIMIT, (name, top[0], LIMIT)
            return nc.alloc_sbuf_tensor_at(f"{name}_{len(used)}", shape, dt, offset=at).ap()

        def rewind(m):
            top[0] = m

        def mark():
            return top[0]

        env = Env()
        env.sb, env.sem, env.dram, env.mark, env.rewind, env.peak = sb, sem, dram, mark, rewind, 0
        env.open = env.mark
        env.close = rewind
        env.ps = ctx.enter_context(nc.psum_tensor("ps", [P, 8, BANK], F32))
        env.rmax = bass.bass_isa.ReduceOp.max
        x = env.x = sb("x", [P, NT, C], F32)
        env.ident = sb("ident", [P, P], F32)
        env.ident_b = sb("ident_b", [P, P], BF16)
        env.minus_half = sb("minus_half", [P, NT * H], F32)
        env.is_reg = sb("is_reg", [P, NT], F32)
        env.half_bproj = sb("half_bproj", [P, C], F32)
        env.qg_unit = sb("qg_unit", [P, C], F32)
        qg_sq = sb("qg_sq", [P, C], F32)
        qg_n2 = sb("qg_n2", [P, 2, H], F32)
        x_in, w_in, const_step, qg_ready, qg_pow = (sem(n) for n in ("x_in", "w_in", "const_step", "qg_ready", "qg_pow"))
        setup_step, out_done = sem("setup_step"), sem("out_done")
        env.w = {}
        loads = []

        def weight(name, src, shape):
            env.w[name] = sb(f"w_{name}", shape, F32)
            loads.append((env.w[name], src))

        weight("qkv", ins["L0_ffn_W_qkv"], [C, 3 * C])
        weight("proj", ins["L0_ffn_W_proj"], [C, C])
        loads.append((env.half_bproj, ins["L0_ffn_b_proj"].rearrange("(o c) -> o c", o=1).broadcast_to([P, C])))
        loads.append((env.qg_unit, ins["L0_ffn_g_info"][0, 0:1, :].broadcast_to([P, C])))
        for name in STAGES:
            if name in EXTRA_WEIGHTS and f"{name}_held" not in env.w:
                env.w[f"{name}_held"] = True
                EXTRA_WEIGHTS[name](env, weight, loads, ins)
        makers = {"attn": attention, "rwkv": rwkv, "moe": moe, "ssm": ssm}
        env.ins = ins
        ends = [sem(f"end{k}") for k in range(len(STAGES) - 1)]
        stages = []
        for k, name in enumerate(STAGES):
            if k >= 2:
                for one in used[k - 1]:
                    nc.release_semaphore(one)
            used.append([])
            stages.append(makers[name](nc, env, name))

        def run(e, part):
            for k, st in enumerate(stages):
                if part in st.parts:
                    st.parts[part](e)
                if k + 1 < len(stages):
                    e.drain().then_inc(ends[k], 1)
                    e.wait_ge(ends[k], 5)
                    if part == "sp" and k + 2 < len(stages):
                        for one in used[k + 1]:
                            e.sem_clear(one)

        block = ctx.enter_context(nc.Block())

        @block.sync
        def _(sp):
            sp.dma_start(x[:], ins["L0_attn_x"].rearrange("b (t p) c -> p (b t) c", p=P)).then_inc(x_in, 16)
            for dst, src in loads:
                sp.dma_start(dst, src).then_inc(w_in, 16)
            run(sp, "sp")
            last, n = stages[-1].done
            sp.wait_ge(last, n)
            sp.dma_start(out.rearrange("b (t p) c -> p (b t) c", p=P), x[:]).then_inc(out_done, 16)
            sp.wait_ge(out_done, 16)

        @block.gpsimd
        def _(pool):
            nc.gpsimd.memset(env.minus_half[:], -0.5).then_inc(const_step, 1)
            nc.gpsimd.memset(env.ident[:], 0.0).then_inc(const_step, 1)
            nc.gpsimd.memset(env.ident_b[:], 0.0).then_inc(const_step, 1)
            nc.gpsimd.memset(env.is_reg[:], 0.0).then_inc(const_step, 1)
            pool.wait_ge(const_step, 4)
            for m in (env.ident, env.ident_b):
                nc.gpsimd.affine_select(out=m[:], in_=m[:], compare_op=ALU.not_equal, fill=1.0, base=0,
                                        pattern=[[-1, P]], channel_multiplier=1).then_inc(const_step, 1)
            for b in range(B):
                nc.gpsimd.memset(env.is_reg[0:REG, b * TPB:b * TPB + 1], 1.0).then_inc(const_step, 1)
            pool.wait_ge(qg_ready, 1)
            nc.gpsimd.tensor_tensor(qg_n2[:, 1, :], qg_n2[:, 0, :], env.minus_half[:, 0:H], ALU.pow).then_inc(qg_pow, 1)
            pool.wait_ge(const_step, 8)
            run(pool, "pool")

        @block.scalar
        def _(act):
            act.wait_ge(const_step, 8)
            act.wait_ge(w_in, 16 * len(loads))
            run(act, "act")

        @block.vector
        def _(dve):
            ch = Chain(dve, setup_step)
            dve.wait_ge(const_step, 8)
            dve.wait_ge(w_in, 16 * len(loads))
            ch(nc.vector.tensor_tensor(qg_sq[:], env.qg_unit[:], env.qg_unit[:], ALU.mult))
            nc.vector.reduce_sum(qg_n2[:, 0, :], qg_sq[:].rearrange("p (h d) -> p h d", d=D), AX_X).then_inc(qg_ready, 1)
            ch(nc.vector.tensor_scalar(env.half_bproj[:], env.half_bproj[:], 0.5, None, ALU.mult))
            dve.wait_ge(qg_pow, 1)
            ch(nc.vector.tensor_scalar(qg_n2[:, 1, :], qg_n2[:, 1, :], 1.0 / H, None, ALU.mult))
            ch(nc.vector.tensor_tensor(env.qg_unit[:].rearrange("p (h d) -> p h d", d=D),
                                       env.qg_unit[:].rearrange("p (h d) -> p h d", d=D),
                                       qg_n2[:, 1, :].unsqueeze(2).broadcast_to([P, H, D]), ALU.mult))
            dve.wait_ge(x_in, 16)
            run(dve, "dve")

        @block.tensor
        def _(pe):
            pe.wait_ge(const_step, 8)
            pe.wait_ge(w_in, 16 * len(loads))
            run(pe, "pe")


_OUT_SHAPE = (B, T, C)


def kernel(**inputs):
    import numpy as _np
    import concourse.bacc as _bacc
    from concourse import mybir as _mybir
    from concourse.bass_utils import run_bass_kernel_spmd as _run

    nc = _bacc.Bacc("TRN2", target_bir_lowering=False, num_devices=1)
    arrays, args = {}, {}
    for name, value in inputs.items():
        a = _np.ascontiguousarray(value)
        arrays[name] = a
        args[name] = nc.dram_tensor(name, a.shape, _mybir.dt.from_np(a.dtype), kind="ExternalInput").ap()
    out = nc.dram_tensor("out", _OUT_SHAPE, _mybir.dt.float32, kind="ExternalOutput").ap()
    build(nc, out, **args)
    r = _run(nc, [arrays], core_ids=[0])
    return r.results[0]["out"]
```

```python
import concourse.bass as bass
from concourse import mybir
from contextlib import ExitStack

F32 = mybir.dt.float32
BF16 = mybir.dt.bfloat16
U32 = mybir.dt.uint32
ALU = mybir.AluOpType
ACT = mybir.ActivationFunctionType
AX_X = mybir.AxisListType.X

P = 128
B, T, C = 2, 1024, 128
TOK = B * T
NT = TOK // P
TPB = T // P
H, D = 16, 8
BANK = 512
NCH = TOK // BANK
LN_EPS = 1e-5


class Env:
    pass


class Sublayer:

    def __init__(self, parts, done):
        self.parts, self.done = parts, done


class LayerNorm:

    def __init__(self, dve_stats, dve_apply, pool, pe, act, ready):
        self.dve_stats, self.dve_apply, self.pool, self.pe, self.act, self.ready = \
            dve_stats, dve_apply, pool, pe, act, ready

    def dve(self, v):
        self.dve_stats(v)
        self.dve_apply(v)


class Chain:

    def __init__(self, eng, sem):
        self.eng, self.sem, self.base, self.n = eng, sem, 0, 0

    def __call__(self, ins):
        self.n += 1
        ins.then_inc(self.sem, 1)
        self.eng.wait_ge(self.sem, self.base + self.n)


def inverse_root(nc, ch, out, root, square, scratch):
    ch(nc.vector.reciprocal(out, root))
    ch(nc.vector.tensor_tensor(scratch, out, out, ALU.mult))
    ch(nc.vector.tensor_tensor(scratch, scratch, square, ALU.mult))
    ch(nc.vector.tensor_scalar(scratch, scratch, -0.5, 1.5, ALU.mult, ALU.add))
    ch(nc.vector.tensor_tensor(out, out, scratch, ALU.mult))


def layer_norm(nc, env, tag, xn_cm, banks):
    sb, sem, x, ident = env.sb, env.sem, env.x, env.ident
    stats = sb(f"{tag}_stats", [P, NT, 6], F32)
    mv = sb(f"{tag}_mv", [P, NT, 2], F32)
    var_eps = sb(f"{tag}_var_eps", [P, NT], F32)
    rstd = sb(f"{tag}_rstd", [P, NT], F32)
    xn_tm = sb(f"{tag}_xn_tm", [P, NT, C], F32)
    stat_step = sem(f"{tag}_stat_step")
    var_ready = sem(f"{tag}_var_ready")
    rstd_ready = sem(f"{tag}_rstd_ready")
    xn_tm_ready = sem(f"{tag}_xn_tm_ready")
    transposed = sem(f"{tag}_transposed")
    xn_ready = sem(f"{tag}_xn_ready")

    def dve_stats(v):
        for k in range(NCH):
            for t in range(4 * k, 4 * k + 4):
                nc.vector.bn_stats(stats[:, t, :], x[:, t, :]).then_inc(stat_step, 1)
            for t in range(4 * k, 4 * k + 4):
                v.wait_ge(stat_step, 4 * k + t + 1)
                nc.vector.bn_aggr(mv[:, t, :], stats[:, t, :]).then_inc(stat_step, 1)
            v.wait_ge(stat_step, 8 * k + 8)
            nc.vector.tensor_scalar(var_eps[:, 4 * k:4 * k + 4], mv[:, 4 * k:4 * k + 4, 1], LN_EPS, None, ALU.add)\
                .then_inc(var_ready, 1)

    def dve_apply(v):
        for t in range(NT):
            if t % 4 == 0:
                v.wait_ge(rstd_ready, t // 4 + 1)
            nc.vector.tensor_scalar(xn_tm[:, t, :], x[:, t, :], mv[:, t, 0:1], rstd[:, t:t + 1],
                                    ALU.subtract, ALU.mult).then_inc(xn_tm_ready, 1)

    def pool(g):
        for k in range(NCH):
            g.wait_ge(var_ready, k + 1)
            nc.gpsimd.tensor_tensor(rstd[:, 4 * k:4 * k + 4], var_eps[:, 4 * k:4 * k + 4], env.minus_half[:, 0:4], ALU.pow)\
                .then_inc(rstd_ready, 1)

    def pe(t_):
        for k in range(NCH):
            if k >= 2:
                t_.wait_ge(xn_ready, k - 1)
            for j in range(4):
                t_.wait_ge(xn_tm_ready, 4 * k + j + 1)
                last = nc.tensor.transpose(banks[k % 2][:, j * P:(j + 1) * P], xn_tm[:, 4 * k + j, :], ident[:])
            last.then_inc(transposed, 1)

    def act(s):
        for k in range(NCH):
            s.wait_ge(transposed, k + 1)
            nc.scalar.activation(xn_cm[:, k * BANK:(k + 1) * BANK], banks[k % 2], ACT.Copy).then_inc(xn_ready, 1)

    return LayerNorm(dve_stats=dve_stats, dve_apply=dve_apply, pool=pool, pe=pe, act=act, ready=xn_ready)


REG = 5
XQ = 32
QW = T + XQ
NQ = T + REG
QC = NQ // 3
KT = T // P
ROWS_S = 2 + 6 * D
ROWS = ROWS_S + 3
NQUAD = B * H // 4
SLOTS = 3
MC = 4 * TPB + 1
HALVES = 2 * MC
LEAD = 14
PAUSE = 2
ROOM = 5
BIG = 1e30
Q_PARTS = [0, 0, 1, 1, 0, 2]
K_PARTS = [0, 1, 0, 1, 2, 0]


def attention(nc, env, tag):
    ctx = env.mark()
    sb, sem, x = env.sb, env.sem, env.x
    ps = env.ps
    bank = [ps[:, i, :] for i in range(8)]

    QS = env.dram(f"{tag}_QS", [B * H, ROWS, QW], BF16)
    KS = env.dram(f"{tag}_KS", [B * H, ROWS_S, T], BF16)
    MR = env.dram(f"{tag}_MR", [4, TOK], BF16)
    CX = env.dram(f"{tag}_CX", [2, XQ], BF16)
    MD = env.dram(f"{tag}_MD", [SLOTS, 3, MC * P], BF16)

    QX = [sb(f"{tag}_QX{i}", [P, 4, QW], BF16) for i in range(SLOTS)]
    KX = [sb(f"{tag}_KX{i}", [P, 2, T], BF16) for i in range(SLOTS)]
    VX = [sb(f"{tag}_VX{i}", [P, KT, 4, 32], F32) for i in range(SLOTS)]
    vq = sb(f"{tag}_vq", [P, NQUAD, KT, 4 * D], F32)
    PR = 4
    prob = [sb(f"{tag}_prob{i}", [P, 2, QC], F32) for i in range(PR)]
    mx = sb(f"{tag}_mx", [P, 2, MC], F32)
    neg = sb(f"{tag}_neg", [P, MC], F32)
    rest = sb(f"{tag}_rest", [P, MC], F32)
    msplit = sb(f"{tag}_msplit", [P, 3, MC], BF16)
    mT = sb(f"{tag}_mT", [3 * MC, P], BF16)
    ast = [sb(f"{tag}_ast{i}", [P, NQ], F32) for i in range(SLOTS)]
    xb = sb(f"{tag}_xb", [P, NT, C], F32)
    span = sb(f"{tag}_span", [P, 2], F32)
    mark = env.mark()
    xn = sb(f"{tag}_xn", [P, TOK], F32)
    qf = sb(f"{tag}_qf", [P, B, QW], F32)
    kf = sb(f"{tag}_kf", [P, B, T], F32)
    qpart = [sb(f"{tag}_qp{i}", [P, B, QW], BF16) for i in range(3)]
    kpart = [sb(f"{tag}_kp{i}", [P, B, T], BF16) for i in range(3)]
    q_tm = sb(f"{tag}_q_tm", [P, NT, C], F32)
    work = sb(f"{tag}_work", [P, NT, C], F32)
    n2 = sb(f"{tag}_n2", [P, NT, H], F32)
    rn = sb(f"{tag}_rn", [P, NT, H], F32)
    root = sb(f"{tag}_root", [P, NT, H], F32)
    half_n2 = sb(f"{tag}_half_n2", [P, NT, H], F32)
    dot = sb(f"{tag}_dot", [P, NT, H], F32)
    sim = sb(f"{tag}_sim", [P, NT], F32)
    ext = sb(f"{tag}_ext", [P, 2, NT], F32)
    mm2 = sb(f"{tag}_mm2", [P, 2], F32)
    mm2a = sb(f"{tag}_mm2a", [P, 2], F32)
    masks = sb(f"{tag}_masks", [P, 4, NT], F32)
    pos = sb(f"{tag}_pos", [P, NT], F32)
    mrow = sb(f"{tag}_mrow", [4 * NT, P], BF16)
    cx = sb(f"{tag}_cx", [2, XQ], BF16)
    ln = layer_norm(nc, env, f"{tag}_ln", xn, [bank[4], bank[5]])
    env.rewind(mark)
    A = sb(f"{tag}_A", [P, NQUAD, NQ], F32)
    o_tm = sb(f"{tag}_o_tm", [P, NT, C], F32)
    o_cm = sb(f"{tag}_o_cm", [P, NT, P], F32)
    rden = sb(f"{tag}_rden", [P, NT + B, H], F32)
    ox = sb(f"{tag}_ox", [REG, B, C], F32)
    env.rewind(ctx)

    s = lambda n: sem(f"{tag}_{n}")
    proj_mm, proj_out, qk_out = s("proj_mm"), s("proj_out"), s("qk_out")
    padded, high_q, rest_q, mid_q, low_q = s("padded"), s("high_q"), s("rest_q"), s("mid_q"), s("low_q")
    high_k, rest_k, mid_k, low_k = s("high_k"), s("rest_k"), s("mid_k"), s("low_k")
    n2_ready, rn_ready, mm_ready, mm_all = s("n2_ready"), s("rn_ready"), s("mm_ready"), s("mm_all")
    masks_ready, masks_t, mrow_ready, cx_ready = s("masks_ready"), s("masks_t"), s("mrow_ready"), s("cx_ready")
    rows_out, consts_out, parts_out, zeros_ready = s("rows_out"), s("consts_out"), s("parts_out"), s("zeros_ready")
    loaded = [s(f"loaded{i}") for i in range(SLOTS)]
    m_saved = [s(f"m_saved{i}") for i in range(SLOTS)]
    m_loaded = [s(f"m_loaded{i}") for i in range(SLOTS)]
    a_free = [s(f"a_free{i}") for i in range(SLOTS)]
    score_ready, score_free = s("score_ready"), s("score_free")
    msplit_ready, m_t, mT_ready = s("msplit_ready"), s("m_t"), s("mT_ready")
    v_ready, ones_ready = s("v_ready"), s("ones_ready")
    st_ready, exp_done, prob_free = s("st_ready"), s("exp_done"), s("prob_free")
    sums_out = s("sums_out")
    chain_sem = s("dve_step")
    fin_t, fin_o, fin_xt, fin_b, fin_oc, fin_p = s("fin_t"), s("fin_o"), s("fin_xt"), s("fin_b"), s("fin_oc"), s("fin_p")
    x_done, passed = s("x_done"), s("passed")
    STEPS = 3 * KT

    score = [bank[4], bank[5], bank[6]]
    acc = bank[7]
    turned = score[0][:, 0:P // 2].bitcast(BF16)[0:3 * MC, :]

    def sums_bank(t):
        return bank[4] if t < TPB else bank[t % 2]

    def back_bank(t):
        return bank[5] if t < TPB else bank[2 + t % 2]

    def out_bank(t):
        return bank[6] if t < TPB else bank[4 + t % 2]

    def sp(e):
        def rows_of(dst, part, b, j, width):
            e.dma_start(dst[b * H:(b + 1) * H, 2 + D * j:2 + D * j + D, 0:width],
                        part[:, b, 0:width]).then_inc(parts_out, 16)
        e.wait_ge(cx_ready, 2)
        e.dma_start(CX, cx[:, :]).then_inc(consts_out, 16)
        e.wait_ge(zeros_ready, 3 * SLOTS)
        e.dma_start(QS[:, ROWS_S:ROWS, :], QX[0][0:B * H, 0:3, :]).then_inc(parts_out, 16)

        def parts(b):
            for part, (q_sem, k_sem) in enumerate(((high_q, high_k), (mid_q, mid_k), (low_q, low_k))):
                for dst, tiles, table, ready, width in ((KS, kpart, K_PARTS, k_sem, T), (QS, qpart, Q_PARTS, q_sem, QW)):
                    e.wait_ge(ready, 1)
                    for j in range(6):
                        if table[j] == part:
                            rows_of(dst, tiles[part], b, j, width)

        def mask_rows(b):
            heads = slice(b * H, (b + 1) * H)
            for dst, rows in ((QS, slice(0, 2)), (KS, slice(2, 4))):
                e.dma_start(dst[heads, 0:2, 0:T], MR[rows, b * T:(b + 1) * T]
                            .rearrange("(o k) n -> o k n", o=1).broadcast_to([H, 2, T])).then_inc(parts_out, 16)
            e.dma_start(QS[heads, 0:2, T:QW], CX.rearrange("(o k) n -> o k n", o=1).broadcast_to([H, 2, XQ]))\
                .then_inc(parts_out, 16)

        parts(0)
        e.wait_ge(mrow_ready, 1)
        e.dma_start(MR.rearrange("k (t p) -> (k t) p", p=P), mrow[:, :]).then_inc(rows_out, 16)
        e.wait_ge(rows_out, 16)
        e.wait_ge(consts_out, 16)
        mask_rows(0)
        e.wait_ge(parts_out, 16 * (12 + 3 + 1))

        def load(q, slot):
            for half in range(2):
                e.dma_start(QX[slot][64 * half:64 * half + ROWS, half::2, :],
                            QS[bass.ds(q * 4, 4)]
                            .rearrange("(p e) r n -> e r p n", e=2)[half]).then_inc(loaded[slot], 16)
                e.dma_start(KX[slot][64 * half:64 * half + ROWS_S, :, :],
                            KS[bass.ds(q * 4, 4)].rearrange("(p e) r n -> e r p n", e=2)[half])\
                    .then_inc(loaded[slot], 16)

        def maxima(q, slot, it):
            e.wait_ge(mT_ready, q + 1)
            e.dma_start(MD[slot].rearrange("j (c p) -> (j c) p", p=P), mT[:, :]).then_inc(m_saved[slot], 16)
            e.wait_ge(m_saved[slot], 16 * (it + 1))
            for half in range(2):
                rows = slice(64 * half + ROWS_S, 64 * half + ROWS)
                src = MD[slot][:, 0:4 * T].rearrange("j (p e n) -> e j p n", p=2, e=2)[half]
                e.dma_start(QX[slot][rows, half::2, 0:T], src).then_inc(m_loaded[slot], 16)
                src = MD[slot][:, 4 * T:].rearrange("j (p e n) -> e j p n", p=2, e=2)[half]
                e.dma_start(QX[slot][rows, half::2, T:QW], src).then_inc(m_loaded[slot], 16)

        def keep(q, slot):
            e.wait_ge(sums_out, 3 * q + 4)
            e.dma_start(A[:, bass.ds(q, 1), :].rearrange("p o n -> p (o n)"), ast[slot][:, :]).then_inc(a_free[slot], 16)

        for slot in range(SLOTS):
            e.sem_inc(a_free[slot], 16)
        load(0, 0)
        load(1, 1)
        parts(1)
        mask_rows(1)
        maxima(0, 0, 0)
        e.wait_ge(parts_out, 16 * (B * (12 + 3) + 1))
        with e.Fori(0, 2) as it:
            for u in range(3):
                q = it * 3 + u
                e.wait_ge(st_ready, q * (2 * STEPS) + 1)
                load(q + 2, (u + 2) % 3)
                maxima(q + 1, (u + 1) % 3, it + (1 if u == 2 else 0))
                keep(q, u)
        maxima(7, 1, 2)
        keep(6, 0)
        keep(7, 1)
        for slot in range(SLOTS):
            e.wait_ge(a_free[slot], 16 * (4 if slot < 2 else 3))

    def pool(g):
        nc.gpsimd.memset(qf[:, :, NQ:QW], 0.0).then_inc(padded, 1)
        nc.gpsimd.memset(cx[:], 0.0).then_inc(cx_ready, 1)
        g.wait_ge(cx_ready, 1)
        nc.gpsimd.memset(cx[0:1, 0:REG], 1.0).then_inc(cx_ready, 1)
        ln.pool(g)
        for i in range(SLOTS):
            nc.gpsimd.memset(KX[i][:, :, :], 1.0).then_inc(zeros_ready, 1)
            nc.gpsimd.memset(QX[i][:, :, :], 0.0).then_inc(zeros_ready, 1)
            nc.gpsimd.memset(VX[i][:, :, :, :], 0.0).then_inc(zeros_ready, 1)
        g.wait_ge(zeros_ready, 3 * SLOTS)
        for i in range(SLOTS):
            nc.gpsimd.memset(VX[i][:, :, :, D:D + 1], 1.0).then_inc(ones_ready, 1)
        g.wait_ge(high_k, 1)
        nc.gpsimd.tensor_tensor(kf[:], kf[:], kpart[0][:], ALU.subtract).then_inc(rest_k, 1)
        g.wait_ge(mm_ready, 1)
        nc.gpsimd.partition_all_reduce(mm2a[:], mm2[:], P, env.rmax).then_inc(mm_all, 1)
        g.wait_ge(mid_k, 1)
        nc.gpsimd.tensor_tensor(kpart[2][:], kf[:], kpart[1][:], ALU.subtract).then_inc(low_k, 1)

    def act(a):
        ln.act(a)
        for j in range(8):
            t0 = 2 * j
            b, k0 = t0 // KT, t0 % KT
            a.wait_ge(proj_mm, j + 1)
            both = bank[j % 4].rearrange("p (t c) -> p t c", t=2)
            nc.scalar.activation(q_tm[:, t0:t0 + 2, :], both[:, :, 0:C], ACT.Copy).then_inc(qk_out, 1)
            for t in range(2):
                last = nc.scalar.activation(vq[:, 4 * b:4 * b + 4, k0 + t, :],
                                            both[:, t, C:2 * C].rearrange("p (q n) -> p q n", q=4), ACT.Copy)
            last.then_inc(proj_out, 1)
        for j in range(8, 16):
            c, is_k = (j - 8) // 2, j % 2
            b, half = c // 2, c % 2
            a.wait_ge(proj_mm, j + 1)
            dst = (kf if is_k else qf)[:, b, half * BANK:(half + 1) * BANK]
            nc.scalar.activation(dst, bank[j % 4], ACT.Copy, scale=1.0 if is_k else D ** -0.5).then_inc(proj_out, 1)
            if j == 13:
                a.wait_ge(n2_ready, 1)
                nc.scalar.activation(root[:], n2[:], ACT.Sqrt).then_inc(rn_ready, 1)
        a.wait_ge(proj_out, 16)
        nc.scalar.activation(kpart[0][:], kf[:], ACT.Copy).then_inc(high_k, 1)
        a.wait_ge(padded, 2)
        nc.scalar.activation(qpart[0][:], qf[:], ACT.Copy).then_inc(high_q, 1)
        a.wait_ge(rest_k, 1)
        nc.scalar.activation(kpart[1][:], kf[:], ACT.Copy).then_inc(mid_k, 1)
        a.wait_ge(rest_q, 1)
        nc.scalar.activation(qpart[1][:], qf[:], ACT.Copy).then_inc(mid_q, 1)
        a.wait_ge(masks_t, 1)
        nc.scalar.activation(mrow[:, :], bank[0][0:4 * NT, 0:P], ACT.Copy).then_inc(mrow_ready, 1)
        a.sem_inc(exp_done, 2)
        a.sem_inc(sums_out, 1)

        def output_copy(t):
            a.wait_ge(fin_b, t + 1)
            nc.scalar.activation(o_cm[:, t, :], back_bank(t)[:, 0:P], ACT.Copy).then_inc(fin_oc, 1)

        def quad(q, slot, it, finish=False):
            for i in range(STEPS):
                for p in range(2):
                    n = 2 * i + p
                    a.wait_ge(prob_free, q * STEPS + i + 1)
                    a.wait_ge(st_ready, q * 2 * STEPS + n + 1)
                    nc.scalar.activation(prob[n % PR][:, :, :], ps[:, 2 * (n % 2):2 * (n % 2) + 2, 0:QC], ACT.Exp)\
                        .then_inc(exp_done, 1)
                if finish and i % 3 == 1:
                    output_copy(i // 3)
                if i % KT == 0 and i:
                    copy_sums(q, slot, it, i // KT - 1)
            copy_sums(q, slot, it, 2)

        def copy_sums(q, slot, it, c):
            a.wait_ge(prob_free, q * STEPS + (c + 1) * KT + 2)
            if c == 0:
                a.wait_ge(a_free[slot], 16 * (it + 1))
            nc.scalar.activation(ast[slot][:, c * QC:(c + 1) * QC], acc[:, 0:QC], ACT.Copy)\
                .then_inc(sums_out, 1)

        with a.Fori(0, 2) as it:
            for u in range(3):
                quad(it * 3 + u, u, it)
        quad(6, 0, 2)
        quad(7, 1, 2, finish=True)
        for t in range(TPB, NT):
            output_copy(t)

    def dve(v):
        ln.dve(v)
        ch = Chain(v, chain_sem)
        v.wait_ge(ln.ready, NCH)
        ch(nc.vector.tensor_tensor(xb[:], x[:], env.half_bproj.unsqueeze(1).broadcast_to([P, NT, C]), ALU.add))
        v.wait_ge(qk_out, 8)
        heads = lambda ap: ap.rearrange("p t (h d) -> p t h d", d=D)
        ch(nc.vector.tensor_tensor(work[:], q_tm[:], q_tm[:], ALU.mult))
        nc.vector.reduce_sum(n2[:], heads(work[:]), AX_X).then_inc(n2_ready, 1)
        v.wait_ge(n2_ready, 1)
        ch(nc.vector.tensor_tensor(work[:], q_tm[:], env.qg_unit.unsqueeze(1).broadcast_to([P, NT, C]), ALU.mult))
        ch(nc.vector.reduce_sum(dot[:], heads(work[:]), AX_X))
        v.wait_ge(rn_ready, 1)
        inverse_root(nc, ch, rn[:], root[:], n2[:], half_n2[:])
        ch(nc.vector.tensor_tensor(dot[:], dot[:], rn[:], ALU.mult))
        ch(nc.vector.reduce_sum(sim[:], dot[:], AX_X))
        ch(nc.vector.tensor_scalar(ext[:, 0, :], sim[:], -1.0, None, ALU.mult))
        ch(nc.vector.tensor_copy(ext[:, 1, :], sim[:]))
        for b in range(B):
            ch(nc.vector.memset(ext[0:REG, :, b * TPB:b * TPB + 1], -3e38))
        nc.vector.reduce_max(mm2[:], ext[:], AX_X).then_inc(mm_ready, 1)
        v.wait_ge(proj_out, 16)
        v.wait_ge(padded, 1)
        nc.vector.tensor_copy(qf[:, :, T:NQ], qf[:, :, 0:REG]).then_inc(padded, 1)
        v.wait_ge(high_q, 1)
        nc.vector.tensor_tensor(qf[:], qf[:], qpart[0][:], ALU.subtract).then_inc(rest_q, 1)
        v.wait_ge(mm_all, 1)
        ch(nc.vector.tensor_tensor(span[:, 0:1], mm2a[:, 0:1], mm2a[:, 1:2], ALU.add))
        ch(nc.vector.reciprocal(span[:, 1:2], span[:, 0:1]))
        ch(nc.vector.tensor_scalar(pos[:], sim[:], mm2a[:, 0:1], span[:, 1:2], ALU.add, ALU.mult))
        ch(nc.vector.tensor_scalar(pos[:], pos[:], 0.9, None, ALU.is_gt))
        ch(nc.vector.tensor_tensor(masks[:, 1, :], pos[:], env.is_reg[:], ALU.max))
        ch(nc.vector.tensor_scalar(masks[:, 0, :], masks[:, 1, :], -1.0, 1.0, ALU.mult, ALU.add))
        ch(nc.vector.tensor_scalar(masks[:, 3, :], masks[:, 0, :], -BIG, None, ALU.mult))
        ch(nc.vector.tensor_tensor(masks[:, 2, :], masks[:, 1, :], env.is_reg[:], ALU.subtract))
        nc.vector.tensor_scalar(masks[:, 2, :], masks[:, 2, :], -BIG, None, ALU.mult).then_inc(masks_ready, 1)
        v.wait_ge(mid_q, 1)
        nc.vector.tensor_tensor(qpart[2][:], qf[:], qpart[1][:], ALU.subtract).then_inc(low_q, 1)
        v.wait_ge(zeros_ready, 3 * SLOTS)
        v.wait_ge(ones_ready, SLOTS)
        v.wait_ge(proj_out, 16)
        v.sem_inc(score_free, 3)
        per, first = 5, ch.n

        def largest(q, slot, ks, used):
            for k in ks:
                if k == HALVES // 2:
                    if used:
                        v.wait_ge(prob_free, (q - 1) * STEPS + 2)
                    nc.vector.tensor_scalar(VX[slot][:, :, :, 0:D],
                                            vq[:, bass.ds(q, 1), :, :].rearrange("p o k (h d) -> p (o k) h d", d=D),
                                            1.0, None, ALU.mult).then_inc(v_ready, 1)
                v.wait_ge(score_ready, q * HALVES + k + 1)
                nc.vector.reduce_max(mx[:, k % 2, k // 2:k // 2 + 1], score[k % 3], AX_X).then_inc(score_free, 1)

        def split(q):
            ch.base, ch.n = q * per + first, 0
            v.wait_ge(score_free, q * HALVES + HALVES + 3)
            ch(nc.vector.tensor_tensor(neg[:], mx[:, 0, :], mx[:, 1, :], ALU.max))
            ch(nc.vector.tensor_scalar(neg[:], neg[:], -1.0, None, ALU.mult))
            ch(nc.vector.tensor_scalar(msplit[:, 0, :], neg[:], 1.0, None, ALU.mult))
            ch(nc.vector.tensor_tensor(rest[:], neg[:], msplit[:, 0, :], ALU.subtract))
            ch(nc.vector.tensor_scalar(msplit[:, 1, :], rest[:], 1.0, None, ALU.mult))
            nc.vector.tensor_tensor(msplit[:, 2, :], rest[:], msplit[:, 1, :], ALU.subtract).then_inc(msplit_ready, 1)
            assert ch.n == per

        def take_turned(q, saved):
            if saved is not None:
                v.wait_ge(*saved)
            v.wait_ge(m_t, q + 1)
            nc.vector.tensor_scalar(mT[:, :], turned, 1.0, None, ALU.mult).then_inc(mT_ready, 1)

        largest(0, 0, range(HALVES), False)
        split(0)
        take_turned(0, None)
        largest(1, 1, range(LEAD), False)
        with v.Fori(0, 2) as it:
            for u in range(3):
                q = it * 3 + u
                largest(q + 1, (u + 1) % 3, range(LEAD, HALVES), True)
                split(q + 1)
                take_turned(q + 1, (m_saved[u], it * 16 + 16))
                largest(q + 2, (u + 2) % 3, range(LEAD), True)
        largest(7, 1, range(LEAD, HALVES), True)
        split(7)
        take_turned(7, (m_saved[0], 48))
        ch.base, ch.n = first + 8 * per, 0
        def registers(b):
            r = NT + b
            v.wait_ge(fin_xt, b + 1)
            hv = bank[6 + b].rearrange("p (h d) -> p h d", d=32)
            ch(nc.vector.reciprocal(rden[0:REG, r, :], hv[0:REG, :, D]))
            ch(nc.vector.tensor_tensor(ox[:, b, :].rearrange("p (h d) -> p h d", d=D), hv[0:REG, :, 0:D],
                                       rden[0:REG, r, :].unsqueeze(2).broadcast_to([REG, H, D]), ALU.mult))

        def normalise(t):
            v.wait_ge(fin_t, t + 1)
            hv = sums_bank(t).rearrange("p (h d) -> p h d", d=32)
            ch(nc.vector.reciprocal(rden[:, t, :], hv[:, :, D]))
            last = nc.vector.tensor_tensor(o_tm[:, t, :].rearrange("p (h d) -> p h d", d=D), hv[:, :, 0:D],
                                           rden[:, t, :].unsqueeze(2).broadcast_to([P, H, D]), ALU.mult)
            if t % TPB == 0:
                ch(last)
                ch(nc.vector.tensor_tensor(o_tm[0:REG, t, :], o_tm[0:REG, t, :], ox[:, t // TPB, :], ALU.add))
                last = nc.vector.tensor_scalar(o_tm[0:REG, t, :], o_tm[0:REG, t, :], 0.5, None, ALU.mult)
            last.then_inc(fin_o, 1)

        registers(0)
        for t in range(TPB):
            normalise(t)
            add(v, t)
        registers(1)
        for t in range(TPB, NT):
            normalise(t)
            if t >= TPB + 2:
                add(v, t - 2)
        add(v, NT - 2)
        add(v, NT - 1)

    def add(v, t):
        v.wait_ge(fin_p, t + 1)
        nc.vector.scalar_tensor_tensor(x[:, t, :], out_bank(t)[:, 0:C], 0.5, xb[:, t, :], ALU.mult, ALU.add)\
            .then_inc(x_done, 1)

    def pe(t_):
        wqkv, wproj = env.w["qkv"], env.w["proj"]
        ln.pe(t_)
        for j in range(8):
            if j >= 4:
                t_.wait_ge(proj_out, j - 3)
            t_.wait_ge(ln.ready, j // 2 + 1)
            for t in range(2):
                tile = 2 * j + t
                for which in (0, 2):
                    at = t * 2 * C + (which // 2) * C
                    last = nc.tensor.matmul(bank[j % 4][:, at:at + C], xn[:, tile * P:(tile + 1) * P],
                                            wqkv[:, which * C:(which + 1) * C], start=True, stop=True)
            last.then_inc(proj_mm, 1)
        for j in range(8, 16):
            c, is_k = (j - 8) // 2, j % 2
            t_.wait_ge(proj_out, j - 3)
            nc.tensor.matmul(bank[j % 4], wqkv[:, is_k * C:(is_k + 1) * C], xn[:, c * BANK:(c + 1) * BANK],
                             start=True, stop=True).then_inc(proj_mm, 1)
        t_.wait_ge(masks_ready, 1)
        t_.wait_ge(proj_out, 16)
        nc.tensor.transpose(bank[0][0:4 * NT, 0:P], masks[:, :, :].rearrange("p k t -> p (k t)"), env.ident[:])\
            .then_inc(masks_t, 1)
        t_.wait_ge(mrow_ready, 1)
        t_.sem_inc(prob_free, 2)

        def scores(q, slot, k):
            col, half = k // 2, k % 2
            t_.wait_ge(score_free, q * HALVES + k + 1)
            if col == MC - 1:
                t_.sem_inc(passed, 1)
                for h in range(4):
                    last = nc.tensor.matmul(score[k % 3][XQ * h:XQ * h + XQ, :], QX[slot][:, h, T:QW],
                                            KX[slot][:, h // 2, half * BANK:(half + 1) * BANK], start=True, stop=True)
            else:
                head, tile = col // TPB, col % TPB
                last = nc.tensor.matmul(score[k % 3], QX[slot][:, head, tile * P:(tile + 1) * P],
                                        KX[slot][:, head // 2, half * BANK:(half + 1) * BANK], start=True, stop=True)
            last.then_inc(score_ready, 1)

        def turn(q):
            t_.wait_ge(msplit_ready, q + 1)
            nc.tensor.transpose(turned, msplit[:, :, :].rearrange("p j c -> p (j c)"), env.ident_b[:]).then_inc(m_t, 1)

        def pair(q, slot, i, p):
            c, kt = i // KT, i % KT
            t_.wait_ge(exp_done, q * 2 * STEPS + 2 * i + p + 1)
            for e in range(2):
                last = nc.tensor.matmul(bank[2 * p + e][:, 0:QC], KX[slot][:, p, kt * P:(kt + 1) * P],
                                        QX[slot][:, 2 * p + e, c * QC:(c + 1) * QC], start=True, stop=True)
            last.then_inc(st_ready, 1)

        def sums(q, slot, i):
            c, kt = i // KT, i % KT
            if kt == 0:
                t_.wait_ge(sums_out, q * 3 + (c + 1))
            t_.wait_ge(exp_done, q * 2 * STEPS + 2 * i + 4)
            for h in range(4):
                n = 2 * i + h // 2
                last = nc.tensor.matmul(acc[32 * h:32 * h + 32, 0:QC], VX[slot][:, kt, h, :],
                                        prob[n % PR][:, h % 2, :], start=(kt == 0), stop=(kt == KT - 1))
            last.then_inc(prob_free, 1)

        def ahead(q, slot, it, j):
            k = j + LEAD
            if k < HALVES:
                scores(q + 1, (slot + 1) % SLOTS, k)
            elif k == HALVES + PAUSE:
                turn(q + 1)
            elif k >= HALVES + ROOM and more(q):
                if k == HALVES + ROOM:
                    t_.wait_ge(loaded[(slot + 2) % SLOTS], 64 * (it + (slot + 2) // SLOTS) + 64)
                    t_.wait_ge(mT_ready, q + 2)
                scores(q + 2, (slot + 2) % SLOTS, k - HALVES - ROOM)

        def more(q):
            return not isinstance(q, int) or q + 2 < NQUAD

        def turn_sums(t):
            if t and t != TPB:
                t_.wait_ge(fin_o, t if t < TPB else t - 1)
            b, tt = t // TPB, t % TPB
            for qd in range(4):
                last = nc.tensor.transpose(sums_bank(t)[:, qd * P:(qd + 1) * P],
                                           A[:, 4 * b + qd, tt * P:(tt + 1) * P], env.ident[:])
            last.then_inc(fin_t, 1)

        def turn_register_sums(b):
            for qd in range(4):
                last = nc.tensor.transpose(bank[6 + b][0:REG, qd * P:(qd + 1) * P], A[:, 4 * b + qd, T:NQ], env.ident[:])
            last.then_inc(fin_xt, 1)

        def back(t):
            t_.wait_ge(fin_o, t + 1)
            if t:
                t_.wait_ge(fin_oc, t if t < TPB else t - 1)
            nc.tensor.transpose(back_bank(t)[:, 0:P], o_tm[:, t, :], env.ident[:]).then_inc(fin_b, 1)

        def project(t):
            t_.wait_ge(fin_oc, t + 1)
            if t:
                t_.wait_ge(x_done, t if t < TPB else t - 1)
            nc.tensor.matmul(out_bank(t)[:, 0:C], o_cm[:, t, :], wproj[:], start=True, stop=True)\
                .then_inc(fin_p, 1)

        def quad(q, slot, it, nxt):
            t_.wait_ge(m_loaded[slot], 64 * it + 64)
            t_.wait_ge(v_ready, q + 1)
            if not nxt:
                for k in range(SLOTS):
                    t_.wait_ge(a_free[k], 16 * (3 if k == 0 else 2))
                turn_register_sums(0)
            for i in range(STEPS):
                beside = range((HALVES + ROOM) * i // STEPS, (HALVES + ROOM) * (i + 1) // STEPS) if nxt else ()
                for p in range(2):
                    pair(q, slot, i, p)
                    for j in beside[p:p + 1]:
                        ahead(q, slot, it, j)
                if not nxt:
                    if i % 3 == 0:
                        turn_sums(i // 3)
                    elif i % 3 == 1:
                        back(i // 3)
                    else:
                        project(i // 3)
                if i:
                    sums(q, slot, i - 1)
                for j in beside[2:]:
                    ahead(q, slot, it, j)
            sums(q, slot, STEPS - 1)

        t_.wait_ge(loaded[0], 64)
        for k in range(HALVES):
            scores(0, 0, k)
        turn(0)
        t_.wait_ge(loaded[1], 64)
        t_.wait_ge(mT_ready, 1)
        for k in range(LEAD):
            scores(1, 1, k)
        with t_.Fori(0, 2) as it:
            for u in range(3):
                quad(it * 3 + u, u, it, True)
        quad(6, 0, 2, True)
        quad(7, 1, 2, False)
        for slot in range(SLOTS):
            t_.wait_ge(a_free[slot], 16 * (4 if slot < 2 else 3))
        t_.wait_ge(sums_out, 3 * NQUAD + 1)
        turn_register_sums(1)
        for t in range(TPB, NT):
            turn_sums(t)
            if t >= TPB + 1:
                back(t - 1)
            if t >= TPB + 2:
                project(t - 2)
        back(NT - 1)
        project(NT - 2)
        project(NT - 1)

    return Sublayer(parts=dict(sp=sp, pool=pool, act=act, dve=dve, pe=pe), done=(x_done, NT))


TM, TD = 32, 64
GN_EPS = 1e-5 * 64
MIXES = ("w", "k", "v", "r", "g")


def rwkv_weights(env, weight, loads, ins):
    for n in "rkvgo":
        weight(f"W_{n}", ins[f"L0_attn_W_{n}"], [C, C])
    weight("maa_w1", ins["L0_attn_time_maa_w1"], [C, 5 * TM])
    weight("td_w1", ins["L0_attn_time_decay_w1"], [C, TD])
    weight("td_w2", ins["L0_attn_time_decay_w2"], [TD, C])
    env.w["rows"] = env.sb("w_rows", [10, C], F32)
    names = ["time_maa_" + m for m in MIXES] + ["time_maa_x", "time_decay", "ln_gamma", "ln_beta"]
    for i, n in enumerate(names):
        loads.append((env.w["rows"][i:i + 1, :], ins[f"L0_attn_{n}"].rearrange("(o c) -> o c", o=1)))
    loads.append((env.w["rows"][9:10, :], ins["L0_attn_time_faaaa"].rearrange("(o h) k -> o (h k)", o=1)))


def rwkv(nc, env, tag):
    m0 = env.mark()
    sb, x, w = env.sb, env.x, env.w
    ps = env.ps
    bank = [ps[:, i, :] for i in range(8)]
    w2_dram = env.ins["L0_attn_time_maa_w2"]
    xn = sb(f"{tag}_xn", [P, B, T], F32)
    xx = sb(f"{tag}_xx", [P, B, T], F32)
    mixed = [sb(f"{tag}_mixed{i}", [P, B, T], F32) for i in range(2)]
    low = [sb(f"{tag}_low{i}", [P, B, T], F32) for i in range(2)]
    w2 = sb(f"{tag}_w2", [P, 5, C], F32)
    cols = sb(f"{tag}_cols", [P, 10], F32)
    r_cm = sb(f"{tag}_r", [P, B, T], F32)
    k_cm = sb(f"{tag}_k", [P, B, T], F32)
    g_cm = sb(f"{tag}_g", [P, B, T], F32)
    wd_cm = sb(f"{tag}_wd", [P, B, T], F32)
    xv = sb(f"{tag}_xv", [P, B, T], F32)
    head_sum = sb(f"{tag}_head_sum", [P, H], F32)
    wv_rep = [sb(f"{tag}_wv_rep{i}", [P, C], F32) for i in range(2)]
    bonus = sb(f"{tag}_bonus", [P, NT, H], F32)
    stat = sb(f"{tag}_stat", [P, 4, NT * H], F32)
    mark = env.mark()
    ln = layer_norm(nc, env, f"{tag}_ln", xn[:].rearrange("p b t -> p (b t)"), [bank[4], bank[5]])
    env.rewind(mark)
    kv = sb(f"{tag}_kv", [P, B, T], F32)
    state = [sb(f"{tag}_state{i}", [P, B, T + 1], F32) for i in range(2)]
    read = [sb(f"{tag}_read{i}", [P, B, T], F32) for i in range(2)]
    env.rewind(m0)
    v_tm, y, yn, yg = low[0], low[1], mixed[0], mixed[1]
    tm = lambda t: t[:].rearrange("p b t -> p (b t)").rearrange("p (n h j) -> p n h j", h=H, j=D)
    flat = lambda t: t[:].rearrange("p b t -> p (b t)")

    s = lambda n: env.sem(f"{tag}_{n}")
    w2_zero, w2_in, cols_t, cols_ready, hs_step, hs_ready = (s(n) for n in ("w2_zero", "w2_in", "cols_t", "cols_ready", "hs_step", "hs_ready"))
    step_sem, xxx_ready, low_mm, low_ready, mix_mm, mix_read, mix_ready = (s(n) for n in ("dve_step", "xxx_ready", "low_mm", "low_ready", "mix_mm", "mix_read", "mix_ready"))
    proj_mm, proj_out, decay_step, td_ready = s("proj_mm"), s("proj_out"), s("decay_step"), s("td_ready")
    rep_w, v_mm, v_read, st_ready, read_ready, y_mm = (s(n) for n in ("rep_w", "v_mm", "v_read", "st_ready", "read_ready", "y_mm"))
    ruk_ready, bonus_mm, vtm_mm, vtm_ready, y_out = s("ruk_ready"), s("bonus_mm"), s("vtm_mm"), s("vtm_ready"), s("y_out")
    var_ready, gn_root, yn_ready, yn_t, yn_cm, gated, out_mm, x_done = (s(n) for n in ("var_ready", "gn_root", "yn_ready", "yn_t", "yn_cm", "gated", "out_mm", "x_done"))
    FN = len(MIXES)

    def sp(e):
        e.wait_ge(w2_zero, 1)
        for f in range(FN):
            at = f * TM if f < 4 else 3 * TM
            e.dma_start(w2[at:at + TM, f, :], w2_dram[f]).then_inc(w2_in, 16)

    def pool(g):
        nc.gpsimd.memset(w2[:], 0.0).then_inc(w2_zero, 1)
        nc.gpsimd.memset(head_sum[:], 1.0).then_inc(hs_step, 1)
        g.wait_ge(hs_step, 1)
        nc.gpsimd.affine_select(out=head_sum[:], in_=head_sum[:], compare_op=ALU.is_ge, fill=0.0, base=0,
                                pattern=[[-D, H]], channel_multiplier=1).then_inc(hs_step, 1)
        g.wait_ge(hs_step, 2)
        nc.gpsimd.affine_select(out=head_sum[:], in_=head_sum[:], compare_op=ALU.is_ge, fill=0.0, base=D - 1,
                                pattern=[[D, H]], channel_multiplier=-1).then_inc(hs_ready, 1)
        ln.pool(g)
        g.wait_ge(proj_out, 3 * NCH)
        with g.Fori(0, D // 2) as it:
            for u in range(2):
                g.wait_ge(y_mm, it * 2 + (u + 1))
                g.wait_ge(st_ready, it * 2 + (u + 1))
                nc.gpsimd.tensor_tensor(read[u][:], state[u][:, :, 0:T], r_cm[:], ALU.mult).then_inc(read_ready, 1)

    def act(a):
        a.wait_ge(cols_t, 1)
        nc.scalar.activation(cols[:], bank[7][:, 0:10], ACT.Copy).then_inc(cols_ready, 1)
        ln.act(a)
        for j in range(2 * NCH):
            i, c = j % 2, j // 2
            a.wait_ge(low_mm, j + 1)
            nc.scalar.activation(flat(low[i])[:, c * BANK:(c + 1) * BANK], bank[i * 2 + c % 2], ACT.Tanh)\
                .then_inc(low_ready, 1)
        a.wait_ge(cols_ready, 1)
        n = 0
        for c in range(NCH):
            a.wait_ge(proj_mm, n + 1)
            nc.scalar.activation(flat(wd_cm)[0:TD, c * BANK:(c + 1) * BANK], bank[4 + n % 2][0:TD, :], ACT.Tanh)\
                .then_inc(td_ready, 1)
            n += 1
        for c in range(NCH):
            a.wait_ge(proj_mm, n + 1)
            nc.scalar.activation(flat(g_cm)[:, c * BANK:(c + 1) * BANK], bank[4 + n % 2], ACT.Exp, bias=cols[:, 6:7])\
                .then_inc(proj_out, 1)
            n += 1
        a.wait_ge(proj_out, NCH)
        nc.scalar.activation(wd_cm[:], g_cm[:], ACT.Exp, scale=-1.0).then_inc(decay_step, 1)
        a.wait_ge(decay_step, 1)
        for dst in (k_cm, r_cm):
            for c in range(NCH):
                a.wait_ge(proj_mm, n + 1)
                nc.scalar.activation(flat(dst)[:, c * BANK:(c + 1) * BANK], bank[4 + n % 2], ACT.Copy).then_inc(proj_out, 1)
                n += 1
        for c in range(NCH):
            a.wait_ge(proj_mm, n + 1)
            nc.scalar.activation(flat(g_cm)[:, c * BANK:(c + 1) * BANK], bank[4 + n % 2], ACT.Silu).then_inc(proj_out, 1)
            n += 1
        for c in range(NCH):
            a.wait_ge(vtm_mm, c + 1)
            nc.scalar.activation(flat(v_tm)[:, c * BANK:(c + 1) * BANK], bank[c], ACT.Copy).then_inc(vtm_ready, 1)
        a.wait_ge(var_ready, 1)
        nc.scalar.activation(stat[:, 3, :], stat[:, 1, :], ACT.Sqrt).then_inc(gn_root, 1)
        for c in range(NCH):
            a.wait_ge(yn_t, c + 1)
            nc.scalar.activation(flat(y)[:, c * BANK:(c + 1) * BANK], bank[c], ACT.Identity,
                                 scale=cols[:, 7:8], bias=cols[:, 8:9]).then_inc(yn_cm, 1)

    def dve(v):
        ln.dve(v)
        ch = Chain(v, step_sem)
        v.wait_ge(ln.ready, NCH)
        nc.vector.tensor_tensor(xx[:, :, 1:T], xn[:, :, 0:T - 1], xn[:, :, 1:T], ALU.subtract).then_inc(step_sem, 1)
        nc.vector.tensor_scalar(xx[:, :, 0:1], xn[:, :, 0:1], -1.0, None, ALU.mult).then_inc(step_sem, 1)
        ch.n += 2
        v.wait_ge(step_sem, ch.n)
        v.wait_ge(cols_ready, 1)
        nc.vector.scalar_tensor_tensor(mixed[0][:], xx[:], cols[:, 5:6], xn[:], ALU.mult, ALU.add).then_inc(xxx_ready, 1)
        for i, m in enumerate(ORDER):
            f = MIXES.index(m)
            dst = xv if m == "v" else mixed[(i + 1) % 2]
            if NEEDED[i]:
                v.wait_ge(proj_mm, NEEDED[i])
            if i == 0:
                v.wait_ge(low_mm, 2 * NCH)
            for c in range(NCH):
                sl = slice(c * BANK, (c + 1) * BANK)
                v.wait_ge(mix_mm, i * NCH + c + 1)
                nc.vector.scalar_tensor_tensor(flat(dst)[:, sl], bank[c], cols[:, f:f + 1], flat(xx)[:, sl],
                                               ALU.add, ALU.mult).then_inc(mix_read, 1)
            v.wait_ge(mix_read, (i + 1) * NCH)
            nc.vector.tensor_tensor(dst[:], dst[:], xn[:], ALU.add).then_inc(mix_ready, 1)
        v.wait_ge(proj_out, 3 * NCH)
        ch(nc.vector.tensor_scalar(kv[:], r_cm[:], cols[:, 9:10], None, ALU.mult))
        nc.vector.tensor_tensor(kv[:], kv[:], k_cm[:], ALU.mult).then_inc(ruk_ready, 1)
        v.wait_ge(bonus_mm, 1)
        ch(nc.vector.tensor_copy(bonus[:].rearrange("p t h -> p (t h)"), bank[6][:, 0:NT * H]))
        for i in range(2):
            ch(nc.vector.memset(state[i][:, :, 0:1], 0.0))
        v.sem_inc(v_read, NCH)
        v.sem_inc(y_mm, 2)
        v.sem_inc(read_ready, 2)
        v.wait_ge(decay_step, 1)
        with v.Fori(0, D // 2) as it:
            for u in range(2):
                v.wait_ge(v_mm, it * 8 + (4 * u + 1))
                nc.vector.tensor_scalar(wv_rep[u][:].rearrange("c (h k) -> c h k", k=D),
                                        w["W_v"][:].rearrange("c (h j) -> c h j", j=D)[:, :, bass.ds(it * 2 + u, 1)]
                                        .broadcast_to([P, H, D]), 1.0, None, ALU.mult).then_inc(rep_w, 1)
                for c in range(NCH):
                    sl = slice(c * BANK, (c + 1) * BANK)
                    v.wait_ge(v_mm, it * 8 + (4 * u + c + 5))
                    nc.vector.tensor_tensor(flat(kv)[:, sl], bank[4 + c], flat(k_cm)[:, sl], ALU.mult).then_inc(v_read, 1)
                v.wait_ge(v_read, it * 8 + (4 * u + 8))
                v.wait_ge(read_ready, it * 2 + (u + 1))
                for b in range(B):
                    last = nc.vector.tensor_tensor_scan(state[u][:, b, 1:T + 1], wd_cm[:, b, :], kv[:, b, :], 0.0,
                                                        ALU.mult, ALU.add)
                last.then_inc(st_ready, 1)
        v.wait_ge(y_mm, D + 2)
        yb = ps[:, 0:4, :].rearrange("p k (n j h) -> p (k n) j h", j=D, h=H)
        nc.vector.tensor_copy(tm(y).rearrange("p n h j -> p n j h"), yb).then_inc(y_out, 1)
        v.wait_ge(y_out, 1)
        v.wait_ge(vtm_ready, NCH)
        ch(nc.vector.tensor_tensor(tm(yn), tm(v_tm), bonus[:].unsqueeze(3).broadcast_to([P, NT, H, D]), ALU.mult))
        ch(nc.vector.tensor_tensor(flat(y), flat(y), flat(yn), ALU.add))
        per_head = lambda k: stat[:, k, :].rearrange("p (n h) -> p n h", h=H)
        ch(nc.vector.reduce_sum(per_head(0), tm(y), AX_X))
        ch(nc.vector.tensor_scalar(stat[:, 0, :], stat[:, 0, :], 1.0 / D, None, ALU.mult))
        ch(nc.vector.tensor_tensor(tm(y), tm(y), per_head(0).unsqueeze(3).broadcast_to([P, NT, H, D]), ALU.subtract))
        ch(nc.vector.tensor_tensor(flat(yn), flat(y), flat(y), ALU.mult))
        ch(nc.vector.reduce_sum(per_head(1), tm(yn), AX_X))
        nc.vector.tensor_scalar(stat[:, 1, :], stat[:, 1, :], 1.0 / D, GN_EPS, ALU.mult, ALU.add).then_inc(var_ready, 1)
        v.wait_ge(gn_root, 1)
        inverse_root(nc, ch, stat[:, 2, :], stat[:, 3, :], stat[:, 1, :], stat[:, 0, :])
        nc.vector.tensor_tensor(tm(yn), tm(y), per_head(2).unsqueeze(3).broadcast_to([P, NT, H, D]), ALU.mult)\
            .then_inc(yn_ready, 1)
        for c in range(NCH):
            sl = slice(c * BANK, (c + 1) * BANK)
            v.wait_ge(yn_cm, c + 1)
            nc.vector.tensor_tensor(flat(yg)[:, sl], flat(y)[:, sl], flat(g_cm)[:, sl], ALU.mult).then_inc(gated, 1)
        for t in range(NT):
            v.wait_ge(out_mm, t + 1)
            nc.vector.tensor_tensor(x[:, t, :], bank[4 + t % 4][:, 0:C], x[:, t, :], ALU.add).then_inc(x_done, 1)

    ORDER = ("w", "k", "r", "g", "v")
    NEEDED = [0, 0, NCH, 3 * NCH, 0]
    PROJ = {"w": "td_w1", "k": "W_k", "r": "W_r", "g": "W_g"}

    def pe(t_):
        nc.tensor.transpose(bank[7][:, 0:10], w["rows"][:], env.ident[0:10, 0:10]).then_inc(cols_t, 1)
        ln.pe(t_)
        t_.wait_ge(xxx_ready, 1)
        for j in range(2 * NCH):
            i, c = j % 2, j // 2
            if c >= 2:
                t_.wait_ge(low_ready, j - 3)
            nc.tensor.matmul(bank[i * 2 + c % 2], w["maa_w1"][:, i * TM:i * TM + 4 * TM],
                             flat(mixed[0])[:, c * BANK:(c + 1) * BANK], start=True, stop=True).then_inc(low_mm, 1)
        t_.wait_ge(w2_in, 16 * FN)
        t_.wait_ge(low_ready, 2 * NCH)
        n = 0

        def mix(i):
            f = MIXES.index(ORDER[i])
            for c in range(NCH):
                if i:
                    t_.wait_ge(mix_read, (i - 1) * NCH + c + 1)
                nc.tensor.matmul(bank[c], w2[:, f, :], flat(low[0 if f < 4 else 1])[:, c * BANK:(c + 1) * BANK],
                                 start=True, stop=True).then_inc(mix_mm, 1)

        def outs(k):
            if k >= NCH:
                t_.wait_ge(td_ready, NCH)
                if k > NCH:
                    t_.wait_ge(proj_out, k - NCH)
            elif k > 0:
                t_.wait_ge(td_ready, k)

        mix(0)
        for i, m in enumerate(ORDER):
            if i + 1 < FN:
                mix(i + 1)
            t_.wait_ge(mix_ready, i + 1)
            if m == "v":
                break
            src = mixed[(i + 1) % 2]
            wt = w[PROJ[m]]
            for c in range(NCH):
                outs(n - 1)
                rows = TD if m == "w" else P
                nc.tensor.matmul(bank[4 + n % 2][0:rows, :], wt[:], flat(src)[:, c * BANK:(c + 1) * BANK],
                                 start=True, stop=True).then_inc(proj_mm, 1)
                n += 1
            if m == "w":
                for c in range(NCH):
                    outs(n - 1)
                    t_.wait_ge(td_ready, c + 1)
                    nc.tensor.matmul(bank[4 + n % 2], w["td_w2"][:], flat(wd_cm)[0:TD, c * BANK:(c + 1) * BANK],
                                     start=True, stop=True).then_inc(proj_mm, 1)
                    n += 1
        t_.wait_ge(hs_ready, 1)
        t_.wait_ge(ruk_ready, 1)
        for t in range(NT):
            last = nc.tensor.matmul(bank[6][:, t * H:(t + 1) * H], flat(kv)[:, t * P:(t + 1) * P], head_sum[:],
                                    start=True, stop=True)
        last.then_inc(bonus_mm, 1)
        t_.wait_ge(proj_out, 4 * NCH)
        t_.wait_ge(mix_read, FN * NCH)
        for t in range(NT):
            last = nc.tensor.matmul(bank[t // 4][:, t % 4 * P:(t % 4 + 1) * P], flat(xv)[:, t * P:(t + 1) * P],
                                    w["W_v"][:], start=True, stop=True)
            if t % 4 == 3:
                last.then_inc(vtm_mm, 1)
        t_.wait_ge(vtm_ready, NCH)
        t_.sem_inc(v_mm, NCH)

        def values(it, u):
            t_.wait_ge(rep_w, it * 2 + (u + 1))
            for c in range(NCH):
                t_.wait_ge(v_read, it * 8 + (4 * u + c + 1))
                nc.tensor.matmul(bank[4 + c], wv_rep[u % 2][:], flat(xv)[:, c * BANK:(c + 1) * BANK],
                                 start=True, stop=True).then_inc(v_mm, 1)

        def readings(it, u):
            t_.wait_ge(read_ready, it * 2 + (u + 3))
            for t in range(NT):
                at = (it * 2 + u) * H + t % 4 * P
                last = nc.tensor.matmul(ps[:, t // 4, bass.ds(at, H)],
                                        flat(read[u])[:, t * P:(t + 1) * P], head_sum[:], start=True, stop=True)
            last.then_inc(y_mm, 1)

        values(0, 0)
        with t_.Fori(0, D // 2 - 1) as it:
            for u in range(2):
                values(it, u + 1)
                readings(it, u)
        values(D // 2 - 1, 1)
        readings(D // 2 - 1, 0)
        readings(D // 2 - 1, 1)
        t_.wait_ge(yn_ready, 1)
        for t in range(NT):
            last = nc.tensor.transpose(bank[t // 4][:, t % 4 * P:(t % 4 + 1) * P], flat(yn)[:, t * P:(t + 1) * P],
                                       env.ident[:])
            if t % 4 == 3:
                last.then_inc(yn_t, 1)
        for t in range(NT):
            t_.wait_ge(gated, t // 4 + 1)
            if t >= 4:
                t_.wait_ge(x_done, t - 3)
            nc.tensor.matmul(bank[4 + t % 4][:, 0:C], flat(yg)[:, t * P:(t + 1) * P], w["W_o"][:],
                             start=True, stop=True).then_inc(out_mm, 1)

    return Sublayer(parts=dict(sp=sp, pool=pool, act=act, dve=dve, pe=pe), done=(x_done, NT))


NE, FF = 8, 512
FB = FF // P


def moe_weights(env, weight, loads, ins):
    weight("router", ins["L1_ffn_router_w"], [C, NE])
    weight("router_b", ins["L1_ffn_router_b"].rearrange("(o e) -> o e", o=1).broadcast_to([P, NE]), [P, NE])
    weight("b1_rows", ins["L1_ffn_b1"].rearrange("e (f p) -> (e f) p", p=P), [NE * FB, P])
    weight("b2", ins["L1_ffn_b2"], [NE, C])


def moe(nc, env, tag):
    m0 = env.mark()
    sb, x = env.sb, env.x
    ps = env.ps
    bank = [ps[:, i, :] for i in range(8)]
    w1, w2 = env.ins["L1_ffn_w1"], env.ins["L1_ffn_w2"]
    xn = sb(f"{tag}_xn", [P, TOK], F32)
    W1 = [sb(f"{tag}_W1_{i}", [P, FF], F32) for i in range(2)]
    W2 = [sb(f"{tag}_W2_{i}", [P, FB, C], F32) for i in range(2)]
    b1_all = sb(f"{tag}_b1_all", [P, NE, FB], F32)
    b1 = [sb(f"{tag}_b1_{i}", [P, FB], F32) for i in range(2)]
    hid = [sb(f"{tag}_hid{i}", [P, FB, BANK], F32) for i in range(2)]
    logits = sb(f"{tag}_logits", [P, NT, NE], F32)
    top = sb(f"{tag}_top", [P, NT, 8], F32)
    idx = sb(f"{tag}_idx", [P, NT, 8], U32)
    idxf = sb(f"{tag}_idxf", [P, NT, 8], F32)
    expert_no = sb(f"{tag}_expert_no", [P, NE], F32)
    gap = sb(f"{tag}_gap", [P, NT], F32)
    ratio = sb(f"{tag}_ratio", [P, NT], F32)
    g1 = sb(f"{tag}_g1", [P, NT], F32)
    g2 = sb(f"{tag}_g2", [P, NT], F32)
    hit = sb(f"{tag}_hit", [P, 2, NT, NE], F32)
    gate = sb(f"{tag}_gate", [P, NT, NE], F32)
    gate_e = sb(f"{tag}_gate_e", [P, NE, NT], F32)
    gate_t = sb(f"{tag}_gate_t", [NE, NT, P], F32)
    ln = layer_norm(nc, env, f"{tag}_ln", xn, [bank[4], bank[5]])
    env.rewind(m0)

    s = lambda n: env.sem(f"{tag}_{n}")
    loaded = [s("loaded0"), s("loaded1")]
    logits_mm, b1_t, b1_all_ready, gap_ready, ratio_ready = (s(n) for n in ("logits_mm", "b1_t", "b1_all_ready", "gap_ready", "ratio_ready"))
    gates_ready, gates_t, gate_t_ready, b2_mm = (s(n) for n in ("gates_ready", "gates_t", "gate_t_ready", "b2_mm"))
    iota_ready, step_sem, b1_ready = s("iota_ready"), s("dve_step"), s("b1_ready")
    up_ready, gelu_done, out_ready, added = s("up_ready"), s("gelu_done"), s("out_ready"), s("added")

    def sp(e):
        def load(i, slot):
            e.dma_start(W1[slot][:], w1[bass.ds(i, 1)].rearrange("o c f -> (o c) f")).then_inc(loaded[slot], 16)
            e.dma_start(W2[slot][:], w2[bass.ds(i, 1)].rearrange("o (f p) c -> p (o f) c", p=P))\
                .then_inc(loaded[slot], 16)
        load(0, 0)
        load(1, 1)
        with e.Fori(0, NE // 2 - 1) as it:
            for u in range(2):
                e.wait_ge(out_ready, (it * 2 + u) * NCH + (NCH + 2))
                load(it * 2 + (u + 2), u)

    def pool(g):
        nc.gpsimd.iota(expert_no[:], pattern=[[1, NE]], base=0, channel_multiplier=0,
                       allow_small_or_imprecise_dtypes=True).then_inc(iota_ready, 1)
        ln.pool(g)

    def act(a):
        a.wait_ge(b1_t, 1)
        nc.scalar.activation(b1_all[:].rearrange("p e f -> p (e f)"), bank[7][:, 0:NE * FB], ACT.Copy)\
            .then_inc(b1_all_ready, 1)
        ln.act(a)
        a.wait_ge(gap_ready, 1)
        nc.scalar.activation(ratio[:], gap[:], ACT.Exp).then_inc(ratio_ready, 1)
        a.sem_inc(gelu_done, FB)
        with a.Fori(0, NE // 2) as it:
            for u in range(2):
                a.wait_ge(b1_ready, it * 2 + (u + 1))
                for c in range(NCH):
                    n = it * (2 * NCH) + (u * NCH + c)
                    a.wait_ge(out_ready, n + 1)
                    for f in range(FB):
                        a.wait_ge(up_ready, n * FB + (f + 1))
                        nc.scalar.activation(hid[c % 2][:, f, :], bank[f], ACT.Gelu, bias=b1[u][:, f:f + 1])\
                            .then_inc(gelu_done, 1)
        for k in range(NCH):
            a.wait_ge(gates_t, k + 1)
            nc.scalar.activation(gate_t[:, 4 * k:4 * k + 4, :].rearrange("e t p -> e (t p)"), bank[k][0:NE, :], ACT.Copy)\
                .then_inc(gate_t_ready, 1)

    def dve(v):
        ln.dve(v)
        ch = Chain(v, step_sem)
        v.wait_ge(b1_all_ready, 1)
        nc.vector.tensor_copy(b1[0][:], b1_all[:, 0, :]).then_inc(b1_ready, 1)
        v.wait_ge(logits_mm, 1)
        ch(nc.vector.tensor_tensor(logits[:], bank[6][:, 0:NT * NE].rearrange("p (t e) -> p t e", e=NE),
                                   env.w["router_b"].unsqueeze(1).broadcast_to([P, NT, NE]), ALU.add))
        for t in range(NT):
            nc.vector.max(top[:, t, :], logits[:, t, :]).then_inc(step_sem, 1)
            ch.n += 1
        for t in range(NT):
            v.wait_ge(step_sem, ch.n - NT + 1 + t)
            nc.vector.max_index(idx[:, t, :], top[:, t, :], logits[:, t, :]).then_inc(step_sem, 1)
        ch.n += NT
        v.wait_ge(step_sem, ch.n)
        nc.vector.tensor_tensor(gap[:], top[:, :, 1], top[:, :, 0], ALU.subtract).then_inc(gap_ready, 1)
        ch(nc.vector.tensor_copy(idxf[:], idx[:]))
        v.wait_ge(iota_ready, 1)
        for k in range(2):
            ch(nc.vector.tensor_tensor(hit[:, k], expert_no[:].unsqueeze(1).broadcast_to([P, NT, NE]),
                                       idxf[:, :, k:k + 1].broadcast_to([P, NT, NE]), ALU.is_equal))
        v.wait_ge(ratio_ready, 1)
        ch(nc.vector.tensor_scalar(g1[:], ratio[:], 1.0, None, ALU.add))
        ch(nc.vector.reciprocal(g1[:], g1[:]))
        ch(nc.vector.tensor_scalar(g1[:], g1[:], 0.5, None, ALU.mult))
        ch(nc.vector.tensor_tensor(g2[:], ratio[:], g1[:], ALU.mult))
        ch(nc.vector.tensor_tensor(hit[:, 0], hit[:, 0], g1[:].unsqueeze(2).broadcast_to([P, NT, NE]), ALU.mult))
        ch(nc.vector.tensor_tensor(hit[:, 1], hit[:, 1], g2[:].unsqueeze(2).broadcast_to([P, NT, NE]), ALU.mult))
        nc.vector.tensor_tensor(gate[:], hit[:, 0], hit[:, 1], ALU.add).then_inc(gates_ready, 1)
        v.wait_ge(gates_ready, 1)
        ch(nc.vector.tensor_copy(gate_e[:].rearrange("p e t -> p t e"), gate[:]))
        v.sem_inc(added, NT)

        def expert(it, u, more):
            i = it * 2 + u
            if more:
                v.wait_ge(gelu_done, i * (NCH * FB) + FB)
                nc.vector.tensor_scalar(b1[1 - u][:], b1_all[:, bass.ds(i + 1, 1), :].rearrange("p o f -> p (o f)"),
                                        1.0, None, ALU.mult).then_inc(b1_ready, 1)
            for c in range(NCH):
                n = it * (2 * NCH) + (u * NCH + c)
                v.wait_ge(out_ready, n + 3)
                for j in range(4):
                    t = 4 * c + j
                    v.wait_ge(added, n * 4 + (j + 1))
                    nc.vector.scalar_tensor_tensor(
                        x[:, t, :], bank[4 + c % 2][:, j * P:(j + 1) * P],
                        gate_e[:, bass.ds(i, 1), t], x[:, t, :], ALU.mult, ALU.add).then_inc(added, 1)

        with v.Fori(0, NE // 2 - 1) as it:
            expert(it, 0, True)
            expert(it, 1, True)
        expert(NE // 2 - 1, 0, True)
        expert(NE // 2 - 1, 1, False)
        for t in range(NT):
            if t % 4 == 0:
                v.wait_ge(b2_mm, t // 4 + 1)
            v.wait_ge(added, NT * NE + t + 1)
            nc.vector.tensor_tensor(x[:, t, :], bank[4 + t // 4 % 2][:, (t % 4) * P:(t % 4 + 1) * P], x[:, t, :], ALU.add)\
                .then_inc(added, 1)

    def pe(t_):
        t_.sem_inc(out_ready, 2)
        nc.tensor.transpose(bank[7][:, 0:NE * FB], env.w["b1_rows"][:], env.ident[0:NE * FB, 0:NE * FB]).then_inc(b1_t, 1)
        ln.pe(t_)
        for t in range(NT):
            if t % 4 == 0:
                t_.wait_ge(ln.ready, t // 4 + 1)
            last = nc.tensor.matmul(bank[6][:, t * NE:(t + 1) * NE], xn[:, t * P:(t + 1) * P], env.w["router"][:],
                                    start=True, stop=True)
        last.then_inc(logits_mm, 1)
        def up(n, u, c):
            for f in range(FB):
                t_.wait_ge(gelu_done, n * FB + (f + 1))
                nc.tensor.matmul(bank[f], W1[u][:, f * P:(f + 1) * P], xn[:, c * BANK:(c + 1) * BANK],
                                 start=True, stop=True).then_inc(up_ready, 1)

        def down(n, u, c):
            t_.wait_ge(gelu_done, n * FB + 2 * FB)
            t_.wait_ge(added, n * 4 + (16 - 4))
            for j in range(4):
                for f in range(FB):
                    last = nc.tensor.matmul(bank[4 + c % 2][:, j * P:(j + 1) * P], hid[c % 2][:, f, j * P:(j + 1) * P],
                                            W2[u][:, f, :], start=(f == 0), stop=(f == FB - 1))
            last.then_inc(out_ready, 1)

        with t_.Fori(0, NE // 2) as it:
            for k in range(2 * NCH + 1):
                if k < 2 * NCH:
                    u, c = k // NCH, k % NCH
                    if c == 0:
                        t_.wait_ge(loaded[u], it * 32 + 32)
                    up(it * (2 * NCH) + k, u, c)
                if k:
                    down(it * (2 * NCH) + (k - 1), (k - 1) // NCH, (k - 1) % NCH)
        t_.wait_ge(gates_ready, 1)
        for k in range(NCH):
            for j in range(4):
                last = nc.tensor.transpose(bank[k][0:NE, j * P:(j + 1) * P], gate[:, 4 * k + j, :], env.ident[:])
            last.then_inc(gates_t, 1)
        for k in range(NCH):
            t_.wait_ge(gate_t_ready, k + 1)
            t_.wait_ge(added, NT * (NE + 1) + (4 * (k - 1) if k >= 2 else 0))
            for j in range(4):
                last = nc.tensor.matmul(bank[4 + k % 2][:, j * P:(j + 1) * P], gate_t[:, 4 * k + j, :], env.w["b2"][:],
                                        start=True, stop=True)
            last.then_inc(b2_mm, 1)

    return Sublayer(parts=dict(sp=sp, pool=pool, act=act, dve=dve, pe=pe), done=(added, NT * (NE + 2)))


HD, NS = 512, 16
DT = HD // P
TWO_PI = 6.283185307179586
TURN_1 = 6.28125
TURN_2 = int((TWO_PI - TURN_1) * 2 ** 21) / 2 ** 21
TURN = (TURN_1, TURN_2, TWO_PI - TURN_1 - TURN_2)
ROUND = 12582912.0


def ssm_weights(env, weight, loads, ins):
    weight("w_in", ins["L1_attn_input_proj"], [C, HD])
    weight("w_out", ins["L1_attn_output_proj"].rearrange("(t p) e -> p t e", p=P), [P, DT, C])
    weight("skip", ins["L1_attn_skip_proj"].rearrange("(t p) e -> p t e", p=P), [P, DT, HD])
    env.w["bc"] = env.sb("w_bc", [P, DT, 2 * NS], F32)
    loads.append((env.w["bc"][:, :, 0:NS], ins["L1_attn_b_proj"].rearrange("(t p) n -> p t n", p=P)))
    loads.append((env.w["bc"][:, :, NS:2 * NS], ins["L1_attn_c_proj"].rearrange("(t p) n -> p t n", p=P)))
    weight("a_log", ins["L1_attn_a_log"].rearrange("(o n) -> o n", o=1).broadcast_to([P, NS]), [P, NS])
    weight("dt_rows", ins["L1_attn_dt_proj"].rearrange("(t p) -> t p", p=P), [DT, P])
    weight("phase_rows", ins["L1_attn_floquet_phases"].rearrange("(t p) -> t p", p=P), [DT, P])


def ssm(nc, env, tag):
    m0 = env.mark()
    sb, x, w = env.sb, env.x, env.w
    ps = env.ps
    bank = [ps[:, i, :] for i in range(8)]
    xn = sb(f"{tag}_xn", [P, TOK], F32)
    X = sb(f"{tag}_X", [P, DT, TOK], F32)
    decay = sb(f"{tag}_decay", [P, NS, DT], F32)
    small = sb(f"{tag}_small", [P, 8, DT], F32)
    rates = sb(f"{tag}_rates", [P, NS], F32)
    bc_part = sb(f"{tag}_bc_part", [6 * NS, TOK], BF16)
    sel = sb(f"{tag}_sel", [6 * NS, 2 * NS, P], BF16)
    Y = sb(f"{tag}_Y", [P, TOK], F32)
    zc = sb(f"{tag}_zc", [P, TOK], F32)
    skip_out = sb(f"{tag}_skip_out", [P, C], F32)
    mark = env.mark()
    Br = [sb(f"{tag}_Br{i}", [P, TOK], F32) for i in range(2)]
    Cr = [sb(f"{tag}_Cr{i}", [P, TOK], F32) for i in range(2)]
    inj = [sb(f"{tag}_inj{i}", [P, TOK], F32) for i in range(2)]
    hst = [sb(f"{tag}_hst{i}", [P, TOK], F32) for i in range(2)]
    env.rewind(mark)
    cosine = sb(f"{tag}_cosine", [P, DT, T], F32)
    turns = sb(f"{tag}_turns", [P, DT, T], F32)
    where = sb(f"{tag}_where", [P, T], F32)
    w_in_t = sb(f"{tag}_w_in_t", [P, DT, C], F32)
    chain_n = sb(f"{tag}_chain_n", [P, HD], F32)
    chain_nt = sb(f"{tag}_chain_nt", [P, DT, C], F32)
    rest = sb(f"{tag}_rest", [2 * NS, TOK], F32)
    mid = sb(f"{tag}_mid", [2 * NS, TOK], BF16)
    ln = layer_norm(nc, env, f"{tag}_ln", xn, [bank[4], bank[5]])
    env.rewind(m0)

    s = lambda n: env.sem(f"{tag}_{n}")
    step_sem, where_ready, sel_zero = s("dve_step"), s("where_ready"), s("sel_zero")
    cols_t, cols_ready, angle_ready, cos_ready = s("cols_t"), s("cols_ready"), s("angle_ready"), s("cos_ready")
    dt_exp_in, dt_exp, dt_ln, rates_exp, decay_in, decay_ready = (s(n) for n in ("dt_exp_in", "dt_exp", "dt_ln", "rates_exp", "decay_in", "decay_ready"))
    win_t, win_t_ready, skip_mm, skip_ready = s("win_t"), s("win_t_ready"), s("skip_mm"), s("skip_ready")
    hd_mm, x_ready, bc_mm, bc_read, x_scaled = s("hd_mm"), s("x_ready"), s("bc_mm"), s("bc_read"), s("x_scaled")
    hi_ready, parts_ready, mid_ready = s("hi_ready"), s("parts_ready"), s("mid_ready")
    rep_mm, rep_ready, inj_dve, inj_pool, scanned, z_mm, z_read, y_ready = (s(n) for n in ("rep_mm", "rep_ready", "inj_dve", "inj_pool", "scanned", "z_mm", "z_read", "y_ready"))
    out_mm, x_done = s("out_mm"), s("x_done")

    def pool(g):
        nc.gpsimd.iota(where[:], pattern=[[1, T]], base=0, channel_multiplier=0,
                       allow_small_or_imprecise_dtypes=True).then_inc(where_ready, 1)
        nc.gpsimd.memset(sel[:], 0.0).then_inc(sel_zero, 1)
        for j in range(3):
            g.wait_ge(sel_zero, j + 1)
            nc.gpsimd.affine_select(out=sel[:], in_=sel[:], compare_op=ALU.not_equal, fill=1.0, base=-2 * NS * j,
                                    pattern=[[-1, 2 * NS], [0, P]], channel_multiplier=1).then_inc(sel_zero, 1)
        ln.pool(g)
        g.wait_ge(x_scaled, DT)
        g.sem_inc(z_read, 2 * NCH)
        with g.Fori(0, NS // 2) as it:
            for u in range(2):
                g.wait_ge(rep_ready, it * 16 + (8 * u + 8))
                for d in range(DT - 1):
                    g.wait_ge(scanned, it * 16 + (8 * u + 2 * d + 2))
                    nc.gpsimd.tensor_tensor(inj[d % 2][:], X[:, d, :], Br[u][:], ALU.mult).then_inc(inj_pool, 1)

    def act(a):
        a.wait_ge(cols_t, 1)
        nc.scalar.activation(small[:, 0:2, :], bank[7][:, 0:2 * DT].rearrange("p (k t) -> p k t", k=2), ACT.Copy)\
            .then_inc(cols_ready, 1)
        nc.scalar.activation(rates[:], w["a_log"][:], ACT.Exp).then_inc(rates_exp, 1)
        a.wait_ge(dt_exp_in, 1)
        nc.scalar.activation(small[:, 3, :], small[:, 2, :], ACT.Exp, scale=-1.0).then_inc(dt_exp, 1)
        a.wait_ge(dt_exp, 1)
        nc.scalar.activation(small[:, 4, :], small[:, 3, :], ACT.Ln, bias=1.0).then_inc(dt_ln, 1)
        a.wait_ge(decay_in, 1)
        nc.scalar.activation(decay[:], decay[:], ACT.Exp, scale=-1.0).then_inc(decay_ready, 1)
        a.wait_ge(win_t, 1)
        nc.scalar.activation(w_in_t[:].rearrange("p t c -> p (t c)"), bank[0], ACT.Copy).then_inc(win_t_ready, 1)
        a.wait_ge(skip_mm, 1)
        nc.scalar.activation(chain_n[:], bank[1], ACT.Copy).then_inc(skip_ready, 1)
        a.wait_ge(skip_mm, 2)
        nc.scalar.activation(chain_nt[:].rearrange("p t c -> p (t c)"), bank[2], ACT.Copy).then_inc(skip_ready, 1)
        a.wait_ge(skip_mm, 3)
        nc.scalar.activation(skip_out[:], bank[3][:, 0:C], ACT.Copy).then_inc(skip_ready, 1)
        ln.act(a)
        a.wait_ge(angle_ready, 1)
        nc.scalar.activation(cosine[:], cosine[:], ACT.Sin).then_inc(cos_ready, 1)
        for k in range(NCH):
            cols = slice(k * BANK, (k + 1) * BANK)
            a.wait_ge(mid_ready, k + 1)
            nc.scalar.activation(bc_part[2 * NS:4 * NS, cols], mid[:, cols], ACT.Copy).then_inc(parts_ready, 1)
        a.sem_inc(rep_ready, NCH)
        with a.Fori(0, NS // 2) as it:
            for u in range(2):
                for k in range(2 * NCH):
                    dst = (Br if k < NCH else Cr)[u]
                    c = k % NCH
                    if k == 0:
                        a.wait_ge(inj_pool, it * 6 + (3 * u + 3))
                        a.wait_ge(inj_dve, it * 2 + (u + 1))
                    if k == NCH:
                        a.wait_ge(z_read, it * 8 + (4 * u + 4))
                    a.wait_ge(rep_mm, it * 16 + (8 * u + k + 1))
                    nc.scalar.activation(dst[:, c * BANK:(c + 1) * BANK], bank[c], ACT.Copy).then_inc(rep_ready, 1)

    def dve(v):
        ch = Chain(v, step_sem)
        ln.dve_stats(v)
        v.wait_ge(cols_ready, 1)
        ch(nc.vector.tensor_scalar(small[:, 2, :], small[:, 0, :], -1.0, None, ALU.mult))
        nc.vector.tensor_tensor(small[:, 2, :], small[:, 2, :], small[:, 0, :], ALU.max).then_inc(dt_exp_in, 1)
        ch(nc.vector.tensor_scalar(small[:, 5, :], small[:, 0, :], 0.0, None, ALU.max))
        v.wait_ge(where_ready, 1)
        for d in range(DT):
            nc.vector.tensor_scalar(cosine[:, d, :], where[:], small[:, 1, d:d + 1], None, ALU.mult).then_inc(step_sem, 1)
            ch.n += 1
        v.wait_ge(step_sem, ch.n)
        v.wait_ge(dt_ln, 1)
        ch(nc.vector.tensor_tensor(small[:, 6, :], small[:, 5, :], small[:, 4, :], ALU.add))
        v.wait_ge(rates_exp, 1)
        nc.vector.tensor_tensor(decay[:], small[:, 6, :].unsqueeze(1).broadcast_to([P, NS, DT]),
                                rates[:].unsqueeze(2).broadcast_to([P, NS, DT]), ALU.mult).then_inc(decay_in, 1)
        ch(nc.vector.tensor_scalar(turns[:], cosine[:], 1.0 / TWO_PI, 0.25, ALU.mult, ALU.add))
        ch(nc.vector.tensor_scalar(turns[:], turns[:], ROUND, ROUND, ALU.add, ALU.subtract))
        ln.dve_apply(v)
        for part in TURN:
            ch(nc.vector.scalar_tensor_tensor(cosine[:], turns[:], -part, cosine[:], ALU.mult, ALU.add))
        ch(nc.vector.tensor_scalar(cosine[:], cosine[:], TWO_PI / 4, 3.1415925, ALU.add, ALU.min))
        nc.vector.tensor_scalar(cosine[:], cosine[:], -3.1415925, None, ALU.max).then_inc(angle_ready, 1)
        v.wait_ge(cos_ready, 1)
        for k in range(NCH):
            half = k % 2
            for d in range(DT):
                n = k * DT + d
                v.wait_ge(hd_mm, n + 1)
                nc.vector.tensor_tensor(X[:, d, k * BANK:(k + 1) * BANK], bank[n % 4],
                                        cosine[:, d, half * BANK:(half + 1) * BANK], ALU.mult).then_inc(x_ready, 1)
        for k in range(NCH):
            cols = slice(k * BANK, (k + 1) * BANK)
            v.wait_ge(bc_mm, k + 1)
            rows = bank[4 + k % 2][0:2 * NS, :]
            nc.vector.tensor_copy(bc_part[0:2 * NS, cols], rows).then_inc(hi_ready, 1)
            v.wait_ge(hi_ready, k + 1)
            nc.vector.tensor_tensor(rest[:, cols], rows, bc_part[0:2 * NS, cols], ALU.subtract).then_inc(bc_read, 1)
            v.wait_ge(bc_read, k + 1)
            nc.vector.tensor_copy(mid[:, cols], rest[:, cols]).then_inc(mid_ready, 1)
            v.wait_ge(mid_ready, k + 1)
            nc.vector.tensor_tensor(bc_part[4 * NS:6 * NS, cols], rest[:, cols], mid[:, cols], ALU.subtract)\
                .then_inc(parts_ready, 1)
        for d in range(DT):
            v.wait_ge(bc_mm, NCH)
            nc.vector.tensor_scalar(X[:, d, :], X[:, d, :], small[:, 6, d:d + 1], None, ALU.mult).then_inc(x_scaled, 1)
        nc.vector.memset(Y[:], 0.0).then_inc(y_ready, 1)
        v.sem_inc(inj_pool, 6)
        v.sem_inc(inj_dve, 2)
        v.sem_inc(scanned, 4)
        v.wait_ge(decay_ready, 1)
        v.wait_ge(x_scaled, DT)

        def scan(it, u, d):
            if d == DT - 1:
                v.wait_ge(rep_ready, it * 16 + (8 * u + 8))
                v.wait_ge(scanned, it * 16 + (8 * u + 8))
                nc.vector.tensor_tensor(inj[d % 2][:], X[:, d, :], Br[u % 2][:], ALU.mult).then_inc(inj_dve, 1)
                v.wait_ge(inj_dve, it * 2 + (u + 3))
            else:
                v.wait_ge(inj_pool, it * 6 + (3 * u + 7 + d))
            v.wait_ge(z_mm, it * 32 + (16 * u + 4 * d + 4))
            decay_at = decay[:, bass.ds(it * 2 + u, 1), d]
            for b in range(B):
                cols = slice(b * T, (b + 1) * T)
                nc.vector.tensor_tensor_scan(hst[d % 2][:, cols], decay_at.broadcast_to([P, T]),
                                             inj[d % 2][:, cols], 0.0, ALU.mult, ALU.add).then_inc(scanned, 1)

        def weigh(it, u):
            for c in range(NCH):
                cols = slice(c * BANK, (c + 1) * BANK)
                if c == 0:
                    v.wait_ge(rep_ready, it * 16 + (8 * u + 12))
                v.wait_ge(z_mm, it * 32 + (16 * u + 21 + c))
                nc.vector.tensor_tensor(zc[:, cols], bank[4 + c], Cr[u][:, cols], ALU.mult).then_inc(z_read, 1)
            v.wait_ge(z_read, it * 8 + (4 * u + 12))
            v.wait_ge(y_ready, it * 2 + (u + 1))
            nc.vector.tensor_tensor(Y[:], Y[:], zc[:], ALU.add).then_inc(y_ready, 1)

        scan(0, 0, 0)
        with v.Fori(0, NS // 2 - 1) as it:
            for u in range(2):
                for d in range(1, DT):
                    scan(it, u, d)
                scan(it, u + 1, 0)
                weigh(it, u)
        for u in range(2):
            for d in range(1, DT):
                scan(NS // 2 - 1, u, d)
            if u == 0:
                scan(NS // 2 - 1, 1, 0)
            weigh(NS // 2 - 1, u)
        for t in range(NT):
            v.wait_ge(out_mm, t + 1)
            nc.vector.tensor_tensor(x[:, t, :], bank[t % 4][:, 0:C], x[:, t, :], ALU.add).then_inc(x_done, 1)

    def pe(t_):
        nc.tensor.transpose(bank[7][:, 0:DT], w["dt_rows"][:], env.ident[0:DT, 0:DT])
        nc.tensor.transpose(bank[7][:, DT:2 * DT], w["phase_rows"][:], env.ident[0:DT, 0:DT]).then_inc(cols_t, 1)
        for d in range(DT):
            last = nc.tensor.transpose(bank[0][:, d * P:(d + 1) * P], w["w_in"][:, d * P:(d + 1) * P], env.ident[:])
        last.then_inc(win_t, 1)
        t_.wait_ge(win_t_ready, 1)
        for d in range(DT):
            last = nc.tensor.matmul(bank[1], w_in_t[:, d, :], w["skip"][:, d, :], start=(d == 0), stop=(d == DT - 1))
        last.then_inc(skip_mm, 1)
        t_.wait_ge(skip_ready, 1)
        for d in range(DT):
            last = nc.tensor.transpose(bank[2][:, d * P:(d + 1) * P], chain_n[:, d * P:(d + 1) * P], env.ident[:])
        last.then_inc(skip_mm, 1)
        t_.wait_ge(skip_ready, 2)
        for d in range(DT):
            last = nc.tensor.matmul(bank[3][:, 0:C], chain_nt[:, d, :], w["w_out"][:, d, :],
                                    start=(d == 0), stop=(d == DT - 1))
        last.then_inc(skip_mm, 1)
        ln.pe(t_)
        t_.wait_ge(skip_ready, 3)
        for k in range(NCH):
            t_.wait_ge(ln.ready, k + 1)
            for d in range(DT):
                n = k * DT + d
                if n >= 4:
                    t_.wait_ge(x_ready, n - 3)
                nc.tensor.matmul(bank[n % 4], w["w_in"][:, d * P:(d + 1) * P], xn[:, k * BANK:(k + 1) * BANK],
                                 start=True, stop=True).then_inc(hd_mm, 1)
        for k in range(NCH):
            t_.wait_ge(x_ready, (k + 1) * DT)
            if k >= 2:
                t_.wait_ge(bc_read, k - 1)
            for d in range(DT):
                last = nc.tensor.matmul(bank[4 + k % 2][0:2 * NS, :], w["bc"][:, d, :], X[:, d, k * BANK:(k + 1) * BANK],
                                        start=(d == 0), stop=(d == DT - 1))
            last.then_inc(bc_mm, 1)
        t_.wait_ge(sel_zero, 4)
        t_.wait_ge(parts_ready, 2 * NCH)
        t_.sem_inc(z_mm, 2 * NCH)

        def spread(it, u, k):
            c = k % NCH
            row = it * 2 + u + (NS if k >= NCH else 0)
            nc.tensor.matmul(bank[c], sel[:, bass.ds(row, 1), :].rearrange("r o p -> r (o p)"),
                             bc_part[:, c * BANK:(c + 1) * BANK], start=True, stop=True).then_inc(rep_mm, 1)

        def spread_all(it, u):
            for k in range(2 * NCH):
                t_.wait_ge(rep_ready, it * 16 + (8 * u + k + 1))
                spread(it, u, k)

        def project(it, u, d):
            for c in range(NCH):
                if c % 2 == 0:
                    t_.wait_ge(scanned, it * 16 + (8 * u + 2 * d + c // 2 + 5))
                if d == 0:
                    t_.wait_ge(z_read, it * 8 + (4 * u + c + 5))
                nc.tensor.matmul(bank[4 + c], w["w_out"][:, d, :], hst[d % 2][:, c * BANK:(c + 1) * BANK],
                                 start=(d == 0), stop=(d == DT - 1)).then_inc(z_mm, 1)

        spread_all(0, 0)
        spread_all(0, 1)
        with t_.Fori(0, NS // 2 - 1) as it:
            for u in range(2):
                for d in range(DT):
                    project(it, u, d)
                spread_all(it, u + 2)
        for u in range(2):
            for d in range(DT):
                project(NS // 2 - 1, u, d)
        t_.wait_ge(y_ready, NS + 1)
        for t in range(NT):
            if t >= 4:
                t_.wait_ge(x_done, t - 3)
            nc.tensor.matmul(bank[t % 4][:, 0:C], Y[:, t * P:(t + 1) * P], env.ident[:], start=True, stop=False)
            nc.tensor.matmul(bank[t % 4][:, 0:C], xn[:, t * P:(t + 1) * P], skip_out[:], start=False, stop=True)\
                .then_inc(out_mm, 1)

    return Sublayer(parts=dict(pool=pool, act=act, dve=dve, pe=pe), done=(x_done, NT))


STAGES = ("attn", "rwkv", "attn", "moe", "ssm", "moe",)
EXTRA_WEIGHTS = {"rwkv": rwkv_weights, "moe": moe_weights, "ssm": ssm_weights}


def build(nc, out, **ins):
    ctx = ExitStack()
    with ctx:
        drams = {}

        def sem(name):
            one = nc.alloc_semaphore(f"{name}_{len(used)}")
            used[-1].append(one)
            return one

        def dram(name, shape, dt):
            if name not in drams:
                drams[name] = nc.dram_tensor(name, shape, dt).ap()
            return drams[name]

        used = [[]]
        LIMIT = nc.sbuf_usable_end
        top = [nc.sbuf_base]
        top[0] = (top[0] + 31) // 32 * 32
        size = {F32: 4, BF16: 2, U32: 4}

        def sb(name, shape, dt):
            n = size[dt]
            for k in shape[1:]:
                n *= k
            at = top[0]
            top[0] = at + (n + 31) // 32 * 32
            assert top[0] <= LIMIT, (name, top[0], LIMIT)
            return nc.alloc_sbuf_tensor_at(f"{name}_{len(used)}", shape, dt, offset=at).ap()

        def rewind(m):
            top[0] = m

        def mark():
            return top[0]

        env = Env()
        env.sb, env.sem, env.dram, env.mark, env.rewind = sb, sem, dram, mark, rewind
        env.ps = ctx.enter_context(nc.psum_tensor("ps", [P, 8, BANK], F32))
        env.rmax = bass.bass_isa.ReduceOp.max
        x = env.x = sb("x", [P, NT, C], F32)
        env.ident = sb("ident", [P, P], F32)
        env.ident_b = sb("ident_b", [P, P], BF16)
        env.minus_half = sb("minus_half", [P, NT * H], F32)
        env.is_reg = sb("is_reg", [P, NT], F32)
        env.half_bproj = sb("half_bproj", [P, C], F32)
        env.qg_unit = sb("qg_unit", [P, C], F32)
        qg_sq = sb("qg_sq", [P, C], F32)
        qg_n2 = sb("qg_n2", [P, 2, H], F32)
        x_in, w_in, const_step, qg_ready, qg_pow = (sem(n) for n in ("x_in", "w_in", "const_step", "qg_ready", "qg_pow"))
        setup_step, out_done = sem("setup_step"), sem("out_done")
        env.w = {}
        loads = []

        def weight(name, src, shape):
            env.w[name] = sb(f"w_{name}", shape, F32)
            loads.append((env.w[name], src))

        weight("qkv", ins["L0_ffn_W_qkv"], [C, 3 * C])
        weight("proj", ins["L0_ffn_W_proj"], [C, C])
        loads.append((env.half_bproj, ins["L0_ffn_b_proj"].rearrange("(o c) -> o c", o=1).broadcast_to([P, C])))
        loads.append((env.qg_unit, ins["L0_ffn_g_info"][0, 0:1, :].broadcast_to([P, C])))
        for name in dict.fromkeys(STAGES):
            if name in EXTRA_WEIGHTS:
                EXTRA_WEIGHTS[name](env, weight, loads, ins)
        makers = {"attn": attention, "rwkv": rwkv, "moe": moe, "ssm": ssm}
        env.ins = ins
        ends = [sem(f"end{k}") for k in range(len(STAGES) - 1)]
        stages = []
        for k, name in enumerate(STAGES):
            if k >= 2:
                for one in used[k - 1]:
                    nc.release_semaphore(one)
            used.append([])
            stages.append(makers[name](nc, env, name))

        def run(e, part):
            for k, st in enumerate(stages):
                if part in st.parts:
                    st.parts[part](e)
                if k + 1 < len(stages):
                    e.drain().then_inc(ends[k], 1)
                    e.wait_ge(ends[k], 5)
                    if part == "sp" and k + 2 < len(stages):
                        for one in used[k + 1]:
                            e.sem_clear(one)

        block = ctx.enter_context(nc.Block())

        @block.sync
        def _(sp):
            sp.dma_start(x[:], ins["L0_attn_x"].rearrange("b (t p) c -> p (b t) c", p=P)).then_inc(x_in, 16)
            for dst, src in loads:
                sp.dma_start(dst, src).then_inc(w_in, 16)
            run(sp, "sp")
            last, n = stages[-1].done
            sp.wait_ge(last, n)
            sp.dma_start(out.rearrange("b (t p) c -> p (b t) c", p=P), x[:]).then_inc(out_done, 16)
            sp.wait_ge(out_done, 16)

        @block.gpsimd
        def _(pool):
            nc.gpsimd.memset(env.minus_half[:], -0.5).then_inc(const_step, 1)
            nc.gpsimd.memset(env.ident[:], 0.0).then_inc(const_step, 1)
            nc.gpsimd.memset(env.ident_b[:], 0.0).then_inc(const_step, 1)
            nc.gpsimd.memset(env.is_reg[:], 0.0).then_inc(const_step, 1)
            pool.wait_ge(const_step, 4)
            for m in (env.ident, env.ident_b):
                nc.gpsimd.affine_select(out=m[:], in_=m[:], compare_op=ALU.not_equal, fill=1.0, base=0,
                                        pattern=[[-1, P]], channel_multiplier=1).then_inc(const_step, 1)
            for b in range(B):
                nc.gpsimd.memset(env.is_reg[0:REG, b * TPB:b * TPB + 1], 1.0).then_inc(const_step, 1)
            pool.wait_ge(qg_ready, 1)
            nc.gpsimd.tensor_tensor(qg_n2[:, 1, :], qg_n2[:, 0, :], env.minus_half[:, 0:H], ALU.pow).then_inc(qg_pow, 1)
            pool.wait_ge(const_step, 8)
            run(pool, "pool")

        @block.scalar
        def _(act):
            act.wait_ge(const_step, 8)
            act.wait_ge(w_in, 16 * len(loads))
            run(act, "act")

        @block.vector
        def _(dve):
            ch = Chain(dve, setup_step)
            dve.wait_ge(const_step, 8)
            dve.wait_ge(w_in, 16 * len(loads))
            ch(nc.vector.tensor_tensor(qg_sq[:], env.qg_unit[:], env.qg_unit[:], ALU.mult))
            nc.vector.reduce_sum(qg_n2[:, 0, :], qg_sq[:].rearrange("p (h d) -> p h d", d=D), AX_X).then_inc(qg_ready, 1)
            ch(nc.vector.tensor_scalar(env.half_bproj[:], env.half_bproj[:], 0.5, None, ALU.mult))
            dve.wait_ge(qg_pow, 1)
            ch(nc.vector.tensor_scalar(qg_n2[:, 1, :], qg_n2[:, 1, :], 1.0 / H, None, ALU.mult))
            ch(nc.vector.tensor_tensor(env.qg_unit[:].rearrange("p (h d) -> p h d", d=D),
                                       env.qg_unit[:].rearrange("p (h d) -> p h d", d=D),
                                       qg_n2[:, 1, :].unsqueeze(2).broadcast_to([P, H, D]), ALU.mult))
            dve.wait_ge(x_in, 16)
            run(dve, "dve")

        @block.tensor
        def _(pe):
            pe.wait_ge(const_step, 8)
            pe.wait_ge(w_in, 16 * len(loads))
            run(pe, "pe")


_OUT_SHAPE = (B, T, C)


def kernel(**inputs):
    import numpy as _np
    import concourse.bacc as _bacc
    from concourse import mybir as _mybir
    from concourse.bass_utils import run_bass_kernel_spmd as _run

    nc = _bacc.Bacc("TRN2", target_bir_lowering=False, num_devices=1)
    arrays, args = {}, {}
    for name, value in inputs.items():
        a = _np.ascontiguousarray(value)
        arrays[name] = a
        args[name] = nc.dram_tensor(name, a.shape, _mybir.dt.from_np(a.dtype), kind="ExternalInput").ap()
    out = nc.dram_tensor("out", _OUT_SHAPE, _mybir.dt.float32, kind="ExternalOutput").ap()
    build(nc, out, **args)
    r = _run(nc, [arrays], core_ids=[0])
    return r.results[0]["out"]
```
